# Optimizing a Trainium2 kernel written in Bass

```python
import numpy as np
import jax
import jax.numpy as jnp

def _softmax(x, axis=-1):
    return jax.nn.softmax(x, axis=axis)

def _gelu(x):
    return jax.nn.gelu(x, approximate=True)

def _silu(x):
    return jax.nn.silu(x)

def _sigmoid(x):
    return jax.nn.sigmoid(x)

def _layernorm(x, axis=-1, eps=1e-05):
    m = jnp.mean(x, axis=axis, keepdims=True)
    v = jnp.var(x, axis=axis, keepdims=True)
    return (x - m) / jnp.sqrt(v + eps)

def _scatter_add(tgt, idx, src, axis=0):
    return tgt.at[idx].add(src)

def _segment_sum(src, seg, n):
    return jax.ops.segment_sum(src, seg, n)
kernel_name = 'mk_seq_postln_d1_jaxref_r4_2033ac'

def setup_inputs(seed: int=0):
    np.random.seed(seed)
    _w = jnp.asarray

    def _L0_attn_setup():
        import jax, jax.numpy as jnp
        import numpy as np
        from jax import lax
        B, S, HID = (4, 512, 512)
        NH, DK, DV, KW = (16, 128, 128, 4)

        def _dconv_causal(y, w, b):
            yt = jnp.transpose(y, (0, 2, 1))
            out = lax.conv_general_dilated(yt, w, window_strides=(1,), padding=[(w.shape[-1] - 1, 0)], dimension_numbers=('NCH', 'OIH', 'NCH'), feature_group_count=w.shape[0])
            return jnp.transpose(out + b[None, :, None], (0, 2, 1))

        def _delta_rule(q, k, v, a, beta):
            qs = jnp.moveaxis(q, 1, 0)
            ks = jnp.moveaxis(k, 1, 0)
            vs = jnp.moveaxis(v, 1, 0)
            as_ = jnp.moveaxis(a, 1, 0)
            bs = jnp.moveaxis(beta, 1, 0)

            def step(St, inp):
                q_t, k_t, v_t, a_t, b_t = inp
                err = jnp.einsum('bhvk,bhk->bhv', St, k_t) - v_t
                St = a_t[..., None] * St - (b_t[..., None] * err)[..., None] * k_t[:, :, None, :]
                o_t = jnp.einsum('bhvk,bhk->bhv', St, q_t)
                return (St, o_t)
            S0 = jnp.zeros(q.shape[:1] + (q.shape[2], v.shape[3], q.shape[3]), q.dtype)
            _, os_ = lax.scan(step, S0, (qs, ks, vs, as_, bs))
            return jnp.moveaxis(os_, 0, 1)
        key = jax.random.key(seed)
        ks = jax.random.split(key, 12)
        w = lambda k, shape, s=0.02: jax.random.normal(k, shape, jnp.float32) * s
        return {'x': jax.random.normal(ks[0], (B, S, HID), jnp.float32), 'Wq': w(ks[1], (HID, NH * DK)), 'Wk': w(ks[2], (HID, NH * DK)), 'Wv': w(ks[3], (HID, NH * DV)), 'Wa': w(ks[4], (HID, NH * DV)), 'ba': jnp.zeros((NH * DV,), jnp.float32), 'Wb': w(ks[5], (HID, NH)), 'bb': jnp.zeros((NH,), jnp.float32), 'Wg': w(ks[6], (HID, NH * DV)), 'Wo': w(ks[7], (NH * DV, HID)), 'cqw': w(ks[8], (NH * DK, 1, KW), 0.2), 'cqb': jnp.zeros((NH * DK,), jnp.float32), 'ckw': w(ks[9], (NH * DK, 1, KW), 0.2), 'ckb': jnp.zeros((NH * DK,), jnp.float32), 'cvw': w(ks[10], (NH * DV, 1, KW), 0.2), 'cvb': jnp.zeros((NH * DV,), jnp.float32), 'ln_w': jnp.ones((DV,), jnp.float32), 'ln_b': jnp.zeros((DV,), jnp.float32)}
    _L0_attn_in = _L0_attn_setup()

    def _L0_ffn_setup():
        import jax, jax.numpy as jnp
        import numpy as np
        D_MODEL = 512
        D_EXPERT = 2048
        EPS = 1e-08

        def ternary_quant(w):
            scale = jnp.mean(jnp.abs(w)) + EPS
            q = jnp.clip(jnp.round(w / scale), -1.0, 1.0) * scale
            return w + jax.lax.stop_gradient(q - w)
        key = jax.random.key(seed)
        k_x, k_up, k_gate, k_down = jax.random.split(key, 4)
        std_in = 1.0 / np.sqrt(D_MODEL)
        std_exp = 1.0 / np.sqrt(D_EXPERT)
        return {'x': jax.random.normal(k_x, (4, 512, D_MODEL), dtype=jnp.float32), 'W_up': jax.random.normal(k_up, (D_EXPERT, D_MODEL), dtype=jnp.float32) * std_in, 'W_gate': jax.random.normal(k_gate, (D_EXPERT, D_MODEL), dtype=jnp.float32) * std_in, 'W_down': jax.random.normal(k_down, (D_MODEL, D_EXPERT), dtype=jnp.float32) * std_exp}
    _L0_ffn_in = _L0_ffn_setup()
    _d = {'L0_attn_x': _L0_attn_in['x'], 'L0_attn_Wq': _L0_attn_in['Wq'], 'L0_attn_Wk': _L0_attn_in['Wk'], 'L0_attn_Wv': _L0_attn_in['Wv'], 'L0_attn_Wa': _L0_attn_in['Wa'], 'L0_attn_ba': _L0_attn_in['ba'], 'L0_attn_Wb': _L0_attn_in['Wb'], 'L0_attn_bb': _L0_attn_in['bb'], 'L0_attn_Wg': _L0_attn_in['Wg'], 'L0_attn_Wo': _L0_attn_in['Wo'], 'L0_attn_cqw': _L0_attn_in['cqw'], 'L0_attn_cqb': _L0_attn_in['cqb'], 'L0_attn_ckw': _L0_attn_in['ckw'], 'L0_attn_ckb': _L0_attn_in['ckb'], 'L0_attn_cvw': _L0_attn_in['cvw'], 'L0_attn_cvb': _L0_attn_in['cvb'], 'L0_attn_ln_w': _L0_attn_in['ln_w'], 'L0_attn_ln_b': _L0_attn_in['ln_b'], 'L0_ffn_W_up': _L0_ffn_in['W_up'], 'L0_ffn_W_gate': _L0_ffn_in['W_gate'], 'L0_ffn_W_down': _L0_ffn_in['W_down']}
    _x0 = _d['L0_attn_x']
    _d['L0_attn_x'] = jax.random.normal(jax.random.fold_in(jax.random.key(seed), 1), (4, 512, 512), dtype=_x0.dtype)
    del _x0
    return _d

def reference(L0_attn_x, L0_attn_Wq, L0_attn_Wk, L0_attn_Wv, L0_attn_Wa, L0_attn_ba, L0_attn_Wb, L0_attn_bb, L0_attn_Wg, L0_attn_Wo, L0_attn_cqw, L0_attn_cqb, L0_attn_ckw, L0_attn_ckb, L0_attn_cvw, L0_attn_cvb, L0_attn_ln_w, L0_attn_ln_b, L0_ffn_W_up, L0_ffn_W_gate, L0_ffn_W_down):

    def _L0_attn_ref(x, Wq, Wk, Wv, Wa, ba, Wb, bb, Wg, Wo, cqw, cqb, ckw, ckb, cvw, cvb, ln_w, ln_b):
        import jax, jax.numpy as jnp
        import numpy as np
        from jax import lax
        B, S, HID = (4, 512, 512)
        NH, DK, DV, KW = (16, 128, 128, 4)

        def _dconv_causal(y, w, b):
            yt = jnp.transpose(y, (0, 2, 1))
            out = lax.conv_general_dilated(yt, w, window_strides=(1,), padding=[(w.shape[-1] - 1, 0)], dimension_numbers=('NCH', 'OIH', 'NCH'), feature_group_count=w.shape[0])
            return jnp.transpose(out + b[None, :, None], (0, 2, 1))

        def _delta_rule(q, k, v, a, beta):
            qs = jnp.moveaxis(q, 1, 0)
            ks = jnp.moveaxis(k, 1, 0)
            vs = jnp.moveaxis(v, 1, 0)
            as_ = jnp.moveaxis(a, 1, 0)
            bs = jnp.moveaxis(beta, 1, 0)

            def step(St, inp):
                q_t, k_t, v_t, a_t, b_t = inp
                err = jnp.einsum('bhvk,bhk->bhv', St, k_t) - v_t
                St = a_t[..., None] * St - (b_t[..., None] * err)[..., None] * k_t[:, :, None, :]
                o_t = jnp.einsum('bhvk,bhk->bhv', St, q_t)
                return (St, o_t)
            S0 = jnp.zeros(q.shape[:1] + (q.shape[2], v.shape[3], q.shape[3]), q.dtype)
            _, os_ = lax.scan(step, S0, (qs, ks, vs, as_, bs))
            return jnp.moveaxis(os_, 0, 1)
        b, s, _ = x.shape
        silu = lambda z: z * jax.nn.sigmoid(z)
        q = silu(_dconv_causal(x @ Wq, cqw, cqb))
        k = silu(_dconv_causal(x @ Wk, ckw, ckb))
        v = silu(_dconv_causal(x @ Wv, cvw, cvb))
        q = q.reshape(b, s, NH, DK)
        k = k.reshape(b, s, NH, DK) * DK ** (-0.5)
        v = v.reshape(b, s, NH, DV)
        a = jax.nn.sigmoid(x @ Wa + ba).reshape(b, s, NH, DV)
        beta = jax.nn.sigmoid(x @ Wb + bb)
        o = _delta_rule(q, k, v, a, beta)
        mu = jnp.mean(o, axis=-1, keepdims=True)
        var = jnp.mean(jnp.square(o - mu), axis=-1, keepdims=True)
        o = (o - mu) * lax.rsqrt(var + 1e-05) * ln_w + ln_b
        g = jax.nn.sigmoid(x @ Wg).reshape(b, s, NH, DV)
        o = (o * g).reshape(b, s, NH * DV)
        return o @ Wo

    def _L0_ffn_ref(x, W_up, W_gate, W_down):
        import jax, jax.numpy as jnp
        import numpy as np
        D_MODEL = 512
        D_EXPERT = 2048
        EPS = 1e-08

        def ternary_quant(w):
            scale = jnp.mean(jnp.abs(w)) + EPS
            q = jnp.clip(jnp.round(w / scale), -1.0, 1.0) * scale
            return w + jax.lax.stop_gradient(q - w)
        wu = ternary_quant(W_up)
        wg = ternary_quant(W_gate)
        wd = ternary_quant(W_down)
        up = jnp.einsum('bsd,ed->bse', x, wu)
        gate = jnp.einsum('bsd,ed->bse', x, wg)
        hidden = jax.nn.silu(up) * gate
        return jnp.einsum('bse,de->bsd', hidden, wd)
    x = L0_attn_x
    x = _layernorm(x + _L0_attn_ref(x, L0_attn_Wq, L0_attn_Wk, L0_attn_Wv, L0_attn_Wa, L0_attn_ba, L0_attn_Wb, L0_attn_bb, L0_attn_Wg, L0_attn_Wo, L0_attn_cqw, L0_attn_cqb, L0_attn_ckw, L0_attn_ckb, L0_attn_cvw, L0_attn_cvb, L0_attn_ln_w, L0_attn_ln_b), axis=-1)
    x = _layernorm(x + _L0_ffn_ref(x, L0_ffn_W_up, L0_ffn_W_gate, L0_ffn_W_down), axis=-1)
    return x

_drawn_inputs = setup_inputs


def setup_inputs(seed=0):
    import zlib

    import numpy as np

    out = dict(_drawn_inputs(seed))
    spreads = {'L0_attn_ba': (0.0, 0.8),
     'L0_attn_bb': (0.0, 0.8),
     'L0_attn_cqb': (0.0, 0.1),
     'L0_attn_ckb': (0.0, 0.1),
     'L0_attn_cvb': (0.0, 0.1),
     'L0_attn_ln_w': (1.0, 0.6),
     'L0_attn_ln_b': (0.0, 0.1)}
    factors = {'L0_attn_Wa': 4.037, 'L0_attn_Wb': 2.784}
    for name, (base, spread) in spreads.items():
        noise = np.random.default_rng([zlib.crc32(name.encode()), seed]).standard_normal(out[name].shape)
        drawn = base * np.exp(spread * noise) if base else spread * noise
        out[name] = jnp.asarray(drawn.astype(out[name].dtype))
    for name, factor in factors.items():
        out[name] = (out[name] * factor).astype(out[name].dtype)
    return out
```

```python
import numpy as np
import concourse.bass as bass
from concourse import mybir
from contextlib import ExitStack

F32 = mybir.dt.float32
F32R = mybir.dt.float32r
ALU = mybir.AluOpType
ACT = mybir.ActivationFunctionType
AX = mybir.AxisListType

P = 128
B, S, HID = 4, 512, 512
NH, DV, KW = 16, 128, 4
E = 2048
HB = NH * B
CH = 32
NCH = S // CH
BL = 8
NBL = CH // BL
KT = HID // P
TOK = B * S
CT = B * CH
Z_MIN = -17.25
EPS = 1e-5
assert CT == P and DV == P


def fp32(ap):
    return ap.bitcast(F32)


class Mem:

    def __init__(self, nc, ctx, phase):
        self.nc, self.ctx, self.phase = nc, ctx, phase

    def sb(self, name, shape, dt=F32):
        return self.ctx.enter_context(self.nc.sbuf_tensor(f"{self.phase}_{name}", shape, dt))

    def ps(self, name):
        return self.ctx.enter_context(self.nc.psum_tensor(f"{self.phase}_{name}", [P, 512], F32))

    def sem(self, name):
        return self.ctx.enter_context(self.nc.semaphore(f"{self.phase}_{name}"))


def make_identity(nc, pool, ident, sem):
    nc.gpsimd.memset(ident[:, :], 0.0).then_inc(sem, 1)
    pool.wait_ge(sem, 1)
    nc.gpsimd.affine_select(out=ident[:, :], in_=ident[:, :], compare_op=ALU.not_equal, fill=1.0,
                            base=0, pattern=[[-1, P]], channel_multiplier=1).then_inc(sem, 1)


def projections(nc, x, w_mats, ba, wb, bb, conv_w, conv_b, scr):
    with ExitStack() as ctx:
        m = Mem(nc, ctx, "pa")
        ident = m.sb("ident", [P, P])
        x_hi = m.sb("x_hi", [P, KT, TOK], F32R)
        x_lo = m.sb("x_lo", [P, KT, TOK], F32R)
        w_in = m.sb("w_in", [P, 5, KT, P])
        x_in = w_in[:, 3:5, :, :]
        w_hi = m.sb("w_hi", [P, 5, KT, P], F32R)
        w_lo = m.sb("w_lo", [P, 5, KT, P], F32R)
        y = [m.sb(f"y{i}", [P, B, KW - 1 + S]) for i in range(2)]
        cv = [m.sb(f"cv{i}", [P, B, S]) for i in range(3)]
        av = m.sb("av", [P, B, S])
        ra = m.sb("ra", [P, B, S])
        outs = {n: m.sb(f"o_{n}", [P, NCH, B, CH]) for n in ("q", "k", "ng", "vt", "A", "g")}
        r_out = m.sb("r_out", [P, 2, NCH, B, NBL])
        taps = m.sb("taps", [P, NH, 3, KW])
        cbias = m.sb("cbias", [P, NH, 3])
        ba_sb = m.sb("ba_sb", [P, NH])
        bb_sb = m.sb("bb_sb", [NH, 1])
        beta = cv[0][0:NH, :, :]
        ps = [m.ps(f"ps{i}") for i in range(8)]

        s_const = m.sem("const")
        s_id = m.sem("id")
        s_x = [m.sem(f"x{i}") for i in range(2)]
        s_xt = m.sem("xt")
        s_xhi = m.sem("xhi")
        s_xlo = m.sem("xlo")
        s_wb = m.sem("wb")
        s_bp = m.sem("bp")
        s_beta = m.sem("beta")
        s_bst = m.sem("bst")
        s_bb = m.sem("bb")
        s_w = [m.sem(f"w{i}") for i in range(5)]
        s_whi = m.sem("whi")
        s_wlo = m.sem("wlo")
        s_mm = m.sem("mm")
        s_y = m.sem("y")
        s_zero = m.sem("zero")
        s_tap = m.sem("tap")
        s_silu = m.sem("silu")
        s_z = m.sem("z")
        s_exp = m.sem("exp")
        s_a = m.sem("a")
        s_ra = m.sem("ra")
        s_ng = m.sem("ng")
        s_g = m.sem("g")
        s_pr = m.sem("pr")
        s_vt = m.sem("vt")
        s_st = {n: m.sem(f"st_{n}") for n in ("q", "k", "ng", "vt", "A", "g", "r")}

        x_rows = x.rearrange("b (s p) d -> (b s) p d", p=P)
        NT = TOK // P
        w_dram = [w.rearrange("(k p) (h c) -> p h k c", p=P, c=P) for w in w_mats]
        st_dram = {n: scr[n].rearrange("n c h t -> c h n t") for n in outs}
        A, G = 3, 4
        YB = (0, 1, 0)
        PER_MAT = B
        TILES = 5 * PER_MAT
        bank = [ps[j % 5] for j in range(TILES)]
        N_PR = 21
        block = ctx.enter_context(nc.Block())

        @block.sync
        def _(sp):
            with nc.allow_non_contiguous_dma(reason="small constants, channels on the partitions"):
                for n in range(3):
                    sp.dma_start(taps[:, :, n, :], conv_w[n].rearrange("(h c) o k -> c h (o k)", c=P)).then_inc(s_const, 16)
                    sp.dma_start(cbias[:, :, n], conv_b[n].rearrange("(h c) -> c h", c=P)).then_inc(s_const, 16)
                sp.dma_start(ba_sb[:, :], ba.rearrange("(h c) -> c h", c=P)).then_inc(s_const, 16)
                sp.dma_start(bb_sb[:, :], bb.rearrange("(h o) -> h o", o=1)).then_inc(s_const, 16)
            for i in range(NT):
                if i >= 2:
                    sp.wait_ge(s_xt, i - 1)
                sp.dma_start(x_in[:, i % 2, :, :], x_rows[i, :, :].rearrange("p (k d) -> p k d", k=KT)).then_inc(s_x[i % 2], 16)
            sp.wait_ge(s_zero, 1)
            sp.dma_start(w_in[:, 0, :, 0:NH], wb.rearrange("(k p) h -> p k h", p=P)).then_inc(s_wb, 16)
            sp.wait_ge(s_beta, B)
            for b in range(B):
                sp.dma_start(scr["beta"].rearrange("h (c b t) -> h b c t", b=B, t=CH)[:, b, :, :],
                             beta[:, b, :].rearrange("h (c t) -> h c t", t=CH)).then_inc(s_bst, 16)
            sp.wait_ge(s_wlo, 1)
            sp.wait_ge(s_xt, NT)
            for mat in range(5):
                sp.dma_start(w_in[:, mat, :, :], w_dram[mat][:, 0, :, :]).then_inc(s_w[mat], 16)
            sp.wait_ge(s_bst, 16 * B)

            def head(h, more):
                if more:
                    sp.wait_ge(s_wlo, 5 * h + 6)
                    for mat in range(5):
                        sp.dma_start(w_in[:, mat, :, :], w_dram[mat][:, h + 1, :, :]).then_inc(s_w[mat], 16)
                sp.wait_ge(s_st["ng"], 16 * h)
                sp.dma_start(outs["ng"][:, :, :, :].rearrange("p c b t -> p (c b t)"),
                             scr["beta"][h, :].partition_broadcast(P)).then_inc(s_bb, 16)

                def store(n):
                    sp.dma_start(st_dram[n][:, h, :, :], outs[n][:, :, :, :].rearrange("p n b t -> p n (b t)")).then_inc(s_st[n], 16)

                sp.wait_ge(s_silu, 3 * h + 2)
                store("q")
                store("k")
                sp.wait_ge(s_ng, h + 1)
                store("ng")
                sp.wait_ge(s_g, 4 * h + 8)
                store("g")
                sp.wait_ge(s_pr, N_PR * (h + 1))
                store("A")
                for i in range(2):
                    sp.dma_start(scr["r"].rearrange("i n c h b k -> i c h n (b k)")[i, :, h, :, :],
                                 r_out[:, i, :, :, :].rearrange("p n b k -> p n (b k)")).then_inc(s_st["r"], 16)
                sp.wait_ge(s_vt, h + 1)
                store("vt")

            with sp.Fori(0, NH - 1) as h:
                head(h, True)
            head(NH - 1, False)
            for n in s_st:
                sp.wait_ge(s_st[n], (32 if n == "r" else 16) * NH)

        @block.gpsimd
        def _(pool):
            make_identity(nc, pool, ident, s_id)
            nc.gpsimd.memset(w_in[:, 0, :, :], 0.0).then_inc(s_zero, 1)
            for i in range(2):
                nc.gpsimd.memset(y[i][:, :, 0:KW - 1], 0.0).then_inc(s_zero, 1)
            nc.gpsimd.memset(r_out[:, :, :, :, :], 0.0).then_inc(s_g, 4)
            at = lambda t, i: t[:, :, :].rearrange("p b (c n i) -> p i b c n", n=NBL, i=BL)[:, i]
            to = lambda t, i: t[:, :, :, :].rearrange("p c b (n i) -> p i b c n", i=BL)[:, i]
            tA, tI = outs["A"], outs["vt"]
            rv = r_out[:, :, :, :, :].rearrange("p i c b n -> p i b c n")
            mid = BL // 2
            nc.gpsimd.memset(to(tA, mid - 1), 1.0)

            def head(h):
                n = [0]

                def step(ins):
                    n[0] += 1
                    ins.then_inc(s_pr, 1)
                    return n[0]

                def mul(out, in0, in1, after=None):
                    if after:
                        pool.wait_ge(s_pr, N_PR * h + after)
                    return step(nc.gpsimd.tensor_tensor(out, in0, in1, ALU.mult))

                pool.wait_ge(s_a, h + 1)
                pool.wait_ge(s_st["vt"], 16 * h)
                k = mul(to(tI, 2), at(av, 3), at(av, 2))
                k = mul(to(tI, 1), to(tI, 2), at(av, 1), k)
                k = mul(to(tI, 0), to(tI, 1), at(av, 0), k)
                step(nc.gpsimd.memset(to(tI, mid), 1.0))
                step(nc.gpsimd.tensor_copy(to(tI, mid - 1), at(av, mid - 1)))
                pool.wait_ge(s_ra, h + 1)
                k = mul(to(tI, 6), at(ra, 4), at(ra, 5))
                k = mul(to(tI, 7), to(tI, 6), at(ra, 6), k)
                step(nc.gpsimd.tensor_copy(to(tI, 5), at(ra, 4)))
                pool.wait_ge(s_st["A"], 16 * h)
                k = mul(to(tA, 1), at(ra, 3), at(ra, 2))
                step(nc.gpsimd.tensor_copy(to(tA, 2), at(ra, 3)))
                k = mul(to(tA, 0), to(tA, 1), at(ra, 1), k)
                step(nc.gpsimd.tensor_copy(to(tA, 4), at(av, 4)))
                k = mul(to(tA, 5), at(av, 4), at(av, 5))
                k = mul(to(tA, 6), to(tA, 5), at(av, 6), k)
                k = mul(to(tA, 7), to(tA, 6), at(av, 7), k)
                pool.wait_ge(s_st["r"], 32 * h)
                mul(rv[:, 0, :, :, 1:], to(tA, 7)[:, :, :, :-1], to(tI, 0)[:, :, :, 1:], k)
                k = mul(rv[:, 0, :, 1:, 0:1], to(tA, 7)[:, :, :-1, NBL - 1:], to(tI, 0)[:, :, 1:, 0:1])
                for j in range(1, NBL):
                    before = rv[:, 1, :, :, j - 1:j] if j > 1 else rv[:, 0, :, :, 0:1]
                    k = mul(rv[:, 1, :, :, j:j + 1], before, rv[:, 0, :, :, j:j + 1], k)
                step(nc.gpsimd.tensor_copy(rv[:, 1, :, :, 0:1], rv[:, 0, :, :, 0:1]))
                assert n[0] == N_PR

            with pool.Fori(0, NH) as h:
                head(h)

        @block.scalar
        def _(act):
            for i in range(NT):
                act.wait_ge(s_xt, i + 1)
                nc.scalar.activation(x_hi[:, :, i * P:(i + 1) * P], ps[i % 4][:, :].rearrange("p (k t) -> p k t", k=KT), ACT.Copy).then_inc(s_xhi, 1)

            def split_hi(mat):
                nc.scalar.activation(w_hi[:, mat, :, :], w_in[:, mat, :, :], ACT.Copy).then_inc(s_whi, 1)

            act.wait_ge(s_wb, 16)
            split_hi(0)
            act.wait_ge(s_const, 128)
            for b in range(B):
                act.wait_ge(s_bp, b + 1)
                nc.scalar.activation(beta[:, b, :], ps[b][0:NH, :], ACT.Sigmoid, bias=bb_sb[:, 0:1]).then_inc(s_beta, 1)
            for mat in range(5):
                act.wait_ge(s_w[mat], 16)
                if mat == 0:
                    act.wait_ge(s_bp, B)
                split_hi(mat)

            def head(h, more):
                def split(mat):
                    if more:
                        act.wait_ge(s_w[mat], 16 * h + 32)
                        act.wait_ge(s_mm, TILES * h + PER_MAT * (mat + 1))
                        split_hi(mat)

                for mat in range(3):
                    if mat == 0:
                        act.wait_ge(s_tap, 12 * h)
                    if mat == 2:
                        act.wait_ge(s_tap, 12 * h + KW)
                    for b in range(B):
                        act.wait_ge(s_mm, TILES * h + PER_MAT * mat + b + 1)
                        nc.scalar.activation(y[YB[mat]][:, b, KW - 1:], bank[PER_MAT * mat + b][:, :], ACT.Copy).then_inc(s_y, 1)
                    split(mat)
                for mat, n in ((0, "q"), (1, "k"), (2, None)):
                    act.wait_ge(s_tap, 12 * h + KW * (mat + 1))
                    if n:
                        act.wait_ge(s_st[n], 16 * h)
                        out = outs[n][:, :, :, :].rearrange("p c b t -> p b c t")
                        nc.scalar.activation(out, cv[mat][:, :, :].rearrange("p b (c t) -> p b c t", t=CH), ACT.Silu).then_inc(s_silu, 1)
                    else:
                        nc.scalar.activation(cv[mat][:, :, :], cv[mat][:, :, :], ACT.Silu).then_inc(s_silu, 1)
                act.wait_ge(s_z, 4 * h + 4)
                act.wait_ge(s_pr, N_PR * h)
                act.wait_ge(s_ng, h)
                nc.scalar.activation(ra[:, :, :], av[:, :, :], ACT.Exp, scale=-1.0).then_inc(s_exp, 1)
                act.wait_ge(s_exp, h + 1)
                nc.scalar.activation(av[:, :, :], av[:, :, :], ACT.Sigmoid).then_inc(s_a, 1)
                split(A)
                act.wait_ge(s_st["g"], 16 * h)
                for b in range(B):
                    act.wait_ge(s_mm, TILES * h + PER_MAT * G + b + 1)
                    nc.scalar.activation(outs["g"][:, :, b, :], bank[PER_MAT * G + b][:, :].rearrange("p (c t) -> p c t", t=CH), ACT.Sigmoid).then_inc(s_g, 1)
                split(G)

            with act.Fori(0, NH - 1) as h:
                head(h, True)
            head(NH - 1, False)

        @block.tensor
        def _(pe):
            pe.wait_ge(s_id, 2)
            for i in range(NT):
                pe.wait_ge(s_x[i % 2], 16 * (i // 2 + 1))
                if i >= 4:
                    pe.wait_ge(s_xlo, i - 3)
                for k in range(KT):
                    last = nc.tensor.transpose(ps[i % 4][:, k * P:(k + 1) * P], x_in[:, i % 2, k, :], ident[:, :])
                last.then_inc(s_xt, 1)
            pe.wait_ge(s_xlo, NT)

            def product(out, mat, b):
                passes = [(w_hi, x_hi), (w_hi, x_lo), (w_lo, x_hi)]
                for k in range(KT):
                    for n, (w, xx) in enumerate(passes):
                        last = nc.tensor.matmul(out, w[:, mat, k, :], xx[:, k, b * S:(b + 1) * S],
                                                start=(k == 0 and n == 0), stop=(k == KT - 1 and n == 2))
                return last

            pe.wait_ge(s_wlo, 1)
            for b in range(B):
                product(ps[b][:, :], 0, b).then_inc(s_bp, 1)
            pe.wait_ge(s_beta, B)

            with pe.Fori(0, NH) as h:
                for mat in range(5):
                    pe.wait_ge(s_wlo, 5 * h + mat + 2)
                    for b in range(B):
                        j = PER_MAT * mat + b
                        before = j - 5
                        if before < 0 and j == 0:
                            pe.wait_ge(s_z, 4 * h)
                        elif before < 0:
                            pe.wait_ge(s_g, 4 * h + j)
                        elif before < 3 * PER_MAT:
                            pe.wait_ge(s_y, 12 * h + before + 1)
                        else:
                            pe.wait_ge(s_z, 4 * h + before - 3 * PER_MAT + 1)
                        product(bank[j][:, :], mat, b).then_inc(s_mm, 1)

        @block.vector
        def _(dve):
            for i in range(NT):
                dve.wait_ge(s_xhi, i + 1)
                nc.vector.tensor_tensor(x_lo[:, :, i * P:(i + 1) * P], ps[i % 4][:, :].rearrange("p (k t) -> p k t", k=KT),
                                        fp32(x_hi[:, :, i * P:(i + 1) * P]), ALU.subtract).then_inc(s_xlo, 1)

            def split_lo(mat):
                nc.vector.tensor_tensor(w_lo[:, mat, :, :], w_in[:, mat, :, :], fp32(w_hi[:, mat, :, :]), ALU.subtract).then_inc(s_wlo, 1)

            dve.wait_ge(s_whi, 1)
            split_lo(0)
            for mat in range(5):
                dve.wait_ge(s_whi, 2 + mat)
                if mat == 0:
                    dve.wait_ge(s_bp, B)
                split_lo(mat)
            dve.wait_ge(s_const, 128)
            dve.wait_ge(s_bst, 16 * B)

            def head(h, more):
                def split(mat):
                    if more:
                        dve.wait_ge(s_whi, 5 * h + mat + 7)
                        split_lo(mat)

                for mat in range(3):
                    dve.wait_ge(s_y, 12 * h + 4 * mat + 4)
                    dve.wait_ge(s_silu, 3 * h)
                    if mat == 0:
                        dve.wait_ge(s_zero, 3)
                    if mat == 2:
                        dve.wait_ge(s_vt, h)
                    yy, out = y[YB[mat]], cv[mat][:, :, :]
                    tap = lambda k: taps[:, bass.ds(h, 1), mat, k:k + 1].rearrange("p a k -> p (a k)")
                    bias = cbias[:, bass.ds(h, 1), mat:mat + 1].rearrange("p a k -> p (a k)")
                    nc.vector.tensor_scalar(out, yy[:, :, KW - 1:], tap(KW - 1), bias, ALU.mult, ALU.add).then_inc(s_tap, 1)
                    for k in range(KW - 1):
                        dve.wait_ge(s_tap, 12 * h + KW * mat + k + 1)
                        nc.vector.scalar_tensor_tensor(out=out, in0=yy[:, :, k:k + S], scalar=tap(k), in1=out,
                                                       op0=ALU.mult, op1=ALU.add).then_inc(s_tap, 1)
                    split(mat)
                dve.wait_ge(s_pr, N_PR * h)
                for b in range(B):
                    dve.wait_ge(s_mm, TILES * h + PER_MAT * A + b + 1)
                    nc.vector.tensor_scalar(av[:, b, :], bank[PER_MAT * A + b][:, :], ba_sb[:, bass.ds(h, 1)], Z_MIN,
                                            ALU.add, ALU.max).then_inc(s_z, 1)
                split(A)
                dve.wait_ge(s_exp, h + 1)
                nc.vector.tensor_scalar(ra[:, :, :], ra[:, :, :], 1.0, None, ALU.add).then_inc(s_ra, 1)
                dve.wait_ge(s_ra, h + 1)
                dve.wait_ge(s_bb, 16 * h + 16)
                tile = lambda t, b: t[:, b, :].rearrange("p (c t) -> p c t", t=CH)
                for b in range(B):
                    out = outs["ng"][:, :, b, :]
                    last = nc.vector.scalar_tensor_tensor(out=out, in0=tile(ra, b), scalar=-1.0 / DV, in1=out,
                                                          op0=ALU.mult, op1=ALU.mult)
                last.then_inc(s_ng, 1)
                split(G)
                dve.wait_ge(s_silu, 3 * h + 3)
                dve.wait_ge(s_pr, N_PR * (h + 1))
                for b in range(B):
                    out = outs["vt"][:, :, b, :]
                    last = nc.vector.scalar_tensor_tensor(out=out, in0=tile(cv[2], b), scalar=float(DV) ** 0.5, in1=out,
                                                          op0=ALU.mult, op1=ALU.mult)
                last.then_inc(s_vt, 1)

            with dve.Fori(0, NH - 1) as h:
                head(h, True)
            head(NH - 1, False)


def recurrence(nc, scr):
    GR = HB // 4
    PAIRS = BL * (BL - 1) // 2
    off = [sum(BL - 1 - i for i in range(j)) for j in range(BL)]
    HALF = HB // 2
    with ExitStack() as ctx:
        m = Mem(nc, ctx, "pb")
        kq = [m.sb(f"kq{i}", [P, 2, HB, CH]) for i in range(2)]
        ng = m.sb("ng", [P, HB, CH])
        rr = [m.sb(f"rr{i}", [P, 2, HB, NBL]) for i in range(2)]
        vt = m.sb("vt", [P, HB, CH])
        A = m.sb("A", [P, HB, CH])
        W = m.sb("W", [P, HB, CH])
        O = m.sb("O", [P, HB, CH])
        X = m.sb("X", [P, HB, CH])
        XT = m.sb("XT", [P, GR, P])
        KTr = m.sb("KT", [P, GR, P])
        Gm = m.sb("Gm", [P, GR, 256])
        mask = m.sb("mask", [P, 256])
        U = m.sb("U", [P, HB, P])
        UT = m.sb("UT", [P, HB, P])
        prod = m.sb("prod", [P, HB, PAIRS])
        gb = [m.sb(f"gb{i}", [P, HB, PAIRS]) for i in range(2)]
        tmp = m.sb("tmp", [P, HB, BL - 1])
        tk = m.sb("tk", [P, HB, BL])
        ident = m.sb("ident", [P, P])
        ones = m.sb("ones", [P, P])
        ps = [m.ps(f"ps{i}") for i in range(8)]
        psG, psT, psD = ps[0:2], ps[2:4], ps[4:8]

        s_id = m.sem("id")
        s_mask = m.sem("mask")
        s_init = m.sem("init")
        s_kq = [m.sem(f"kq{i}") for i in range(2)]
        s_ngl = m.sem("ngl")
        s_rl = [m.sem(f"rl{i}") for i in range(2)]
        s_vl = m.sem("vl")
        s_al = m.sem("al")
        s_prod = m.sem("prod")
        s_gp = m.sem("gp")
        s_ge = m.sem("ge")
        s_tp = m.sem("tp")
        s_te = m.sem("te")
        s_dp = m.sem("dp")
        s_de = m.sem("de")
        s_w = m.sem("w")
        s_x = m.sem("x")
        s_mul = m.sem("mul")
        s_add = m.sem("add")
        s_tk = m.sem("tk")
        s_wn = m.sem("wn")
        s_rs = m.sem("rs")
        s_us = m.sem("us")
        s_o = m.sem("o")
        s_os = m.sem("os")
        T_CH, D_CH, G_CH = 36, 40, 16
        T_X, T_U, D_G, D_X, D_S = 4, 20, 8, 16, 24
        block = ctx.enter_context(nc.Block())

        @block.sync
        def _(sp):
            def load_ahead(c, p):
                for i, n in enumerate(("k", "q")):
                    sp.dma_start(kq[p][:, i, :, :].rearrange("p h t -> p (h t)"), scr[n][c, :, :, :].rearrange("p h t -> p (h t)")).then_inc(s_kq[p], 16)
                for i in range(2):
                    sp.dma_start(rr[p][:, i, :, :].rearrange("p h n -> p (h n)"), scr["r"][i, c, :, :, :, :].rearrange("p h b n -> p (h b n)")).then_inc(s_rl[p], 16)

            def chunk(c, p, more):
                sp.wait_ge(s_x, 64 * c + 2 * BL)
                sp.dma_start(ng[:, :, :].rearrange("p h t -> p (h t)"), scr["ng"][c, :, :, :].rearrange("p h t -> p (h t)")).then_inc(s_ngl, 16)
                sp.wait_ge(s_w, c)
                sp.dma_start(vt[:, :, :].rearrange("p h t -> p (h t)"), scr["vt"][c, :, :, :].rearrange("p h t -> p (h t)")).then_inc(s_vl, 16)
                sp.wait_ge(s_o, c)
                sp.dma_start(A[:, :, :].rearrange("p h t -> p (h t)"), scr["A"][c, :, :, :].rearrange("p h t -> p (h t)")).then_inc(s_al, 16)
                sp.wait_ge(s_o, c + 1)
                sp.dma_start(scr["o"][c, :, :, :].rearrange("p h t -> p (h t)"), O[:, :, :].rearrange("p h t -> p (h t)")).then_inc(s_os, 16)
                if more:
                    sp.wait_ge(s_x, 64 * c + 80)
                    sp.wait_ge(s_rs, 3 * c + 3)
                    sp.wait_ge(s_us, c + 1)
                    load_ahead(c + 2, p)

            for p in range(2):
                load_ahead(p, p)
            with sp.Fori(0, NCH // 2 - 1) as i:
                for p in range(2):
                    chunk(i * 2 + p, p, True)
            for p in range(2):
                chunk(NCH - 2 + p, p, False)
            sp.wait_ge(s_os, 16 * NCH)

        @block.gpsimd
        def _(pool):
            make_identity(nc, pool, ident, s_id)
            nc.gpsimd.memset(ones[:, :], 1.0).then_inc(s_init, 1)
            nc.gpsimd.memset(U[:, :, :], 0.0).then_inc(s_init, 1)
            nc.gpsimd.memset(UT[:, :, :], 0.0).then_inc(s_te, 2)
            nc.gpsimd.memset(X[:, :, :], 0.0).then_inc(s_x, 2 * BL)
            nc.gpsimd.memset(tmp[:, :, :], 0.0).then_inc(s_ge, 2)
            nc.gpsimd.memset(tk[:, :, :], 0.0).then_inc(s_de, 4)
            nc.gpsimd.memset(mask[:, :], 1.0).then_inc(s_mask, 1)
            mv = mask[:, :].rearrange("p (n a i t) -> p n a i t", n=NBL, a=2, i=4)
            pool.wait_ge(s_mask, 1)
            for n in range(NBL):
                rows = mask[:, 64 * n:64 * n + 64].rearrange("p (a i t) -> p a i t", a=2, i=4)
                nc.gpsimd.affine_select(out=rows, in_=rows, compare_op=ALU.is_ge, fill=0.0, base=0,
                                        pattern=[[0, 2], [-CH, 4], [0, BL]], channel_multiplier=1).then_inc(s_mask, 1)
                pool.wait_ge(s_mask, 3 * n + 2)
                nc.gpsimd.affine_select(out=rows[:, 0, :, :], in_=rows[:, 0, :, :], compare_op=ALU.is_ge, fill=0.0, base=BL * n,
                                        pattern=[[CH, 4], [1, BL]], channel_multiplier=-1).then_inc(s_mask, 1)
                nc.gpsimd.affine_select(out=rows[:, 1, :, :], in_=rows[:, 1, :, :], compare_op=ALU.is_ge, fill=0.0, base=BL * n + BL - 1,
                                        pattern=[[CH, 4], [0, BL]], channel_multiplier=-1).then_inc(s_mask, 1)

            def products(c, p, n):
                pool.wait_ge(s_gp, G_CH * c + 4 * n)
                for j in range(BL - 1):
                    w = BL - 1 - j
                    k = kq[p][:, 0, :, BL * n:BL * (n + 1)]
                    last = nc.gpsimd.tensor_tensor(prod[:, :, off[j]:off[j] + w], k[:, :, j + 1:],
                                                   k[:, :, j:j + 1].broadcast_to([P, HB, w]), ALU.mult)
                last.then_inc(s_prod, 1)

            def chunk(c, i, p):
                pool.wait_ge(s_kq[p], 32 * i + 32)
                products(c, p, 0)
                pool.wait_ge(s_rl[p], 32 * i + 32)
                pool.wait_ge(s_tp, T_CH * c)
                nc.gpsimd.tensor_tensor(U[:, :, :], U[:, :, :], rr[p][:, 1, :, NBL - 1:NBL].broadcast_to([P, HB, P]), ALU.mult).then_inc(s_us, 1)
                products(c, p, 1)
                for n in range(NBL - 1):
                    pool.wait_ge(s_tp, T_CH * c + T_X + 4 * (n + 1))
                    xx = X[:, :, 0:BL * (n + 1)]
                    nc.gpsimd.tensor_tensor(xx, xx, rr[p][:, 0, :, n + 1:n + 2].broadcast_to([P, HB, BL * (n + 1)]), ALU.mult).then_inc(s_rs, 1)
                    if n + 2 < NBL:
                        products(c, p, n + 2)

            pool.wait_ge(s_init, 2)
            with pool.Fori(0, NCH // 2) as i:
                for p in range(2):
                    chunk(i * 2 + p, i, p)

        @block.scalar
        def _(act):
            def copy_t(c, j, out):
                act.wait_ge(s_tp, T_CH * c + j + 1)
                nc.scalar.activation(out, psT[j % 2][:, :].rearrange("p (g k) -> p g k", g=4), ACT.Copy).then_inc(s_te, 1)

            def copy_g(c, n):
                act.wait_ge(s_x, 2 * BL * (NBL * c + n))
                for j in range(4):
                    act.wait_ge(s_gp, G_CH * c + 4 * n + j + 1)
                    nc.scalar.activation(gb[n % 2][:, 16 * j:16 * j + 16, :], psG[j % 2][:, 0:16 * PAIRS].rearrange("p (h k) -> p h k", k=PAIRS), ACT.Copy).then_inc(s_ge, 1)

            with act.Fori(0, NCH) as c:
                for j in range(4):
                    copy_t(c, j, KTr[:, 4 * j:4 * j + 4, :])
                copy_g(c, 0)
                for n in range(NBL):
                    if n + 1 < NBL:
                        copy_g(c, n + 1)
                    for j in range(4):
                        copy_t(c, T_X + 4 * n + j, XT[:, 4 * j:4 * j + 4, :])
                for j in range(16):
                    copy_t(c, T_U + j, UT[:, 4 * j:4 * j + 4, :])

        @block.tensor
        def _(pe):
            pe.wait_ge(s_id, 2)
            pe.wait_ge(s_init, 1)

            def transposes(c, j, srcs):
                pe.wait_ge(s_te, T_CH * c + j + 1)
                for q, src in enumerate(srcs):
                    last = nc.tensor.transpose(psT[j % 2][:, q * P:(q + 1) * P], src, ident[:, :])
                last.then_inc(s_tp, 1)

            def sums(c, n):
                pe.wait_ge(s_prod, NBL * c + n + 1)
                for j in range(4):
                    pe.wait_ge(s_ge, G_CH * c + 4 * n + j + 1)
                    nc.tensor.matmul(psG[j % 2][:, 0:16 * PAIRS], ones[:, :], prod[:, 16 * j:16 * j + 16, :].rearrange("p h k -> p (h k)"),
                                     start=True, stop=True).then_inc(s_gp, 1)

            def bank_free(c, j):
                pe.wait_ge(s_de, D_CH * c + j + 1)
                return psD[j % 4]

            flat = lambda t: t.rearrange("p h t -> p (h t)")

            def chunk(c, i, p):
                pe.wait_ge(s_kq[p], 32 * i + 32)
                for j in range(4):
                    transposes(c, j, [flat(kq[p][:, 0, 4 * g:4 * g + 4, :]) for g in range(4 * j, 4 * j + 4)])
                sums(c, 0)
                pe.wait_ge(s_te, T_CH * c + 2)
                for j in range(8):
                    bank = bank_free(c, j)
                    for q in range(8):
                        last = nc.tensor.matmul(bank[:, 64 * q:64 * q + 64].rearrange("p (a t) -> p a t", a=2), UT[:, 8 * j + q, :],
                                                kq[p][:, :, 8 * j + q, :], start=True, stop=True)
                    last.then_inc(s_dp, 1)
                for j in range(8):
                    bank = bank_free(c, D_G + j)
                    for gg in range(2):
                        g = 2 * j + gg
                        out = bank[:, 256 * gg:256 * gg + 256].rearrange("p (n a i t) -> p n a i t", n=NBL, a=2, i=4)
                        mov = kq[p][:, :, 4 * g:4 * g + 4, :].rearrange("p a i (n t) -> p a n i t", t=BL)
                        stat = flat(kq[p][:, 0, 4 * g:4 * g + 4, :])
                        nc.tensor.matmul(out[:, :, 0, :, :], stat, mov[:, 1, :, :, :], start=True, stop=True)
                        last = nc.tensor.matmul(out[:, 0:NBL - 1, 1, :, :], stat, mov[:, 0, 1:, :, :], start=True, stop=True)
                    last.then_inc(s_dp, 1)
                for n in range(NBL):
                    if n + 1 < NBL:
                        sums(c, n + 1)
                    pe.wait_ge(s_x, 2 * BL * (NBL * c + n + 1) + 2 * BL)
                    if n:
                        pe.wait_ge(s_rs, 3 * c + n)
                    for j in range(4):
                        transposes(c, T_X + 4 * n + j, [flat(X[:, 4 * g:4 * g + 4, :]) for g in range(4 * j, 4 * j + 4)])
                    if n == 0:
                        pe.wait_ge(s_de, D_CH * c + D_X + 4)
                    w = 64 if n + 1 < NBL else 32
                    for j in range(2):
                        pe.wait_ge(s_te, T_CH * c + T_X + 4 * n + 2 * j + 4)
                        bank = bank_free(c, D_X + 2 * n + j)
                        for q in range(8):
                            g = 8 * j + q
                            last = nc.tensor.matmul(bank[:, 64 * q:64 * q + w], XT[:, g, :], Gm[:, g, 64 * n:64 * n + w], start=True, stop=True)
                        last.then_inc(s_dp, 1)

                def state(r):
                    for q in range(4):
                        for t in range(4):
                            g = 4 * r + q
                            rows = slice(32 * t, 32 * t + 32)
                            if q == 0:
                                bank_free(c, D_S + 4 * r + t)
                            last = nc.tensor.matmul(psD[t][:, q * P:(q + 1) * P], XT[rows, g, :], KTr[rows, g, :], start=True, stop=True)
                            if q == 3:
                                last.then_inc(s_dp, 1)

                def new_state(r):
                    pe.wait_ge(s_de, D_CH * c + D_S + 4 * (r + 1) + 4)
                    for j in range(4 * r, 4 * r + 4):
                        transposes(c, T_U + j, [U[:, 4 * j + q, :] for q in range(4)])

                state(0)
                for r in range(4):
                    if r < 3:
                        state(r + 1)
                    new_state(r)

            with pe.Fori(0, NCH // 2) as i:
                for p in range(2):
                    chunk(i * 2 + p, i, p)

        @block.vector
        def _(dve):
            tt = nc.vector.tensor_tensor
            blocks = lambda t: t.rearrange("p h (n t) -> p h n t", t=BL)
            dve.wait_ge(s_mask, 13)

            def tile(c, j):
                dve.wait_ge(s_dp, D_CH * c + j + 1)
                return psD[j % 4]

            def chunk(c, i, p):
                dve.wait_ge(s_rl[p], 32 * i + 32)
                dve.wait_ge(s_os, 16 * c)
                for j in range(8):
                    src = tile(c, j)[:, :].rearrange("p (h a t) -> p h a t", h=8, a=2)
                    hs = slice(8 * j, 8 * j + 8)
                    cr = rr[p][:, 1, hs, :].unsqueeze(3).broadcast_to([P, 8, NBL, BL])
                    tt(blocks(W[:, hs, :]), blocks(src[:, :, 0, :]), cr, ALU.mult)
                    tt(blocks(O[:, hs, :]), blocks(src[:, :, 1, :]), cr, ALU.mult).then_inc(s_de, 1)
                dve.wait_ge(s_vl, 16 * c + 16)
                dve.wait_ge(s_de, D_CH * c + D_G + 4)
                tt(W[:, :, :], W[:, :, :], vt[:, :, :], ALU.subtract).then_inc(s_w, 1)
                for j in range(8):
                    src = tile(c, D_G + j)[:, :].rearrange("p (g n) -> p g n", g=2)[:, :, 0:224]
                    tt(Gm[:, 2 * j:2 * j + 2, 0:224], src, mask[:, 0:224].unsqueeze(1).broadcast_to([P, 2, 224]), ALU.mult).then_inc(s_de, 1)
                dve.wait_ge(s_ngl, 16 * c + 16)
                halves = [(hf, slice(HALF * hf, HALF * (hf + 1))) for hf in range(2)]
                for n in range(NBL):
                    m14 = 14 * (NBL * c + n)
                    x0 = 2 * BL * (NBL * c + n) + 2 * BL
                    dve.wait_ge(s_ge, G_CH * c + 4 * n + 4 + 2)
                    if n == 0:
                        dve.wait_ge(s_w, c + 1)
                    for t in range(BL):
                        at = BL * n + t
                        for hf, hs in halves:
                            if t == 0 and n:
                                dve.wait_ge(s_wn, 6 * c + 2 * (n - 1) + hf + 1)
                            if t:
                                dve.wait_ge(s_add, m14 + 2 * (t - 1) + hf + 1)
                            tt(X[:, hs, at], ng[:, hs, at], W[:, hs, at], ALU.mult).then_inc(s_x, 1)
                        if t == BL - 1:
                            break
                        w = BL - 1 - t
                        for hf, hs in halves:
                            dve.wait_ge(s_x, x0 + 2 * t + hf + 1)
                            tt(tmp[:, hs, 0:w], gb[n % 2][:, hs, off[t]:off[t] + w], X[:, hs, at:at + 1].broadcast_to([P, HALF, w]),
                               ALU.mult).then_inc(s_mul, 1)
                        for hf, hs in halves:
                            dve.wait_ge(s_mul, m14 + 2 * t + hf + 1)
                            ww = W[:, hs, at + 1:BL * (n + 1)]
                            tt(ww, ww, tmp[:, hs, 0:w], ALU.add).then_inc(s_add, 1)
                    for j in range(2):
                        src = tile(c, D_X + 2 * n + j)[:, :].rearrange("p (g a i t) -> p g a i t", g=8, a=2, i=4)
                        hs = slice(HALF * j, HALF * (j + 1))
                        groups = lambda t: t.rearrange("p (g i) t -> p g i t", i=4)
                        if n + 1 < NBL:
                            rb = groups(rr[p][:, 0, hs, n + 1:n + 2]).broadcast_to([P, 8, 4, BL])
                            tt(groups(tk[:, hs, :]), src[:, :, 1, :, :], rb, ALU.mult).then_inc(s_tk, 1)
                        oo = groups(O[:, hs, BL * n:BL * (n + 1)])
                        tt(oo, oo, src[:, :, 0, :, :], ALU.add).then_inc(s_de, 1)
                        if n + 1 < NBL:
                            dve.wait_ge(s_tk, 6 * c + 2 * n + j + 1)
                            ww = W[:, hs, BL * (n + 1):BL * (n + 2)]
                            tt(ww, ww, tk[:, hs, :], ALU.add).then_inc(s_wn, 1)
                dve.wait_ge(s_al, 16 * c + 16)
                dve.wait_ge(s_de, D_CH * c + D_S + 4)
                tt(O[:, :, :], O[:, :, :], A[:, :, :], ALU.mult).then_inc(s_o, 1)
                dve.wait_ge(s_us, c + 1)
                for r in range(4):
                    for t in range(4):
                        src = tile(c, D_S + 4 * r + t)[:, :].rearrange("p (g k) -> p g k", g=4)
                        uu = U[:, 16 * r:16 * r + 16, :].rearrange("p (g i) k -> p g i k", i=4)[:, :, t, :]
                        tt(uu, uu, src, ALU.add).then_inc(s_de, 1)

            with dve.Fori(0, NCH // 2) as i:
                for p in range(2):
                    chunk(i * 2 + p, i, p)


def attention_out(nc, x, wo, ln_w, ln_b, scr, res, stat):
    with ExitStack() as ctx:
        m = Mem(nc, ctx, "pc")
        wo_in = [m.sb(f"wo_in{i}", [P, HID]) for i in range(2)]
        wo_hi = m.sb("wo_hi", [P, NH, HID], F32R)
        wo_lo = m.sb("wo_lo", [P, NH, HID], F32R)
        o_in = [m.sb(f"o_in{i}", [P, NH, CT]) for i in range(2)]
        g_in = m.sb("g_in", [P, NH, CT])
        x_in = [m.sb(f"x_in{i}", [P, HID]) for i in range(2)]
        sq = m.sb("sq", [P, NH, CT])
        og_hi = m.sb("og_hi", [P, NH, CT], F32R)
        og_lo = m.sb("og_lo", [P, NH, CT], F32R)
        lnw = m.sb("lnw", [P, 1])
        lnb = m.sb("lnb", [P, 1])
        eps = m.sb("eps", [P, 1])
        mean1 = m.sb("mean1", [P, P])
        rs = m.sb("rs", [P, HID])
        bn = m.sb("bn", [P, 6])
        bn_all = m.sb("bn_all", [P, NCH, 6])
        ps = [m.ps(f"ps{i}") for i in range(8)]

        s_c = m.sem("c")
        s_wl = [m.sem(f"wl{i}") for i in range(2)]
        s_wh = m.sem("wh")
        s_wo = m.sem("wo")
        s_o = [m.sem(f"o{i}") for i in range(2)]
        s_g = m.sem("g")
        s_x = [m.sem(f"x{i}") for i in range(2)]
        s_mu = m.sem("mu")
        s_d = m.sem("d")
        s_sq = m.sem("sq")
        s_var = m.sem("var")
        s_ln = m.sem("ln")
        s_rs = m.sem("rs")
        s_n = m.sem("n")
        s_hi = m.sem("hi")
        s_lo = m.sem("lo")
        s_p = m.sem("p")
        s_r = m.sem("r")
        s_bn = m.sem("bn")
        s_st = m.sem("st")
        block = ctx.enter_context(nc.Block())
        four = lambda t, j: t[:, 4 * j:4 * j + 4, :].rearrange("p h t -> p (h t)")

        @block.sync
        def _(sp):
            sp.dma_start(lnw[:, :], ln_w.rearrange("(p o) -> p o", o=1)).then_inc(s_c, 16)
            sp.dma_start(lnb[:, :], ln_b.rearrange("(p o) -> p o", o=1)).then_inc(s_c, 16)

            def load(c, p):
                sp.dma_start(o_in[p][:, :, :].rearrange("p h t -> p (h t)"), scr["o"][c, :, :, :].rearrange("p h t -> p (h t)")).then_inc(s_o[p], 16)
                for b in range(B):
                    sp.dma_start(x_in[p][b * CH:(b + 1) * CH, :], x.rearrange("b (c t) d -> c b t d", t=CH)[c, b, :, :]).then_inc(s_x[p], 16)

            load(0, 0)
            for h in range(NH):
                if h >= 2:
                    sp.wait_ge(s_wo, h - 1)
                sp.dma_start(wo_in[h % 2][:, :], wo[h * P:(h + 1) * P, :]).then_inc(s_wl[h % 2], 16)
            load(1, 1)

            def chunk(c, p, more):
                sp.wait_ge(s_n, 3 * c)
                sp.dma_start(g_in[:, :, :].rearrange("p h t -> p (h t)"), scr["g"][c, :, :, :].rearrange("p h t -> p (h t)")).then_inc(s_g, 16)
                if more:
                    sp.wait_ge(s_lo, c + 1)
                    sp.wait_ge(s_r, c + 1)
                    load(c + 2, p)

            with sp.Fori(0, NCH // 2 - 1) as i:
                for p in range(2):
                    chunk(i * 2 + p, p, True)
            for p in range(2):
                chunk(NCH - 2 + p, p, False)

        @block.gpsimd
        def _(pool):
            nc.gpsimd.memset(mean1[:, :], 1.0 / DV).then_inc(s_c, 1)
            nc.gpsimd.memset(eps[:, :], EPS).then_inc(s_c, 1)

        @block.scalar
        def _(act):
            for h in range(NH):
                act.wait_ge(s_wl[h % 2], 16 * (h // 2 + 1))
                nc.scalar.activation(wo_hi[:, h, :], wo_in[h % 2][:, :], ACT.Copy).then_inc(s_wh, 1)
            act.wait_ge(s_c, 34)

            def stage1(c, i, p):
                act.wait_ge(s_n, 3 * c)
                for j in range(4):
                    act.wait_ge(s_d, 4 * c + j + 1)
                    nc.scalar.activation(four(sq, j), four(o_in[p], j), ACT.Square).then_inc(s_sq, 1)
                for j in range(4):
                    act.wait_ge(s_var, 4 * c + j + 1)
                    nc.scalar.activation(four(sq, j), ps[j][:, :], ACT.Ln, bias=eps[:, 0:1]).then_inc(s_ln, 1)
                act.wait_ge(s_ln, 4 * c + 4)
                nc.scalar.activation(sq[:, :, :], sq[:, :, :], ACT.Exp, scale=-0.5).then_inc(s_rs, 1)

            def stage2(c, i, p):
                act.wait_ge(s_n, 3 * c + 3)
                act.wait_ge(s_p, c)
                nc.scalar.activation(og_hi[:, :, :], o_in[p][:, :, :], ACT.Copy).then_inc(s_hi, 1)

            stage1(0, 0, 0)
            with act.Fori(0, NCH // 2 - 1) as i:
                stage2(i * 2, i, 0)
                stage1(i * 2 + 1, i, 1)
                stage2(i * 2 + 1, i, 1)
                stage1(i * 2 + 2, i + 1, 0)
            stage2(NCH - 2, NCH // 2 - 1, 0)
            stage1(NCH - 1, NCH // 2 - 1, 1)
            stage2(NCH - 1, NCH // 2 - 1, 1)

        @block.tensor
        def _(pe):
            pe.wait_ge(s_c, 34)

            def stage1(c, i, p):
                pe.wait_ge(s_o[p], 16 * i + 16)
                pe.wait_ge(s_ln, 4 * c)
                for j in range(4):
                    nc.tensor.matmul(ps[j][:, :], mean1[:, :], four(o_in[p], j), start=True, stop=True).then_inc(s_mu, 1)

            def stage1b(c):
                for j in range(4):
                    pe.wait_ge(s_sq, 4 * c + j + 1)
                    nc.tensor.matmul(ps[j][:, :], mean1[:, :], four(sq, j), start=True, stop=True).then_inc(s_var, 1)

            def stage2(c, i, p):
                pe.wait_ge(s_lo, c + 1)
                pe.wait_ge(s_wo, NH)
                pe.wait_ge(s_r, c)
                passes = [(og_hi, wo_hi), (og_hi, wo_lo), (og_lo, wo_hi)]
                for h in range(NH):
                    for n, (og, w) in enumerate(passes):
                        last = nc.tensor.matmul(ps[4 + p][:, :], og[:, h, :], w[:, h, :], start=(h == 0 and n == 0), stop=(h == NH - 1 and n == 2))
                last.then_inc(s_p, 1)

            stage1(0, 0, 0)
            stage1b(0)
            with pe.Fori(0, NCH // 2 - 1) as i:
                for p in range(2):
                    stage1(i * 2 + p + 1, i + p, 1 - p)
                    stage2(i * 2 + p, i, p)
                    stage1b(i * 2 + p + 1)
            stage1(NCH - 1, NCH // 2 - 1, 1)
            stage2(NCH - 2, NCH // 2 - 1, 0)
            stage1b(NCH - 1)
            stage2(NCH - 1, NCH // 2 - 1, 1)

        @block.vector
        def _(dve):
            for h in range(NH):
                dve.wait_ge(s_wh, h + 1)
                nc.vector.tensor_tensor(wo_lo[:, h, :], wo_in[h % 2][:, :], fp32(wo_hi[:, h, :]), ALU.subtract).then_inc(s_wo, 1)
            dve.wait_ge(s_c, 34)

            def stage1(c, i, p):
                for j in range(4):
                    dve.wait_ge(s_mu, 4 * c + j + 1)
                    nc.vector.tensor_tensor(four(o_in[p], j), four(o_in[p], j), ps[j][:, :], ALU.subtract).then_inc(s_d, 1)

            def stage2(c, i, p):
                t = o_in[p][:, :, :]
                dve.wait_ge(s_rs, c + 1)
                nc.vector.tensor_tensor(t, t, sq[:, :, :], ALU.mult).then_inc(s_n, 1)
                dve.wait_ge(s_n, 3 * c + 1)
                nc.vector.tensor_scalar(t, t, lnw[:, 0:1], lnb[:, 0:1], ALU.mult, ALU.add).then_inc(s_n, 1)
                dve.wait_ge(s_n, 3 * c + 2)
                dve.wait_ge(s_g, 16 * c + 16)
                nc.vector.tensor_tensor(t, t, g_in[:, :, :], ALU.mult).then_inc(s_n, 1)
                dve.wait_ge(s_hi, c + 1)
                nc.vector.tensor_tensor(og_lo[:, :, :], t, fp32(og_hi[:, :, :]), ALU.subtract).then_inc(s_lo, 1)

            def stage3(c, i, p):
                dve.wait_ge(s_p, c + 1)
                dve.wait_ge(s_x[p], 64 * i + 64)
                dve.wait_ge(s_st, c)
                nc.vector.tensor_tensor(rs[:, :], ps[4 + p][:, :], x_in[p][:, :], ALU.add).then_inc(s_r, 1)
                dve.wait_ge(s_r, c + 1)
                nc.vector.bn_stats(bn[:, :], rs[:, :]).then_inc(s_bn, 1)
                nc.vector.tensor_copy(res[:, bass.ds(c, 1), :], rs[:, :].unsqueeze(1))
                dve.wait_ge(s_bn, c + 1)
                nc.vector.tensor_copy(bn_all[:, bass.ds(c, 1), :], bn[:, :].unsqueeze(1)).then_inc(s_st, 1)

            stage1(0, 0, 0)
            with dve.Fori(0, NCH // 2 - 1) as i:
                for p in range(2):
                    stage2(i * 2 + p, i, p)
                    stage1(i * 2 + p + 1, i + p, 1 - p)
                    stage3(i * 2 + p, i, p)
            stage2(NCH - 2, NCH // 2 - 1, 0)
            stage1(NCH - 1, NCH // 2 - 1, 1)
            stage3(NCH - 2, NCH // 2 - 1, 0)
            stage2(NCH - 1, NCH // 2 - 1, 1)
            stage3(NCH - 1, NCH // 2 - 1, 1)
            dve.wait_ge(s_st, NCH)
            for c in range(NCH):
                nc.vector.bn_aggr(stat[:, c, :], bn_all[:, c, :])


def ternary(nc, mats, tern, scales):
    NP = E * HID // P // HID
    COUNT = float(E * HID)
    with ExitStack() as ctx:
        m = Mem(nc, ctx, "pd")
        w = [m.sb(f"w{i}", [P, NP, HID]) for i in range(2)]
        junk = m.sb("junk", [P, 4, HID], mybir.dt.bfloat16)
        low = m.sb("low", [P, 4, HID])
        ident = m.sb("ident", [P, P])
        ones = m.sb("ones", [P, P])
        part = m.sb("part", [P, 3, 4])
        tot = m.sb("tot", [P, 3])
        half = m.sb("half", [P, 3, 2])
        ps = [m.ps(f"ps{i}") for i in range(8)]
        s_id = m.sem("id")
        s_c = m.sem("c")
        s_w = [m.sem(f"w{i}") for i in range(2)]
        s_abs = m.sem("abs")
        s_tot = m.sem("tot")
        s_sum = m.sem("sum")
        s_sc = m.sem("sc")
        s_low = m.sem("low")
        s_q = m.sem("q")
        s_tr = m.sem("tr")
        s_ev = m.sem("ev")
        block = ctx.enter_context(nc.Block())
        views = [mats[0].rearrange("(n p) d -> p n d", p=P), mats[1].rearrange("(n p) d -> p n d", p=P),
                 mats[2].rearrange("(n p) (m d) -> p n m d", p=P, d=HID)]

        @block.sync
        def _(sp):
            for i in range(3):
                if i == 2:
                    sp.wait_ge(s_tr, NP)
                dst = w[i % 2][:, :, :] if i < 2 else w[0][:, :, :].rearrange("p (n m) d -> p n m d", n=4)
                sp.dma_start(dst, views[i]).then_inc(s_w[i % 2], 16)

        @block.gpsimd
        def _(pool):
            make_identity(nc, pool, ident, s_id)
            nc.gpsimd.memset(ones[:, :], 1.0).then_inc(s_c, 1)

        @block.scalar
        def _(act):
            def absolute(i):
                act.wait_ge(s_w[i % 2], 16 * (i // 2 + 1))
                for j in range(4):
                    if i or j:
                        act.wait_ge(s_abs, 4 * i + j)
                    nc.scalar.activation(junk[:, :, :], w[i % 2][:, 4 * j:4 * j + 4, :], ACT.Abs,
                                         accum_out=part[:, i, j:j + 1]).then_inc(s_abs, 1)

            absolute(0)
            absolute(1)
            for i in range(3):
                if i == 2:
                    absolute(2)
                for n in range(0, NP):
                    act.wait_ge(s_tr, NP * i + n + 1)
                    nc.scalar.activation(dest(tern, i, n), ps[2 + n % 4][:, :].rearrange("p (k e) -> p k e", k=4), ACT.Copy).then_inc(s_ev, 1)

        @block.tensor
        def _(pe):
            pe.wait_ge(s_c, 1)
            pe.wait_ge(s_id, 2)
            for i in range(3):
                pe.wait_ge(s_tot, i + 1)
                nc.tensor.matmul(ps[i % 2][:, 0:1], ones[:, :], tot[:, i:i + 1], start=True, stop=True).then_inc(s_sum, 1)
                for n in range(NP):
                    j = NP * i + n
                    pe.wait_ge(s_q, 4 * i + n // 4 + 1)
                    if j >= 4:
                        pe.wait_ge(s_ev, j - 3)
                    for k in range(4):
                        last = nc.tensor.transpose(ps[2 + n % 4][:, k * P:(k + 1) * P], w[i % 2][:, n, k * P:(k + 1) * P], ident[:, :])
                    last.then_inc(s_tr, 1)

        @block.vector
        def _(dve):
            for i in range(3):
                dve.wait_ge(s_abs, 4 * i + 4)
                nc.vector.tensor_reduce(tot[:, i:i + 1], part[:, i, :], AX.X, ALU.add).then_inc(s_tot, 1)
                dve.wait_ge(s_sum, i + 1)
                nc.vector.tensor_scalar(scales[:, i:i + 1], ps[i % 2][:, 0:1], 1.0 / COUNT, 1e-8, ALU.mult, ALU.add).then_inc(s_sc, 1)
                dve.wait_ge(s_sc, 3 * i + 1)
                nc.vector.tensor_scalar(half[:, i, 0:1], scales[:, i:i + 1], 0.5, None, ALU.mult).then_inc(s_sc, 1)
                nc.vector.tensor_scalar(half[:, i, 1:2], scales[:, i:i + 1], -0.5, None, ALU.mult).then_inc(s_sc, 1)
                dve.wait_ge(s_sc, 3 * i + 3)
                for j in range(4):
                    ww = w[i % 2][:, 4 * j:4 * j + 4, :].rearrange("p n d -> p (n d)")
                    ll = low[:, :, :].rearrange("p n d -> p (n d)")
                    if i or j:
                        dve.wait_ge(s_q, 4 * i + j)
                    nc.vector.tensor_scalar(ll, ww, half[:, i, 1:2], None, ALU.is_lt).then_inc(s_low, 1)
                    dve.wait_ge(s_low, 4 * i + j + 1)
                    nc.vector.scalar_tensor_tensor(out=ww, in0=ww, scalar=half[:, i, 0:1], in1=ll, op0=ALU.is_gt, op1=ALU.subtract).then_inc(s_q, 1)


def dest(tern, i, n):
    if i < 2:
        return tern[i][:, :, n * P:(n + 1) * P]
    a, b = n // 4, n % 4
    return tern[2][:, 4 * b:4 * b + 4, a * P:(a + 1) * P]


def feed_forward(nc, tern, scales, res, stat, out):
    EB = E // 512
    with ExitStack() as ctx:
        m = Mem(nc, ctx, "pe")
        ident = m.sb("ident", [P, P])
        eps = m.sb("eps", [P, 1])
        rstd = m.sb("rstd", [P, NCH])
        std = m.sb("std", [P, NCH])
        x1s = [m.sb(f"x1s{i}", [P, HID]) for i in range(2)]
        xT_hi = [m.sb(f"xT_hi{i}", [P, KT, P], F32R) for i in range(2)]
        xT_lo = [m.sb(f"xT_lo{i}", [P, KT, P], F32R) for i in range(2)]
        sil = [m.sb(f"sil{i}", [P, 512]) for i in range(2)]
        hid = [m.sb(f"hid{i}", [P, 512]) for i in range(2)]
        hT_hi = [m.sb(f"hT_hi{i}", [P, 4, P], F32R) for i in range(2)]
        hT_lo = [m.sb(f"hT_lo{i}", [P, 4, P], F32R) for i in range(2)]
        ys = m.sb("ys", [P, HID])
        bn = m.sb("bn", [P, 6])
        bn_all = m.sb("bn_all", [P, NCH, 6])
        ps = [m.ps(f"ps{i}") for i in range(8)]
        s_ag = m.sem("ag")
        s_id = m.sem("id")
        s_c = m.sem("c")
        s_sd = m.sem("sd")
        s_rd = m.sem("rd")
        s_x1 = m.sem("x1")
        s_xt = m.sem("xt")
        s_xh = m.sem("xh")
        s_xl = m.sem("xl")
        s_ug = m.sem("ug")
        s_si = m.sem("si")
        s_h = m.sem("h")
        s_ht = m.sem("ht")
        s_hh = m.sem("hh")
        s_hl = m.sem("hl")
        s_dn = m.sem("dn")
        s_r = m.sem("r")
        s_bn = m.sem("bn")
        s_st = m.sem("st")
        s_y = m.sem("y")
        s_out = m.sem("out")
        block = ctx.enter_context(nc.Block())
        tile = lambda t, c: t[:, bass.ds(c, 1), :].rearrange("p o d -> p (o d)")
        out_v = out.rearrange("b (c t) d -> c b t d", t=CH)

        @block.sync
        def _(sp):
            with sp.Fori(0, NCH) as c:
                sp.wait_ge(s_y, c + 1)
                for b in range(B):
                    sp.dma_start(out_v[c, b, :, :], tile(res, c)[b * CH:(b + 1) * CH, :]).then_inc(s_out, 16)
            sp.wait_ge(s_out, 16 * B * NCH)

        @block.gpsimd
        def _(pool):
            make_identity(nc, pool, ident, s_id)
            nc.gpsimd.memset(eps[:, :], EPS).then_inc(s_c, 1)

        def split_hi(act, out, bank):
            return nc.scalar.activation(out[:, :, :], bank[:, :].rearrange("p (k t) -> p k t", k=4), ACT.Copy)

        @block.scalar
        def _(act):
            act.wait_ge(s_c, 1)
            nc.scalar.activation(std[:, :], stat[:, :, 1], ACT.Sqrt, bias=eps[:, 0:1]).then_inc(s_sd, 1)

            def x_hi(c, p):
                act.wait_ge(s_xt, c + 1)
                split_hi(act, xT_hi[p], ps[7]).then_inc(s_xh, 1)

            def silu(c, e):
                act.wait_ge(s_ug, EB * c + e + 1)
                nc.scalar.activation(sil[e % 2][:, :], ps[2 * (e % 2)][:, :], ACT.Silu, scale=scales[:, 0:1]).then_inc(s_si, 1)

            def h_hi(c, e):
                act.wait_ge(s_ht, EB * c + e + 1)
                split_hi(act, hT_hi[e % 2], ps[4 + e % 2]).then_inc(s_hh, 1)

            def chunk(c, p, more):
                silu(c, 0)
                silu(c, 1)
                h_hi(c, 0)
                silu(c, 2)
                h_hi(c, 1)
                silu(c, 3)
                if more:
                    x_hi(c + 1, 1 - p)
                h_hi(c, 2)
                h_hi(c, 3)

            x_hi(0, 0)
            with act.Fori(0, NCH // 2 - 1) as i:
                for p in range(2):
                    chunk(i * 2 + p, p, True)
            chunk(NCH - 2, 0, True)
            chunk(NCH - 1, 1, False)
            act.wait_ge(s_ag, NCH)
            nc.scalar.activation(std[:, :], stat[:, :, 1], ACT.Sqrt, bias=eps[:, 0:1]).then_inc(s_sd, 1)

        @block.tensor
        def _(pe):
            pe.wait_ge(s_id, 2)

            def x_tp(c, p):
                pe.wait_ge(s_x1, c + 1)
                pe.wait_ge(s_xl, c)
                for k in range(KT):
                    last = nc.tensor.transpose(ps[7][:, k * P:(k + 1) * P], x1s[p][:, k * P:(k + 1) * P], ident[:, :])
                last.then_inc(s_xt, 1)

            def up_gate(c, p, e):
                pe.wait_ge(s_xl, c + 1)
                pe.wait_ge(s_h, EB * c + e + (2 - 1))
                for n in range(2):
                    for k in range(KT):
                        for q, xx in enumerate((xT_hi[p], xT_lo[p])):
                            last = nc.tensor.matmul(ps[2 * (e % 2) + n][:, :], xx[:, k, :], tern[n][:, k, e * 512:(e + 1) * 512],
                                                    start=(k == 0 and q == 0), stop=(k == KT - 1 and q == 1))
                last.then_inc(s_ug, 1)

            def h_t(c, e):
                pe.wait_ge(s_h, EB * c + e + 1 + 2)
                pe.wait_ge(s_hl, EB * c + e + 1)
                for k in range(4):
                    last = nc.tensor.transpose(ps[4 + e % 2][:, k * P:(k + 1) * P], hid[e % 2][:, k * P:(k + 1) * P], ident[:, :])
                last.then_inc(s_ht, 1)

            def down(c, e):
                pe.wait_ge(s_hl, EB * c + e + 1 + 2)
                if e == 0:
                    pe.wait_ge(s_r, c)
                for k in range(4):
                    for q, hh in enumerate((hT_hi[e % 2], hT_lo[e % 2])):
                        last = nc.tensor.matmul(ps[6][:, :], hh[:, k, :], tern[2][:, 4 * e + k, :],
                                                start=(e == 0 and k == 0 and q == 0), stop=(e == EB - 1 and k == 3 and q == 1))
                last.then_inc(s_dn, 1)

            def chunk(c, p, more):
                up_gate(c, p, 0)
                up_gate(c, p, 1)
                h_t(c, 0)
                up_gate(c, p, 2)
                h_t(c, 1)
                down(c, 0)
                up_gate(c, p, 3)
                h_t(c, 2)
                down(c, 1)
                if more:
                    x_tp(c + 1, 1 - p)
                h_t(c, 3)
                down(c, 2)
                down(c, 3)

            x_tp(0, 0)
            with pe.Fori(0, NCH // 2 - 1) as i:
                for p in range(2):
                    chunk(i * 2 + p, p, True)
            chunk(NCH - 2, 0, True)
            chunk(NCH - 1, 1, False)

        @block.vector
        def _(dve):
            nc.vector.memset(bn[:, :], 0.0).then_inc(s_h, 2)
            nc.vector.memset(rstd[:, :], 0.0).then_inc(s_hl, 2)
            dve.wait_ge(s_sd, 1)
            dve.wait_ge(s_hl, 2)
            nc.vector.reciprocal(rstd[:, :], std[:, :]).then_inc(s_rd, 1)
            dve.wait_ge(s_rd, 1)

            def x1(c, p):
                nc.vector.tensor_scalar(x1s[p][:, :], tile(res, c), stat[:, bass.ds(c, 1), 0:1].rearrange("p o d -> p (o d)"),
                                        rstd[:, bass.ds(c, 1)], ALU.subtract, ALU.mult).then_inc(s_x1, 1)

            def x_lo(c, p):
                dve.wait_ge(s_xh, c + 1)
                nc.vector.tensor_tensor(xT_lo[p][:, :, :], ps[7][:, :].rearrange("p (k t) -> p k t", k=4), fp32(xT_hi[p][:, :, :]), ALU.subtract).then_inc(s_xl, 1)

            def hidden(c, e):
                dve.wait_ge(s_si, EB * c + e + 1)
                nc.vector.scalar_tensor_tensor(out=hid[e % 2][:, :], in0=ps[2 * (e % 2) + 1][:, :], scalar=scales[:, 1:2], in1=sil[e % 2][:, :],
                                               op0=ALU.mult, op1=ALU.mult).then_inc(s_h, 1)

            def h_lo(c, e):
                dve.wait_ge(s_hh, EB * c + e + 1)
                nc.vector.tensor_tensor(hT_lo[e % 2][:, :, :], ps[4 + e % 2][:, :].rearrange("p (k t) -> p k t", k=4), fp32(hT_hi[e % 2][:, :, :]), ALU.subtract).then_inc(s_hl, 1)

            def chunk(c, p, more):
                if more:
                    dve.wait_ge(s_r, c)
                    x1(c + 1, 1 - p)
                hidden(c, 0)
                hidden(c, 1)
                h_lo(c, 0)
                hidden(c, 2)
                h_lo(c, 1)
                hidden(c, 3)
                if more:
                    x_lo(c + 1, 1 - p)
                h_lo(c, 2)
                h_lo(c, 3)
                dve.wait_ge(s_dn, EB * (c + 1))
                dve.wait_ge(s_x1, c + 1)
                dve.wait_ge(s_st, c)
                nc.vector.scalar_tensor_tensor(out=ys[:, :], in0=ps[6][:, :], scalar=scales[:, 2:3], in1=x1s[p][:, :],
                                               op0=ALU.mult, op1=ALU.add).then_inc(s_r, 1)
                dve.wait_ge(s_r, c + 1)
                nc.vector.bn_stats(bn[:, :], ys[:, :]).then_inc(s_bn, 1)
                nc.vector.tensor_copy(res[:, bass.ds(c, 1), :], ys[:, :].unsqueeze(1))
                dve.wait_ge(s_bn, c + 1)
                nc.vector.tensor_copy(bn_all[:, bass.ds(c, 1), :], bn[:, :].unsqueeze(1)).then_inc(s_st, 1)

            x1(0, 0)
            x_lo(0, 0)
            with dve.Fori(0, NCH // 2 - 1) as i:
                for p in range(2):
                    chunk(i * 2 + p, p, True)
            chunk(NCH - 2, 0, True)
            chunk(NCH - 1, 1, False)
            dve.wait_ge(s_st, NCH)
            for c in range(NCH):
                nc.vector.bn_aggr(stat[:, c, :], bn_all[:, c, :]).then_inc(s_ag, 1)
            dve.wait_ge(s_sd, 2)
            nc.vector.reciprocal(rstd[:, :], std[:, :]).then_inc(s_rd, 1)
            dve.wait_ge(s_rd, 2)
            with dve.Fori(0, NCH) as c:
                nc.vector.tensor_scalar(tile(res, c), tile(res, c), stat[:, bass.ds(c, 1), 0:1].rearrange("p o d -> p (o d)"),
                                        rstd[:, bass.ds(c, 1)], ALU.subtract, ALU.mult).then_inc(s_y, 1)


def layer(nc, x, Wq, Wk, Wv, Wa, ba, Wb, bb, Wg, Wo, cqw, cqb, ckw, ckb, cvw, cvb, ln_w, ln_b, W_up, W_gate, W_down, out):
    scr = {n: nc.dram_tensor(f"scratch_{n}", (NCH, P, NH, CT), F32, kind="Internal").ap() for n in ("q", "k", "ng", "vt", "A", "g", "o")}
    scr["beta"] = nc.dram_tensor("scratch_beta", (NH, TOK), F32, kind="Internal").ap()
    scr["r"] = nc.dram_tensor("scratch_r", (2, NCH, P, NH, B, NBL), F32, kind="Internal").ap()
    projections(nc, x, [Wq, Wk, Wv, Wa, Wg], ba, Wb, bb, [cqw, ckw, cvw], [cqb, ckb, cvb], scr)
    recurrence(nc, scr)
    with ExitStack() as ctx:
        m = Mem(nc, ctx, "all")
        res = m.sb("res", [P, NCH, HID])
        stat = m.sb("stat", [P, NCH, 2])
        attention_out(nc, x, Wo, ln_w, ln_b, scr, res, stat)
        tern = [m.sb("t_up", [P, KT, E], F32R), m.sb("t_gate", [P, KT, E], F32R), m.sb("t_down", [P, E // P, HID], F32R)]
        scales = m.sb("scales", [P, 3])
        ternary(nc, [W_up, W_gate, W_down], tern, scales)
        feed_forward(nc, tern, scales, res, stat, out)


_INS = ["x", "Wq", "Wk", "Wv", "Wa", "ba", "Wb", "bb", "Wg", "Wo", "cqw", "cqb", "ckw", "ckb", "cvw", "cvb", "ln_w", "ln_b",
        "W_up", "W_gate", "W_down"]


def kernel(**inputs):
    import numpy as _np
    import concourse.bacc as _bacc
    from concourse import mybir as _mybir
    from concourse.bass_utils import run_bass_kernel_spmd as _run

    nc = _bacc.Bacc("TRN2", target_bir_lowering=False, num_devices=1)
    arrays, args = {}, []
    for name in _INS:
        full = f"L0_ffn_{name}" if name.startswith("W_") else f"L0_attn_{name}"
        a = _np.ascontiguousarray(inputs[full])
        arrays[f"in_{name}"] = a
        args.append(nc.dram_tensor(f"in_{name}", a.shape, _mybir.dt.from_np(a.dtype), kind="ExternalInput").ap())
    args.append(nc.dram_tensor("out_0", (B, S, HID), _mybir.dt.float32, kind="ExternalOutput").ap())
    layer(nc, *args)
    r = _run(nc, [arrays], core_ids=[0])
    return r.results[0]["out_0"]
```

```python
import numpy as np
import concourse.bass as bass
from concourse import mybir
from contextlib import ExitStack

F32 = mybir.dt.float32
F32R = mybir.dt.float32r
ALU = mybir.AluOpType
ACT = mybir.ActivationFunctionType
AX = mybir.AxisListType

P = 128
B, S, HID = 4, 512, 512
NH, DV, KW = 16, 128, 4
E = 2048
HB = NH * B
CH = 32
NCH = S // CH
BL = 8
NBL = CH // BL
PAIRS = BL * (BL - 1) // 2
KT = HID // P
TOK = B * S
CT = B * CH
Z_MIN = -17.25
EPS = 1e-5
assert CT == P and DV == P


def fp32(ap):
    return ap.bitcast(F32)


class Mem:

    def __init__(self, nc, ctx, phase):
        self.nc, self.ctx, self.phase = nc, ctx, phase

    def sb(self, name, shape, dt=F32):
        return self.ctx.enter_context(self.nc.sbuf_tensor(f"{self.phase}_{name}", shape, dt))

    def ps(self, name):
        return self.ctx.enter_context(self.nc.psum_tensor(f"{self.phase}_{name}", [P, 512], F32))

    def sem(self, name):
        return self.ctx.enter_context(self.nc.semaphore(f"{self.phase}_{name}"))


def make_identity(nc, pool, ident, sem):
    nc.gpsimd.memset(ident[:, :], 0.0).then_inc(sem, 1)
    pool.wait_ge(sem, 1)
    nc.gpsimd.affine_select(out=ident[:, :], in_=ident[:, :], compare_op=ALU.not_equal, fill=1.0,
                            base=0, pattern=[[-1, P]], channel_multiplier=1).then_inc(sem, 1)


def projections(nc, x, w_mats, ba, wb, bb, conv_w, conv_b, scr):
    with ExitStack() as ctx:
        m = Mem(nc, ctx, "pa")
        ident = m.sb("ident", [P, P])
        x_hi = m.sb("x_hi", [P, KT, TOK], F32R)
        x_lo = m.sb("x_lo", [P, KT, TOK], F32R)
        w_in = m.sb("w_in", [P, 5, KT, P])
        x_in = w_in[:, 3:5, :, :]
        w_hi = m.sb("w_hi", [P, 5, KT, P], F32R)
        w_lo = m.sb("w_lo", [P, 5, KT, P], F32R)
        y = [m.sb(f"y{i}", [P, B, KW - 1 + S]) for i in range(2)]
        cv = [m.sb(f"cv{i}", [P, B, S]) for i in range(3)]
        av = m.sb("av", [P, B, S])
        ra = m.sb("ra", [P, B, S])
        outs = {n: m.sb(f"o_{n}", [P, NCH, B, CH]) for n in ("q", "k", "ng", "vt", "A", "g")}
        r_out = m.sb("r_out", [P, 2, NCH, B, NBL])
        taps = m.sb("taps", [P, NH, 3, KW])
        cbias = m.sb("cbias", [P, NH, 3])
        ba_sb = m.sb("ba_sb", [P, NH])
        bb_sb = m.sb("bb_sb", [NH, 1])
        beta = cv[0][0:NH, :, :]
        ps = [m.ps(f"ps{i}") for i in range(8)]

        s_const = m.sem("const")
        s_id = m.sem("id")
        s_x = [m.sem(f"x{i}") for i in range(2)]
        s_xt = m.sem("xt")
        s_xhi = m.sem("xhi")
        s_xlo = m.sem("xlo")
        s_wb = m.sem("wb")
        s_bp = m.sem("bp")
        s_beta = m.sem("beta")
        s_bst = m.sem("bst")
        s_bb = m.sem("bb")
        s_w = [m.sem(f"w{i}") for i in range(5)]
        s_whi = m.sem("whi")
        s_wlo = m.sem("wlo")
        s_mm = m.sem("mm")
        s_y = m.sem("y")
        s_zero = m.sem("zero")
        s_tap = m.sem("tap")
        s_silu = m.sem("silu")
        s_z = m.sem("z")
        s_exp = m.sem("exp")
        s_a = m.sem("a")
        s_ra = m.sem("ra")
        s_ng = m.sem("ng")
        s_g = m.sem("g")
        s_pr = m.sem("pr")
        s_vt = m.sem("vt")
        s_st = {n: m.sem(f"st_{n}") for n in ("q", "k", "ng", "vt", "A", "g", "r")}

        x_rows = x.rearrange("b (s p) d -> (b s) p d", p=P)
        NT = TOK // P
        w_dram = [w.rearrange("(k p) (h c) -> p h k c", p=P, c=P) for w in w_mats]
        st_dram = {n: scr[n].rearrange("n c h t -> c h n t") for n in outs}
        A, G = 3, 4
        YB = (0, 1, 0)
        PER_MAT = B
        TILES = 5 * PER_MAT
        bank = [ps[j % 5] for j in range(TILES)]
        N_PR = 21
        block = ctx.enter_context(nc.Block())

        @block.sync
        def _(sp):
            with nc.allow_non_contiguous_dma(reason="small constants, channels on the partitions"):
                for n in range(3):
                    sp.dma_start(taps[:, :, n, :], conv_w[n].rearrange("(h c) o k -> c h (o k)", c=P)).then_inc(s_const, 16)
                    sp.dma_start(cbias[:, :, n], conv_b[n].rearrange("(h c) -> c h", c=P)).then_inc(s_const, 16)
                sp.dma_start(ba_sb[:, :], ba.rearrange("(h c) -> c h", c=P)).then_inc(s_const, 16)
                sp.dma_start(bb_sb[:, :], bb.rearrange("(h o) -> h o", o=1)).then_inc(s_const, 16)
            for i in range(NT):
                if i >= 2:
                    sp.wait_ge(s_xt, i - 1)
                sp.dma_start(x_in[:, i % 2, :, :], x_rows[i, :, :].rearrange("p (k d) -> p k d", k=KT)).then_inc(s_x[i % 2], 16)
            sp.wait_ge(s_zero, 1)
            sp.dma_start(w_in[:, 0, :, 0:NH], wb.rearrange("(k p) h -> p k h", p=P)).then_inc(s_wb, 16)
            sp.wait_ge(s_beta, B)
            for b in range(B):
                sp.dma_start(scr["beta"].rearrange("h (c b t) -> h b c t", b=B, t=CH)[:, b, :, :],
                             beta[:, b, :].rearrange("h (c t) -> h c t", t=CH)).then_inc(s_bst, 16)
            sp.wait_ge(s_wlo, 1)
            sp.wait_ge(s_xt, NT)
            for mat in range(5):
                sp.dma_start(w_in[:, mat, :, :], w_dram[mat][:, 0, :, :]).then_inc(s_w[mat], 16)
            sp.wait_ge(s_bst, 16 * B)

            def head(h, more):
                if more:
                    sp.wait_ge(s_wlo, 5 * h + 6)
                    for mat in range(5):
                        sp.dma_start(w_in[:, mat, :, :], w_dram[mat][:, h + 1, :, :]).then_inc(s_w[mat], 16)
                sp.wait_ge(s_st["ng"], 16 * h)
                sp.dma_start(outs["ng"][:, :, :, :].rearrange("p c b t -> p (c b t)"),
                             scr["beta"][h, :].partition_broadcast(P)).then_inc(s_bb, 16)

                def store(n):
                    sp.dma_start(st_dram[n][:, h, :, :], outs[n][:, :, :, :].rearrange("p n b t -> p n (b t)")).then_inc(s_st[n], 16)

                sp.wait_ge(s_silu, 3 * h + 2)
                store("q")
                store("k")
                sp.wait_ge(s_ng, h + 1)
                store("ng")
                sp.wait_ge(s_g, 4 * h + 8)
                store("g")
                sp.wait_ge(s_pr, N_PR * (h + 1))
                store("A")
                for i in range(2):
                    sp.dma_start(scr["r"].rearrange("i n c h b k -> i c h n (b k)")[i, :, h, :, :],
                                 r_out[:, i, :, :, :].rearrange("p n b k -> p n (b k)")).then_inc(s_st["r"], 16)
                sp.wait_ge(s_vt, h + 1)
                store("vt")

            with sp.Fori(0, NH - 1) as h:
                head(h, True)
            head(NH - 1, False)
            for n in s_st:
                sp.wait_ge(s_st[n], (32 if n == "r" else 16) * NH)

        @block.gpsimd
        def _(pool):
            make_identity(nc, pool, ident, s_id)
            nc.gpsimd.memset(w_in[:, 0, :, :], 0.0).then_inc(s_zero, 1)
            for i in range(2):
                nc.gpsimd.memset(y[i][:, :, 0:KW - 1], 0.0).then_inc(s_zero, 1)
            nc.gpsimd.memset(r_out[:, :, :, :, :], 0.0).then_inc(s_g, 4)
            at = lambda t, i: t[:, :, :].rearrange("p b (c n i) -> p i b c n", n=NBL, i=BL)[:, i]
            to = lambda t, i: t[:, :, :, :].rearrange("p c b (n i) -> p i b c n", i=BL)[:, i]
            tA, tI = outs["A"], outs["vt"]
            rv = r_out[:, :, :, :, :].rearrange("p i c b n -> p i b c n")
            mid = BL // 2
            nc.gpsimd.memset(to(tA, mid - 1), 1.0)

            def head(h):
                n = [0]

                def step(ins):
                    n[0] += 1
                    ins.then_inc(s_pr, 1)
                    return n[0]

                def mul(out, in0, in1, after=None):
                    if after:
                        pool.wait_ge(s_pr, N_PR * h + after)
                    return step(nc.gpsimd.tensor_tensor(out, in0, in1, ALU.mult))

                pool.wait_ge(s_a, h + 1)
                pool.wait_ge(s_st["vt"], 16 * h)
                k = mul(to(tI, 2), at(av, 3), at(av, 2))
                k = mul(to(tI, 1), to(tI, 2), at(av, 1), k)
                k = mul(to(tI, 0), to(tI, 1), at(av, 0), k)
                step(nc.gpsimd.memset(to(tI, mid), 1.0))
                step(nc.gpsimd.tensor_copy(to(tI, mid - 1), at(av, mid - 1)))
                pool.wait_ge(s_ra, h + 1)
                k = mul(to(tI, 6), at(ra, 4), at(ra, 5))
                k = mul(to(tI, 7), to(tI, 6), at(ra, 6), k)
                step(nc.gpsimd.tensor_copy(to(tI, 5), at(ra, 4)))
                pool.wait_ge(s_st["A"], 16 * h)
                k = mul(to(tA, 1), at(ra, 3), at(ra, 2))
                step(nc.gpsimd.tensor_copy(to(tA, 2), at(ra, 3)))
                k = mul(to(tA, 0), to(tA, 1), at(ra, 1), k)
                step(nc.gpsimd.tensor_copy(to(tA, 4), at(av, 4)))
                k = mul(to(tA, 5), at(av, 4), at(av, 5))
                k = mul(to(tA, 6), to(tA, 5), at(av, 6), k)
                k = mul(to(tA, 7), to(tA, 6), at(av, 7), k)
                pool.wait_ge(s_st["r"], 32 * h)
                mul(rv[:, 0, :, :, 1:], to(tA, 7)[:, :, :, :-1], to(tI, 0)[:, :, :, 1:], k)
                k = mul(rv[:, 0, :, 1:, 0:1], to(tA, 7)[:, :, :-1, NBL - 1:], to(tI, 0)[:, :, 1:, 0:1])
                for j in range(1, NBL):
                    before = rv[:, 1, :, :, j - 1:j] if j > 1 else rv[:, 0, :, :, 0:1]
                    k = mul(rv[:, 1, :, :, j:j + 1], before, rv[:, 0, :, :, j:j + 1], k)
                step(nc.gpsimd.tensor_copy(rv[:, 1, :, :, 0:1], rv[:, 0, :, :, 0:1]))
                assert n[0] == N_PR

            with pool.Fori(0, NH) as h:
                head(h)

        @block.scalar
        def _(act):
            for i in range(NT):
                act.wait_ge(s_xt, i + 1)
                nc.scalar.activation(x_hi[:, :, i * P:(i + 1) * P], ps[i % 4][:, :].rearrange("p (k t) -> p k t", k=KT), ACT.Copy).then_inc(s_xhi, 1)

            def split_hi(mat):
                nc.scalar.activation(w_hi[:, mat, :, :], w_in[:, mat, :, :], ACT.Copy).then_inc(s_whi, 1)

            act.wait_ge(s_wb, 16)
            split_hi(0)
            act.wait_ge(s_const, 128)
            for b in range(B):
                act.wait_ge(s_bp, b + 1)
                nc.scalar.activation(beta[:, b, :], ps[b][0:NH, :], ACT.Sigmoid, bias=bb_sb[:, 0:1]).then_inc(s_beta, 1)
            for mat in range(5):
                act.wait_ge(s_w[mat], 16)
                if mat == 0:
                    act.wait_ge(s_bp, B)
                split_hi(mat)

            def head(h, more):
                def split(mat):
                    if more:
                        act.wait_ge(s_w[mat], 16 * h + 32)
                        act.wait_ge(s_mm, TILES * h + PER_MAT * (mat + 1))
                        split_hi(mat)

                for mat in range(3):
                    if mat == 0:
                        act.wait_ge(s_tap, 12 * h)
                    if mat == 2:
                        act.wait_ge(s_tap, 12 * h + KW)
                    for b in range(B):
                        act.wait_ge(s_mm, TILES * h + PER_MAT * mat + b + 1)
                        nc.scalar.activation(y[YB[mat]][:, b, KW - 1:], bank[PER_MAT * mat + b][:, :], ACT.Copy).then_inc(s_y, 1)
                    split(mat)
                for mat, n in ((0, "q"), (1, "k"), (2, None)):
                    act.wait_ge(s_tap, 12 * h + KW * (mat + 1))
                    if n:
                        act.wait_ge(s_st[n], 16 * h)
                        out = outs[n][:, :, :, :].rearrange("p c b t -> p b c t")
                        nc.scalar.activation(out, cv[mat][:, :, :].rearrange("p b (c t) -> p b c t", t=CH), ACT.Silu).then_inc(s_silu, 1)
                    else:
                        nc.scalar.activation(cv[mat][:, :, :], cv[mat][:, :, :], ACT.Silu).then_inc(s_silu, 1)
                act.wait_ge(s_z, 4 * h + 4)
                act.wait_ge(s_pr, N_PR * h)
                act.wait_ge(s_ng, h)
                nc.scalar.activation(ra[:, :, :], av[:, :, :], ACT.Exp, scale=-1.0).then_inc(s_exp, 1)
                act.wait_ge(s_exp, h + 1)
                nc.scalar.activation(av[:, :, :], av[:, :, :], ACT.Sigmoid).then_inc(s_a, 1)
                split(A)
                act.wait_ge(s_st["g"], 16 * h)
                for b in range(B):
                    act.wait_ge(s_mm, TILES * h + PER_MAT * G + b + 1)
                    nc.scalar.activation(outs["g"][:, :, b, :], bank[PER_MAT * G + b][:, :].rearrange("p (c t) -> p c t", t=CH), ACT.Sigmoid).then_inc(s_g, 1)
                split(G)

            with act.Fori(0, NH - 1) as h:
                head(h, True)
            head(NH - 1, False)

        @block.tensor
        def _(pe):
            pe.wait_ge(s_id, 2)
            for i in range(NT):
                pe.wait_ge(s_x[i % 2], 16 * (i // 2 + 1))
                if i >= 4:
                    pe.wait_ge(s_xlo, i - 3)
                for k in range(KT):
                    last = nc.tensor.transpose(ps[i % 4][:, k * P:(k + 1) * P], x_in[:, i % 2, k, :], ident[:, :])
                last.then_inc(s_xt, 1)
            pe.wait_ge(s_xlo, NT)

            def product(out, mat, b):
                passes = [(w_hi, x_hi), (w_hi, x_lo), (w_lo, x_hi)]
                for k in range(KT):
                    for n, (w, xx) in enumerate(passes):
                        last = nc.tensor.matmul(out, w[:, mat, k, :], xx[:, k, b * S:(b + 1) * S],
                                                start=(k == 0 and n == 0), stop=(k == KT - 1 and n == 2))
                return last

            pe.wait_ge(s_wlo, 1)
            for b in range(B):
                product(ps[b][:, :], 0, b).then_inc(s_bp, 1)
            pe.wait_ge(s_beta, B)

            with pe.Fori(0, NH) as h:
                for mat in range(5):
                    pe.wait_ge(s_wlo, 5 * h + mat + 2)
                    for b in range(B):
                        j = PER_MAT * mat + b
                        before = j - 5
                        if before < 0 and j == 0:
                            pe.wait_ge(s_z, 4 * h)
                        elif before < 0:
                            pe.wait_ge(s_g, 4 * h + j)
                        elif before < 3 * PER_MAT:
                            pe.wait_ge(s_y, 12 * h + before + 1)
                        else:
                            pe.wait_ge(s_z, 4 * h + before - 3 * PER_MAT + 1)
                        product(bank[j][:, :], mat, b).then_inc(s_mm, 1)

        @block.vector
        def _(dve):
            for i in range(NT):
                dve.wait_ge(s_xhi, i + 1)
                nc.vector.tensor_tensor(x_lo[:, :, i * P:(i + 1) * P], ps[i % 4][:, :].rearrange("p (k t) -> p k t", k=KT),
                                        fp32(x_hi[:, :, i * P:(i + 1) * P]), ALU.subtract).then_inc(s_xlo, 1)

            def split_lo(mat):
                nc.vector.tensor_tensor(w_lo[:, mat, :, :], w_in[:, mat, :, :], fp32(w_hi[:, mat, :, :]), ALU.subtract).then_inc(s_wlo, 1)

            dve.wait_ge(s_whi, 1)
            split_lo(0)
            for mat in range(5):
                dve.wait_ge(s_whi, 2 + mat)
                if mat == 0:
                    dve.wait_ge(s_bp, B)
                split_lo(mat)
            dve.wait_ge(s_const, 128)
            dve.wait_ge(s_bst, 16 * B)

            def head(h, more):
                def split(mat):
                    if more:
                        dve.wait_ge(s_whi, 5 * h + mat + 7)
                        split_lo(mat)

                for mat in range(3):
                    dve.wait_ge(s_y, 12 * h + 4 * mat + 4)
                    dve.wait_ge(s_silu, 3 * h)
                    if mat == 0:
                        dve.wait_ge(s_zero, 3)
                    if mat == 2:
                        dve.wait_ge(s_vt, h)
                    yy, out = y[YB[mat]], cv[mat][:, :, :]
                    tap = lambda k: taps[:, bass.ds(h, 1), mat, k:k + 1].rearrange("p a k -> p (a k)")
                    bias = cbias[:, bass.ds(h, 1), mat:mat + 1].rearrange("p a k -> p (a k)")
                    nc.vector.tensor_scalar(out, yy[:, :, KW - 1:], tap(KW - 1), bias, ALU.mult, ALU.add).then_inc(s_tap, 1)
                    for k in range(KW - 1):
                        dve.wait_ge(s_tap, 12 * h + KW * mat + k + 1)
                        nc.vector.scalar_tensor_tensor(out=out, in0=yy[:, :, k:k + S], scalar=tap(k), in1=out,
                                                       op0=ALU.mult, op1=ALU.add).then_inc(s_tap, 1)
                    split(mat)
                dve.wait_ge(s_pr, N_PR * h)
                for b in range(B):
                    dve.wait_ge(s_mm, TILES * h + PER_MAT * A + b + 1)
                    nc.vector.tensor_scalar(av[:, b, :], bank[PER_MAT * A + b][:, :], ba_sb[:, bass.ds(h, 1)], Z_MIN,
                                            ALU.add, ALU.max).then_inc(s_z, 1)
                split(A)
                dve.wait_ge(s_exp, h + 1)
                nc.vector.tensor_scalar(ra[:, :, :], ra[:, :, :], 1.0, None, ALU.add).then_inc(s_ra, 1)
                dve.wait_ge(s_ra, h + 1)
                dve.wait_ge(s_bb, 16 * h + 16)
                tile = lambda t, b: t[:, b, :].rearrange("p (c t) -> p c t", t=CH)
                for b in range(B):
                    out = outs["ng"][:, :, b, :]
                    last = nc.vector.scalar_tensor_tensor(out=out, in0=tile(ra, b), scalar=-1.0 / DV, in1=out,
                                                          op0=ALU.mult, op1=ALU.mult)
                last.then_inc(s_ng, 1)
                split(G)
                dve.wait_ge(s_silu, 3 * h + 3)
                dve.wait_ge(s_pr, N_PR * (h + 1))
                for b in range(B):
                    out = outs["vt"][:, :, b, :]
                    last = nc.vector.scalar_tensor_tensor(out=out, in0=tile(cv[2], b), scalar=float(DV) ** 0.5, in1=out,
                                                          op0=ALU.mult, op1=ALU.mult)
                last.then_inc(s_vt, 1)

            with dve.Fori(0, NH - 1) as h:
                head(h, True)
            head(NH - 1, False)


def decay_rows(nc, scr):
    with ExitStack() as ctx:
        m = Mem(nc, ctx, "pr")
        cr = m.sb("cr", [P, NCH, HB, NBL])
        rows = m.sb("rows", [HB, NCH, P])
        ident = m.sb("ident", [P, P])
        ps = [m.ps(f"ps{i}") for i in range(NCH // 4)]
        s_id = m.sem("id")
        s_cr = m.sem("cr")
        s_t = m.sem("t")
        s_e = m.sem("e")
        s_st = m.sem("st")
        block = ctx.enter_context(nc.Block())

        @block.sync
        def _(sp):
            sp.dma_start(cr[:, :, :, :].rearrange("p c h n -> p c (h n)"),
                         scr["r"][1, :, :, :, :, :].rearrange("c p h b n -> p c (h b n)")).then_inc(s_cr, 16)
            sp.wait_ge(s_e, NCH // 4)
            sp.dma_start(scr["crow"].rearrange("c h v -> h c v"), rows[:, :, :]).then_inc(s_st, 16)
            sp.wait_ge(s_st, 16)

        @block.gpsimd
        def _(pool):
            make_identity(nc, pool, ident, s_id)

        @block.tensor
        def _(pe):
            pe.wait_ge(s_id, 2)
            pe.wait_ge(s_cr, 16)
            for j in range(NCH // 4):
                for q in range(4):
                    last = nc.tensor.transpose(ps[j][0:HB, q * P:(q + 1) * P], cr[:, 4 * j + q, :, NBL - 1], ident[:, :])
                last.then_inc(s_t, 1)

        @block.scalar
        def _(act):
            for j in range(NCH // 4):
                act.wait_ge(s_t, j + 1)
                nc.scalar.activation(rows[:, 4 * j:4 * j + 4, :], ps[j][0:HB, :].rearrange("p (c v) -> p c v", c=4), ACT.Copy).then_inc(s_e, 1)


def recurrence(nc, scr):
    GR = HB // 4
    off = [sum(BL - 1 - i for i in range(j)) for j in range(BL)]
    HALF, QUART = HB // 2, HB // 4
    with ExitStack() as ctx:
        m = Mem(nc, ctx, "pb")
        kq = [m.sb(f"kq{i}", [P, 2, HB, CH]) for i in range(2)]
        ng = m.sb("ng", [P, HB, CH])
        rr = [m.sb(f"rr{i}", [P, 2, HB, NBL]) for i in range(2)]
        vt = m.sb("vt", [P, HB, CH])
        W = m.sb("W", [P, HB, CH])
        O = [m.sb(f"O{i}", [P, HB, CH]) for i in range(2)]
        X = m.sb("X", [P, HB, CH])
        XT = m.sb("XT", [P, GR, P])
        KTr = m.sb("KT", [P, GR, P])
        Gm = m.sb("Gm", [P, GR, 2, 4, CH])
        mask = m.sb("mask", [P, 2, 4, CH])
        XD = [m.sb(f"XD{i}", [P, 4, 4, P]) for i in range(2)]
        crow = m.sb("crow", [P, HALF, P])
        UT = m.sb("UT", [P, HB, P])
        gst = m.sb("gst", [CH, 2, 512])
        gb = [m.sb(f"gb{i}", [P, HB, PAIRS]) for i in range(2)]
        tmp = m.sb("tmp", [P, HB, BL - 1])
        tk = m.sb("tk", [P, HB, BL])
        ident = m.sb("ident", [P, P])
        ps = [m.ps(f"ps{i}") for i in range(8)]
        psT, psD = ps[0:4], ps[4:8]

        s_id = m.sem("id")
        s_mask = m.sem("mask")
        s_kq = [m.sem(f"kq{i}") for i in range(2)]
        s_ngl = m.sem("ngl")
        s_rl = [m.sem(f"rl{i}") for i in range(2)]
        s_vl = m.sem("vl")
        s_crl = m.sem("crl")
        s_xz = m.sem("xz")
        s_gw = [m.sem(f"gw{i}") for i in range(2)]
        s_gc = m.sem("gc")
        s_gb = [m.sem(f"gb{i}") for i in range(2)]
        s_tp = m.sem("tp")
        s_te = m.sem("te")
        s_dp = m.sem("dp")
        s_de = m.sem("de")
        s_gm = m.sem("gm")
        s_w = m.sem("w")
        s_x = m.sem("x")
        s_mul = m.sem("mul")
        s_add = m.sem("add")
        s_tk = m.sem("tk")
        s_wn = m.sem("wn")
        s_rs = m.sem("rs")
        s_us = m.sem("us")
        s_os = [m.sem(f"os{i}") for i in range(2)]
        T_START, T_CH = 12, 32
        T_KT, T_GRAM = 0, 6
        T_XT = [4, 10, 12, 16, 20, 22, 24, 26]
        t_xt = lambda n, hf, more: T_XT[2 * n + hf] if more else 2 * (2 * n + hf)
        t_key = lambda w, hf: 28 + 2 * hf if w else 14 + 4 * hf
        D_START, D_CH = 8, 32
        d_cross = lambda n, hf, more: 14 + 13 * hf if n == NBL - 1 and more else 2 * n + hf
        D_STATE = [6, 10, 19, 23]
        d_s = lambda j: 15 + j if j < 4 else 24 + j
        block = ctx.enter_context(nc.Block())
        flat = lambda t: t.rearrange("p h t -> p (h t)")
        window = lambda w: (slice(16 * w, 16 * w + 16), slice(max(16 * w - BL, 0), 16 * w + BL))
        solved = lambda c, n: 4 * BL * (NBL * c + n + 2)

        @block.sync
        def _(sp):
            def load(dst, name, c, sem):
                sp.dma_start(flat(dst), flat(scr[name][c, :, :, :])).then_inc(sem, 16)

            def load_kq(c, p):
                load(kq[p][:, 0, :, :], "k", c, s_kq[p])
                load(kq[p][:, 1, :, :], "q", c, s_kq[p])
                for i in range(2):
                    sp.dma_start(flat(rr[p][:, i, :, :]), scr["r"][i, c, :, :, :, :].rearrange("p h b n -> p (h b n)")).then_inc(s_rl[p], 16)

            def load_crow(c, hf):
                sp.dma_start(flat(crow[:, :, :]), scr["crow"][c, HALF * hf:HALF * (hf + 1), :].rearrange("h v -> (h v)").partition_broadcast(P)).then_inc(s_crl, 16)

            def write_grams(c, first):
                for j in range(4):
                    sp.wait_ge(s_te, first + j + 1 + 4)
                    sp.dma_start(scr["gram"][c, 0:CH * HB * CH].rearrange("(j x) -> j x", j=CH)[:, 512 * j:512 * j + 512],
                                 gst[:, j % 2, :]).then_inc(s_gw[j % 2], 16)

            def compact(c):
                for k in range(2):
                    sp.wait_ge(s_gw[k], 32 * (c + 1))
                row = HB * CH
                with nc.allow_non_contiguous_dma(reason="compaction to the pairs, once per chunk"):
                    for j in range(BL - 1):
                        first = j * row + j + 1
                        src = scr["gram"][c, first:first + NBL * (BL * row + BL)].rearrange("(n s) -> n s", n=NBL)[:, 0:row]
                        sp.dma_start(scr["pairs"][c, :, :, off[j]:off[j + 1]],
                                     src.rearrange("n (h t) -> n h t", t=CH)[:, :, 0:BL - 1 - j]).then_inc(s_gc, 16)

            def load_gb(c, n):
                sp.dma_start(flat(gb[n % 2][:, :, :]), scr["pairs"][c, n, :, :].rearrange("h k -> (h k)").partition_broadcast(P)).then_inc(s_gb[n % 2], 16)

            def chunk(c, p, more, more2):
                if more:
                    write_grams(c + 1, T_START + T_CH * c + T_GRAM)
                    sp.wait_ge(s_us, 8 * c + 4)
                    load_crow(c, 1)
                sp.wait_ge(s_x, solved(c, 0))
                load_gb(c, 2)
                if more:
                    compact(c + 1)
                sp.wait_ge(s_x, solved(c, 1))
                load_gb(c, 3)
                if more:
                    sp.wait_ge(s_gc, 112 * (c + 2))
                    load(vt[:, :, :], "vt", c + 1, s_vl)
                if more2:
                    sp.wait_ge(s_us, 8 * (c + 1))
                    load_crow(c + 1, 0)
                if more:
                    sp.wait_ge(s_x, solved(c, 2))
                    load_gb(c + 1, 0)
                    sp.wait_ge(s_x, solved(c, 3))
                    load(ng[:, :, :], "ng", c + 1, s_ngl)
                    load_gb(c + 1, 1)
                sp.wait_ge(s_de, D_START + D_CH * c + d_cross(NBL - 1, 1, more) + 1 + 4)
                sp.dma_start(flat(scr["o"][c, :, :, :]), flat(O[p][:, :, :])).then_inc(s_os[p], 16)
                if more2:
                    load_kq(c + 2, p)

            load_kq(0, 0)
            write_grams(0, 0)
            load(ng[:, :, :], "ng", 0, s_ngl)
            load(vt[:, :, :], "vt", 0, s_vl)
            compact(0)
            load_kq(1, 1)
            load_crow(0, 0)
            sp.wait_ge(s_gc, 112)
            for n in range(2):
                load_gb(0, n)
            with sp.Fori(0, NCH // 2 - 1) as i:
                for p in range(2):
                    chunk(i * 2 + p, p, True, True)
            chunk(NCH - 2, 0, True, False)
            chunk(NCH - 1, 1, False, False)
            for p in range(2):
                sp.wait_ge(s_os[p], 8 * NCH)

        def over_chunks(eng, chunk):
            with eng.Fori(0, NCH // 2 - 1) as i:
                for p in range(2):
                    chunk(i * 2 + p, i, p, True)
            chunk(NCH - 2, NCH // 2 - 1, 0, True)
            chunk(NCH - 1, NCH // 2 - 1, 1, False)

        @block.gpsimd
        def _(pool):
            tt = nc.gpsimd.tensor_tensor
            make_identity(nc, pool, ident, s_id)
            for i in range(2):
                nc.gpsimd.memset(XD[i][:, :, :, :], 0.0).then_inc(s_xz, 1)
            nc.gpsimd.memset(UT[:, :, :], 0.0).then_inc(s_te, 4)
            nc.gpsimd.memset(X[:, :, :], 0.0).then_inc(s_x, 4 * BL)
            nc.gpsimd.memset(tmp[:, :, :], 0.0).then_inc(s_de, 4)
            nc.gpsimd.memset(mask[:, :, :, :], 1.0).then_inc(s_mask, 1)
            pool.wait_ge(s_mask, 1)
            nc.gpsimd.affine_select(out=mask[:, :, :, :], in_=mask[:, :, :, :], compare_op=ALU.is_ge, fill=0.0, base=0,
                                    pattern=[[0, 2], [-CH, 4], [0, CH]], channel_multiplier=1).then_inc(s_mask, 1)
            pool.wait_ge(s_mask, 2)
            nc.gpsimd.affine_select(out=mask[:, 0, :, :], in_=mask[:, 0, :, :], compare_op=ALU.is_ge, fill=0.0, base=0,
                                    pattern=[[CH, 4], [1, CH]], channel_multiplier=-1).then_inc(s_mask, 1)
            rows = mask[:, 1, :, :].rearrange("p i (n t) -> p i n t", t=BL)
            nc.gpsimd.affine_select(out=rows, in_=rows, compare_op=ALU.is_ge, fill=0.0, base=BL - 1,
                                    pattern=[[CH, 4], [BL, NBL], [0, BL]], channel_multiplier=-1).then_inc(s_mask, 1)

            def masked(made, w, hf):
                pool.wait_ge(s_te, made + 4)
                for a, steps in enumerate(window(w)):
                    gm = Gm[:, 8 * hf:8 * hf + 8, a, :, steps]
                    by = mask[:, a, :, steps].unsqueeze(1).broadcast_to([P, 8, 4, steps.stop - steps.start])
                    tt(gm, gm, by, ALU.mult).then_inc(s_gm, 1)

            def decay(e):
                uu = UT[:, 8 * e:8 * e + 8, :]
                tt(uu, uu, crow[:, 8 * (e % 4):8 * (e % 4) + 8, :], ALU.mult).then_inc(s_us, 1)

            def chunk(c, i, p, more):
                pool.wait_ge(s_rl[p], 32 * i + 32)
                if more:
                    pool.wait_ge(s_crl, 32 * c + 16)
                    pool.wait_ge(s_dp, D_START + D_CH * c - 4)
                    decay(0)
                    decay(1)
                for n in range(NBL):
                    for hf in range(2):
                        if n + 1 < NBL:
                            pool.wait_ge(s_tp, T_START + T_CH * c + t_xt(n, hf, more) + 2)
                            xx = X[:, HALF * hf:HALF * (hf + 1), 0:BL * (n + 1)]
                            by = rr[p][:, 0, HALF * hf:HALF * (hf + 1), n + 1:n + 2].broadcast_to([P, HALF, BL * (n + 1)])
                            tt(xx, xx, by, ALU.mult).then_inc(s_rs, 1)
                        if n % 2 and more:
                            masked(T_START + T_CH * c + t_key(n // 2, hf) + 2, n // 2, hf)
                        if n + 1 < NBL and more:
                            if (n, hf) == (1, 0):
                                pool.wait_ge(s_crl, 32 * c + 32)
                                pool.wait_ge(s_dp, D_START + D_CH * c)
                            decay(2 + 2 * n + hf)

            pool.wait_ge(s_mask, 4)
            for w in range(2):
                for hf in range(2):
                    masked(4 + 4 * w + 2 * hf + 2, w, hf)
            over_chunks(pool, chunk)

        @block.scalar
        def _(act):
            def copy_t(at, j, out):
                act.wait_ge(s_tp, at + j + 1)
                nc.scalar.activation(out, psT[j % 4][:, :].rearrange("p (g k) -> p g k", g=4), ACT.Copy).then_inc(s_te, 1)

            def copy_x(c, at, hf, j):
                r, tile = 2 * hf + j, t_xt(NBL - 1, hf, True) + j
                act.wait_ge(s_tp, at + tile + 1)
                src = psT[tile % 4][:, :].rearrange("p (g k) -> p g k", g=4)
                nc.scalar.activation(XT[:, 4 * r:4 * r + 4, :], src, ACT.Copy)
                if r >= 2:
                    act.wait_ge(s_dp, D_START + D_CH * c + D_STATE[r - 2] + 4)
                for i in range(4):
                    rows = slice(CH * i, CH * (i + 1))
                    last = nc.scalar.activation(XD[j][rows, :, i, :], src[rows, :, :], ACT.Copy)
                last.then_inc(s_te, 1)

            def copy_grams(at, first, c):
                for j in range(4):
                    act.wait_ge(s_gw[j % 2], 16 * (2 * c + j // 2))
                    act.wait_ge(s_tp, at + first + j + 1)
                    nc.scalar.activation(gst[:, j % 2, :], psT[(first + j) % 4][0:CH, :], ACT.Copy).then_inc(s_te, 1)

            def copy_key(at, first, w, hf):
                for j in range(2):
                    act.wait_ge(s_tp, at + first + j + 1)
                    src = psT[(first + j) % 4][:, :].rearrange("p (g a i t) -> p g a i t", g=4, a=2, i=4)
                    g = 8 * hf + 4 * j
                    for a, steps in enumerate(window(w)):
                        part = slice(16 - (steps.stop - steps.start), 16)
                        last = nc.scalar.activation(Gm[:, g:g + 4, a, :, steps], src[:, :, 1 - a, :, part], ACT.Copy)
                    last.then_inc(s_te, 1)

            def chunk(c, i, p, more):
                at = T_START + T_CH * c
                if more:
                    for j in range(4):
                        copy_t(at, T_KT + j, KTr[:, 4 * j:4 * j + 4, :])
                for n in range(NBL):
                    for hf in range(2):
                        for j in range(2):
                            g = 8 * hf + 4 * j
                            if n == NBL - 1 and more:
                                copy_x(c, at, hf, j)
                            else:
                                copy_t(at, t_xt(n, hf, more) + j, XT[:, g:g + 4, :])
                        if (n, hf) == (0, 0) and more:
                            copy_grams(at, T_GRAM, c + 1)
                        if n == 1 and more:
                            copy_key(at, t_key(0, hf), 0, hf)
                if more:
                    for hf in range(2):
                        copy_key(at, t_key(1, hf), 1, hf)

            act.wait_ge(s_xz, 2)
            copy_grams(0, 0, 0)
            for w in range(2):
                for hf in range(2):
                    copy_key(0, 4 + 4 * w + 2 * hf, w, hf)
            over_chunks(act, chunk)

        @block.tensor
        def _(pe):
            pe.wait_ge(s_id, 2)

            def bank_t(at, j):
                pe.wait_ge(s_te, at + j + 1)
                return psT[j % 4]

            def bank_d(at, j):
                pe.wait_ge(s_de, at + j + 1)
                return psD[j % 4]

            def transposes(at, j, srcs):
                bank = bank_t(at, j)
                for q, src in enumerate(srcs):
                    last = nc.tensor.transpose(bank[:, q * P:(q + 1) * P], src, ident[:, :])
                last.then_inc(s_tp, 1)

            def grams(at, first, p):
                for j in range(4):
                    bank = bank_t(at, first + j)
                    for q in range(16):
                        k = kq[p][:, 0, 16 * j + q, :]
                        last = nc.tensor.matmul(bank[0:CH, CH * q:CH * (q + 1)], k, k, start=True, stop=True)
                    last.then_inc(s_tp, 1)

            def key_products(at, first, p, w, hf):
                for j in range(2):
                    bank = bank_t(at, first + j)
                    for q in range(4):
                        g = 8 * hf + 4 * j + q
                        last = nc.tensor.matmul(bank[:, q * P:(q + 1) * P].rearrange("p (a i t) -> p a i t", a=2, i=4),
                                                flat(kq[p][:, 0, 4 * g:4 * g + 4, :]), kq[p][:, :, 4 * g:4 * g + 4, 16 * w:16 * w + 16], start=True, stop=True)
                    last.then_inc(s_tp, 1)

            def state_products(at, d, p, j):
                bank = bank_d(at, d)
                for q in range(8):
                    last = nc.tensor.matmul(bank[:, 64 * q:64 * q + 64].rearrange("p (a t) -> p a t", a=2), UT[:, 8 * j + q, :],
                                            kq[p][:, :, 8 * j + q, :], start=True, stop=True)
                last.then_inc(s_dp, 1)

            def chunk(c, i, p, more):
                at_t, at_d = T_START + T_CH * c, D_START + D_CH * c

                def x_transposes(n, hf):
                    pe.wait_ge(s_x, 4 * BL * (NBL * c + n + 1) + 2 * BL * (hf + 1))
                    if n:
                        pe.wait_ge(s_rs, 6 * c + 2 * (n - 1) + hf + 1)
                    for j in range(2):
                        g = 8 * hf + 4 * j
                        transposes(at_t, t_xt(n, hf, more) + j, [flat(X[:, 4 * g + 4 * q:4 * g + 4 * q + 4, :]) for q in range(4)])

                def cross(n, hf):
                    kinds = 2 if n + 1 < NBL else 1
                    pe.wait_ge(s_te, at_t + t_xt(n, hf, more) + 2 + 4)
                    pe.wait_ge(s_gm, 8 * c + 4 * min(n, 1) + 2 * hf + 2)
                    bank = bank_d(at_d, d_cross(n, hf, more))
                    for q in range(8):
                        g = 8 * hf + q
                        last = nc.tensor.matmul(bank[:, 64 * q:64 * q + 32 * kinds].rearrange("p (a i t) -> p a i t", i=4, t=BL),
                                                XT[:, g, :], Gm[:, g, 0:kinds, :, BL * n:BL * (n + 1)], start=True, stop=True)
                    last.then_inc(s_dp, 1)

                def state(r):
                    pe.wait_ge(s_te, at_t + t_xt(NBL - 1, r // 2, True) + r % 2 + 1 + 4)
                    for q in range(4):
                        bank = bank_d(at_d, D_STATE[r] + q)
                        nc.tensor.matmul(bank[:, :], KTr[:, 4 * r + q, :], XD[r % 2][:, q, :, :].rearrange("p i v -> p (i v)"),
                                         start=True, stop=True).then_inc(s_dp, 1)

                if more:
                    for j in range(4):
                        transposes(at_t, T_KT + j, [flat(kq[p][:, 0, 4 * g:4 * g + 4, :]) for g in range(4 * j, 4 * j + 4)])
                for n in range(NBL if not more else NBL - 1):
                    for hf in range(2):
                        x_transposes(n, hf)
                        cross(n, hf)
                        if (n, hf) == (0, 0) and more:
                            pe.wait_ge(s_kq[1 - p], 32 * (i + p) + 32)
                            grams(at_t, T_GRAM, 1 - p)
                        if n == 1 and more:
                            key_products(at_t, t_key(0, hf), 1 - p, 0, hf)
                if more:
                    x_transposes(NBL - 1, 0)
                    state(0)
                    x_transposes(NBL - 1, 1)
                    state(1)
                    cross(NBL - 1, 0)
                    pe.wait_ge(s_de, at_d + D_STATE[1] + 4 + 4)
                    for j in range(4):
                        state_products(at_d, d_s(j), 1 - p, j)
                    state(2)
                    state(3)
                    cross(NBL - 1, 1)
                    pe.wait_ge(s_de, at_d + D_STATE[3] + 4 + 4)
                    for j in range(4, 8):
                        state_products(at_d, d_s(j), 1 - p, j)
                    for hf in range(2):
                        key_products(at_t, t_key(1, hf), 1 - p, 1, hf)

            pe.wait_ge(s_kq[0], 32)
            grams(0, 0, 0)
            for w in range(2):
                for hf in range(2):
                    key_products(0, 4 + 4 * w + 2 * hf, 0, w, hf)
            pe.wait_ge(s_te, 4)
            for j in range(8):
                state_products(0, j, 0, j)
            over_chunks(pe, chunk)

        @block.vector
        def _(dve):
            tt = nc.vector.tensor_tensor
            blocks = lambda t: t.rearrange("p h (n t) -> p h n t", t=BL)
            groups = lambda t: t.rearrange("p (g i) t -> p g i t", i=4)

            def tile(at, j):
                dve.wait_ge(s_dp, at + j + 1)
                return psD[j % 4]

            def start(at, d, c, p, hf):
                for j in range(4):
                    src = tile(at, d + j)[:, :].rearrange("p (h a t) -> p h a t", h=8, a=2)
                    hs = slice(HALF * hf + 8 * j, HALF * hf + 8 * j + 8)
                    cr = rr[p][:, 1, hs, :].unsqueeze(3).broadcast_to([P, 8, NBL, BL])
                    tt(blocks(W[:, hs, :]), blocks(src[:, :, 0, :]), cr, ALU.mult)
                    tt(blocks(O[p][:, hs, :]), blocks(src[:, :, 1, :]), cr, ALU.mult).then_inc(s_de, 1)
                dve.wait_ge(s_vl, 16 * c + 16)
                dve.wait_ge(s_de, at + d + 4 + 4)
                hs = slice(HALF * hf, HALF * (hf + 1))
                tt(W[:, hs, :], W[:, hs, :], vt[:, hs, :], ALU.subtract).then_inc(s_w, 1)

            def chunk(c, i, p, more):
                at = D_START + D_CH * c

                def solve(n, hf):
                    m28 = 28 * (NBL * c + n) + 14 * hf
                    x0 = 4 * BL * (NBL * c + n + 1) + 2 * BL * hf
                    if n == 0:
                        dve.wait_ge(s_w, 2 * c + hf + 1)
                    else:
                        dve.wait_ge(s_wn, 6 * c + 2 * (n - 1) + hf + 1)
                    dve.wait_ge(s_gb[n % 2], 16 * (2 * c + n // 2 + 1))
                    quarters = [(q, slice(QUART * (2 * hf + q), QUART * (2 * hf + q + 1))) for q in range(2)]
                    for t in range(BL):
                        step = BL * n + t
                        w = BL - 1 - t
                        for q, hs in quarters:
                            if t:
                                dve.wait_ge(s_add, m28 + 2 * (t - 1) + q + 1)
                            tt(X[:, hs, step], ng[:, hs, step], W[:, hs, step], ALU.mult).then_inc(s_x, 1)
                        if not w:
                            break
                        for q, hs in quarters:
                            dve.wait_ge(s_x, x0 + 2 * t + q + 1)
                            tt(tmp[:, hs, 0:w], gb[n % 2][:, hs, off[t]:off[t] + w], X[:, hs, step:step + 1].broadcast_to([P, QUART, w]),
                               ALU.mult).then_inc(s_mul, 1)
                        for q, hs in quarters:
                            dve.wait_ge(s_mul, m28 + 2 * t + q + 1)
                            ww = W[:, hs, step + 1:BL * (n + 1)]
                            tt(ww, ww, tmp[:, hs, 0:w], ALU.add).then_inc(s_add, 1)

                def cross(n, hf):
                    src = tile(at, d_cross(n, hf, more))[:, :].rearrange("p (g a i t) -> p g a i t", g=8, a=2, i=4)
                    hs = slice(HALF * hf, HALF * (hf + 1))
                    if n + 1 < NBL:
                        rb = groups(rr[p][:, 0, hs, n + 1:n + 2]).broadcast_to([P, 8, 4, BL])
                        tt(groups(tk[:, hs, :]), src[:, :, 1, :, :], rb, ALU.mult).then_inc(s_tk, 1)
                    oo = groups(O[p][:, hs, BL * n:BL * (n + 1)])
                    tt(oo, oo, src[:, :, 0, :, :], ALU.add).then_inc(s_de, 1)
                    if n + 1 < NBL:
                        dve.wait_ge(s_tk, 6 * c + 2 * n + hf + 1)
                        ww = W[:, hs, BL * (n + 1):BL * (n + 2)]
                        tt(ww, ww, tk[:, hs, :], ALU.add).then_inc(s_wn, 1)

                def state(r):
                    dve.wait_ge(s_us, 8 * c + 2 * (r + 1))
                    for q in range(4):
                        g = 4 * r + q
                        uu = flat(UT[:, 4 * g:4 * g + 4, :])
                        tt(uu, uu, tile(at, D_STATE[r] + q)[:, :], ALU.add).then_inc(s_de, 1)

                dve.wait_ge(s_ngl, 16 * c + 16)
                for n in range(NBL):
                    for hf in range(2):
                        if (n, hf) == (0, 1):
                            start(at, -4, c, p, 1)
                        if n:
                            cross(n - 1, hf)
                        solve(n, hf)
                if not more:
                    cross(NBL - 1, 0)
                    cross(NBL - 1, 1)
                    return
                state(0)
                state(1)
                cross(NBL - 1, 0)
                dve.wait_ge(s_rl[1 - p], 32 * (i + p) + 32)
                dve.wait_ge(s_os[1 - p], 16 * (i + p))
                start(at, d_s(0), c + 1, 1 - p, 0)
                state(2)
                state(3)
                cross(NBL - 1, 1)

            dve.wait_ge(s_rl[0], 32)
            start(0, 0, 0, 0, 0)
            over_chunks(dve, chunk)


def attention_out(nc, x, wo, ln_w, ln_b, scr, res, stat):
    with ExitStack() as ctx:
        m = Mem(nc, ctx, "pc")
        wo_in = [m.sb(f"wo_in{i}", [P, HID]) for i in range(2)]
        wo_hi = m.sb("wo_hi", [P, NH, HID], F32R)
        wo_lo = m.sb("wo_lo", [P, NH, HID], F32R)
        o_in = [m.sb(f"o_in{i}", [P, NH, CT]) for i in range(2)]
        g_in = m.sb("g_in", [P, NH, CT])
        a_in = m.sb("a_in", [P, NH, CT])
        x_in = [m.sb(f"x_in{i}", [P, HID]) for i in range(2)]
        sq = m.sb("sq", [P, NH, CT])
        og_hi = m.sb("og_hi", [P, NH, CT], F32R)
        og_lo = m.sb("og_lo", [P, NH, CT], F32R)
        lnw = m.sb("lnw", [P, 1])
        lnb = m.sb("lnb", [P, 1])
        eps = m.sb("eps", [P, 1])
        mean1 = m.sb("mean1", [P, P])
        rs = m.sb("rs", [P, HID])
        bn = m.sb("bn", [P, 6])
        bn_all = m.sb("bn_all", [P, NCH, 6])
        ps = [m.ps(f"ps{i}") for i in range(8)]

        s_c = m.sem("c")
        s_wl = [m.sem(f"wl{i}") for i in range(2)]
        s_wh = m.sem("wh")
        s_wo = m.sem("wo")
        s_o = [m.sem(f"o{i}") for i in range(2)]
        s_a = m.sem("a")
        s_oa = m.sem("oa")
        s_g = m.sem("g")
        s_x = [m.sem(f"x{i}") for i in range(2)]
        s_mu = m.sem("mu")
        s_d = m.sem("d")
        s_sq = m.sem("sq")
        s_var = m.sem("var")
        s_ln = m.sem("ln")
        s_rs = m.sem("rs")
        s_n = m.sem("n")
        s_hi = m.sem("hi")
        s_lo = m.sem("lo")
        s_p = m.sem("p")
        s_r = m.sem("r")
        s_bn = m.sem("bn")
        s_st = m.sem("st")
        block = ctx.enter_context(nc.Block())
        four = lambda t, j: t[:, 4 * j:4 * j + 4, :].rearrange("p h t -> p (h t)")

        @block.sync
        def _(sp):
            sp.dma_start(lnw[:, :], ln_w.rearrange("(p o) -> p o", o=1)).then_inc(s_c, 16)
            sp.dma_start(lnb[:, :], ln_b.rearrange("(p o) -> p o", o=1)).then_inc(s_c, 16)

            def load(c, p):
                sp.dma_start(o_in[p][:, :, :].rearrange("p h t -> p (h t)"), scr["o"][c, :, :, :].rearrange("p h t -> p (h t)")).then_inc(s_o[p], 16)
                for b in range(B):
                    sp.dma_start(x_in[p][b * CH:(b + 1) * CH, :], x.rearrange("b (c t) d -> c b t d", t=CH)[c, b, :, :]).then_inc(s_x[p], 16)

            def load_a(c):
                sp.dma_start(a_in[:, :, :].rearrange("p h t -> p (h t)"), scr["A"][c, :, :, :].rearrange("p h t -> p (h t)")).then_inc(s_a, 16)

            load(0, 0)
            load_a(0)
            for h in range(NH):
                if h >= 2:
                    sp.wait_ge(s_wo, h - 1)
                sp.dma_start(wo_in[h % 2][:, :], wo[h * P:(h + 1) * P, :]).then_inc(s_wl[h % 2], 16)
            load(1, 1)

            def chunk(c, p, more, more_a=True):
                if more_a:
                    sp.wait_ge(s_oa, c + 1)
                    load_a(c + 1)
                sp.wait_ge(s_n, 3 * c)
                sp.dma_start(g_in[:, :, :].rearrange("p h t -> p (h t)"), scr["g"][c, :, :, :].rearrange("p h t -> p (h t)")).then_inc(s_g, 16)
                if more:
                    sp.wait_ge(s_lo, c + 1)
                    sp.wait_ge(s_r, c + 1)
                    load(c + 2, p)

            with sp.Fori(0, NCH // 2 - 1) as i:
                for p in range(2):
                    chunk(i * 2 + p, p, True)
            chunk(NCH - 2, 0, False)
            chunk(NCH - 1, 1, False, False)

        @block.gpsimd
        def _(pool):
            nc.gpsimd.memset(mean1[:, :], 1.0 / DV).then_inc(s_c, 1)
            nc.gpsimd.memset(eps[:, :], EPS).then_inc(s_c, 1)
            with pool.Fori(0, NCH // 2) as i:
                for p in range(2):
                    pool.wait_ge(s_o[p], 16 * i + 16)
                    pool.wait_ge(s_a, 32 * i + 16 * p + 16)
                    nc.gpsimd.tensor_tensor(o_in[p][:, :, :], o_in[p][:, :, :], a_in[:, :, :], ALU.mult).then_inc(s_oa, 1)

        @block.scalar
        def _(act):
            for h in range(NH):
                act.wait_ge(s_wl[h % 2], 16 * (h // 2 + 1))
                nc.scalar.activation(wo_hi[:, h, :], wo_in[h % 2][:, :], ACT.Copy).then_inc(s_wh, 1)
            act.wait_ge(s_c, 34)

            def stage1(c, i, p):
                act.wait_ge(s_n, 3 * c)
                for j in range(4):
                    act.wait_ge(s_d, 4 * c + j + 1)
                    nc.scalar.activation(four(sq, j), four(o_in[p], j), ACT.Square).then_inc(s_sq, 1)
                for j in range(4):
                    act.wait_ge(s_var, 4 * c + j + 1)
                    nc.scalar.activation(four(sq, j), ps[j][:, :], ACT.Ln, bias=eps[:, 0:1]).then_inc(s_ln, 1)
                act.wait_ge(s_ln, 4 * c + 4)
                nc.scalar.activation(sq[:, :, :], sq[:, :, :], ACT.Exp, scale=-0.5).then_inc(s_rs, 1)

            def stage2(c, i, p):
                act.wait_ge(s_n, 3 * c + 3)
                act.wait_ge(s_p, c)
                nc.scalar.activation(og_hi[:, :, :], o_in[p][:, :, :], ACT.Copy).then_inc(s_hi, 1)

            stage1(0, 0, 0)
            with act.Fori(0, NCH // 2 - 1) as i:
                stage2(i * 2, i, 0)
                stage1(i * 2 + 1, i, 1)
                stage2(i * 2 + 1, i, 1)
                stage1(i * 2 + 2, i + 1, 0)
            stage2(NCH - 2, NCH // 2 - 1, 0)
            stage1(NCH - 1, NCH // 2 - 1, 1)
            stage2(NCH - 1, NCH // 2 - 1, 1)

        @block.tensor
        def _(pe):
            pe.wait_ge(s_c, 34)

            def stage1(c, i, p):
                pe.wait_ge(s_oa, c + 1)
                pe.wait_ge(s_ln, 4 * c)
                for j in range(4):
                    nc.tensor.matmul(ps[j][:, :], mean1[:, :], four(o_in[p], j), start=True, stop=True).then_inc(s_mu, 1)

            def stage1b(c):
                for j in range(4):
                    pe.wait_ge(s_sq, 4 * c + j + 1)
                    nc.tensor.matmul(ps[j][:, :], mean1[:, :], four(sq, j), start=True, stop=True).then_inc(s_var, 1)

            def stage2(c, i, p):
                pe.wait_ge(s_lo, c + 1)
                pe.wait_ge(s_wo, NH)
                pe.wait_ge(s_r, c)
                passes = [(og_hi, wo_hi), (og_hi, wo_lo), (og_lo, wo_hi)]
                for h in range(NH):
                    for n, (og, w) in enumerate(passes):
                        last = nc.tensor.matmul(ps[4 + p][:, :], og[:, h, :], w[:, h, :], start=(h == 0 and n == 0), stop=(h == NH - 1 and n == 2))
                last.then_inc(s_p, 1)

            stage1(0, 0, 0)
            stage1b(0)
            with pe.Fori(0, NCH // 2 - 1) as i:
                for p in range(2):
                    stage1(i * 2 + p + 1, i + p, 1 - p)
                    stage2(i * 2 + p, i, p)
                    stage1b(i * 2 + p + 1)
            stage1(NCH - 1, NCH // 2 - 1, 1)
            stage2(NCH - 2, NCH // 2 - 1, 0)
            stage1b(NCH - 1)
            stage2(NCH - 1, NCH // 2 - 1, 1)

        @block.vector
        def _(dve):
            for h in range(NH):
                dve.wait_ge(s_wh, h + 1)
                nc.vector.tensor_tensor(wo_lo[:, h, :], wo_in[h % 2][:, :], fp32(wo_hi[:, h, :]), ALU.subtract).then_inc(s_wo, 1)
            dve.wait_ge(s_c, 34)

            def stage1(c, i, p):
                for j in range(4):
                    dve.wait_ge(s_mu, 4 * c + j + 1)
                    nc.vector.tensor_tensor(four(o_in[p], j), four(o_in[p], j), ps[j][:, :], ALU.subtract).then_inc(s_d, 1)

            def stage2(c, i, p):
                t = o_in[p][:, :, :]
                dve.wait_ge(s_rs, c + 1)
                nc.vector.tensor_tensor(t, t, sq[:, :, :], ALU.mult).then_inc(s_n, 1)
                dve.wait_ge(s_n, 3 * c + 1)
                nc.vector.tensor_scalar(t, t, lnw[:, 0:1], lnb[:, 0:1], ALU.mult, ALU.add).then_inc(s_n, 1)
                dve.wait_ge(s_n, 3 * c + 2)
                dve.wait_ge(s_g, 16 * c + 16)
                nc.vector.tensor_tensor(t, t, g_in[:, :, :], ALU.mult).then_inc(s_n, 1)
                dve.wait_ge(s_hi, c + 1)
                nc.vector.tensor_tensor(og_lo[:, :, :], t, fp32(og_hi[:, :, :]), ALU.subtract).then_inc(s_lo, 1)

            def stage3(c, i, p):
                dve.wait_ge(s_p, c + 1)
                dve.wait_ge(s_x[p], 64 * i + 64)
                dve.wait_ge(s_st, c)
                nc.vector.tensor_tensor(rs[:, :], ps[4 + p][:, :], x_in[p][:, :], ALU.add).then_inc(s_r, 1)
                dve.wait_ge(s_r, c + 1)
                nc.vector.bn_stats(bn[:, :], rs[:, :]).then_inc(s_bn, 1)
                nc.vector.tensor_copy(res[:, bass.ds(c, 1), :], rs[:, :].unsqueeze(1))
                dve.wait_ge(s_bn, c + 1)
                nc.vector.tensor_copy(bn_all[:, bass.ds(c, 1), :], bn[:, :].unsqueeze(1)).then_inc(s_st, 1)

            stage1(0, 0, 0)
            with dve.Fori(0, NCH // 2 - 1) as i:
                for p in range(2):
                    stage2(i * 2 + p, i, p)
                    stage1(i * 2 + p + 1, i + p, 1 - p)
                    stage3(i * 2 + p, i, p)
            stage2(NCH - 2, NCH // 2 - 1, 0)
            stage1(NCH - 1, NCH // 2 - 1, 1)
            stage3(NCH - 2, NCH // 2 - 1, 0)
            stage2(NCH - 1, NCH // 2 - 1, 1)
            stage3(NCH - 1, NCH // 2 - 1, 1)
            dve.wait_ge(s_st, NCH)
            for c in range(NCH):
                nc.vector.bn_aggr(stat[:, c, :], bn_all[:, c, :])


def ternary(nc, mats, tern, scales):
    NP = E * HID // P // HID
    COUNT = float(E * HID)
    with ExitStack() as ctx:
        m = Mem(nc, ctx, "pd")
        w = [m.sb(f"w{i}", [P, NP, HID]) for i in range(2)]
        junk = m.sb("junk", [P, 4, HID], mybir.dt.bfloat16)
        low = m.sb("low", [P, 4, HID])
        ident = m.sb("ident", [P, P])
        ones = m.sb("ones", [P, P])
        part = m.sb("part", [P, 3, 4])
        tot = m.sb("tot", [P, 3])
        half = m.sb("half", [P, 3, 2])
        ps = [m.ps(f"ps{i}") for i in range(8)]
        s_id = m.sem("id")
        s_c = m.sem("c")
        s_w = [m.sem(f"w{i}") for i in range(2)]
        s_abs = m.sem("abs")
        s_tot = m.sem("tot")
        s_sum = m.sem("sum")
        s_sc = m.sem("sc")
        s_low = m.sem("low")
        s_q = m.sem("q")
        s_tr = m.sem("tr")
        s_ev = m.sem("ev")
        block = ctx.enter_context(nc.Block())
        views = [mats[0].rearrange("(n p) d -> p n d", p=P), mats[1].rearrange("(n p) d -> p n d", p=P),
                 mats[2].rearrange("(n p) (m d) -> p n m d", p=P, d=HID)]

        @block.sync
        def _(sp):
            for i in range(3):
                if i == 2:
                    sp.wait_ge(s_tr, NP)
                dst = w[i % 2][:, :, :] if i < 2 else w[0][:, :, :].rearrange("p (n m) d -> p n m d", n=4)
                sp.dma_start(dst, views[i]).then_inc(s_w[i % 2], 16)

        @block.gpsimd
        def _(pool):
            make_identity(nc, pool, ident, s_id)
            nc.gpsimd.memset(ones[:, :], 1.0).then_inc(s_c, 1)

        @block.scalar
        def _(act):
            def absolute(i):
                act.wait_ge(s_w[i % 2], 16 * (i // 2 + 1))
                for j in range(4):
                    if i or j:
                        act.wait_ge(s_abs, 4 * i + j)
                    nc.scalar.activation(junk[:, :, :], w[i % 2][:, 4 * j:4 * j + 4, :], ACT.Abs,
                                         accum_out=part[:, i, j:j + 1]).then_inc(s_abs, 1)

            absolute(0)
            absolute(1)
            for i in range(3):
                if i == 2:
                    absolute(2)
                for n in range(0, NP):
                    act.wait_ge(s_tr, NP * i + n + 1)
                    nc.scalar.activation(dest(tern, i, n), ps[2 + n % 4][:, :].rearrange("p (k e) -> p k e", k=4), ACT.Copy).then_inc(s_ev, 1)

        @block.tensor
        def _(pe):
            pe.wait_ge(s_c, 1)
            pe.wait_ge(s_id, 2)
            for i in range(3):
                pe.wait_ge(s_tot, i + 1)
                nc.tensor.matmul(ps[i % 2][:, 0:1], ones[:, :], tot[:, i:i + 1], start=True, stop=True).then_inc(s_sum, 1)
                for n in range(NP):
                    j = NP * i + n
                    pe.wait_ge(s_q, 4 * i + n // 4 + 1)
                    if j >= 4:
                        pe.wait_ge(s_ev, j - 3)
                    for k in range(4):
                        last = nc.tensor.transpose(ps[2 + n % 4][:, k * P:(k + 1) * P], w[i % 2][:, n, k * P:(k + 1) * P], ident[:, :])
                    last.then_inc(s_tr, 1)

        @block.vector
        def _(dve):
            for i in range(3):
                dve.wait_ge(s_abs, 4 * i + 4)
                nc.vector.tensor_reduce(tot[:, i:i + 1], part[:, i, :], AX.X, ALU.add).then_inc(s_tot, 1)
                dve.wait_ge(s_sum, i + 1)
                nc.vector.tensor_scalar(scales[:, i:i + 1], ps[i % 2][:, 0:1], 1.0 / COUNT, 1e-8, ALU.mult, ALU.add).then_inc(s_sc, 1)
                dve.wait_ge(s_sc, 3 * i + 1)
                nc.vector.tensor_scalar(half[:, i, 0:1], scales[:, i:i + 1], 0.5, None, ALU.mult).then_inc(s_sc, 1)
                nc.vector.tensor_scalar(half[:, i, 1:2], scales[:, i:i + 1], -0.5, None, ALU.mult).then_inc(s_sc, 1)
                dve.wait_ge(s_sc, 3 * i + 3)
                for j in range(4):
                    ww = w[i % 2][:, 4 * j:4 * j + 4, :].rearrange("p n d -> p (n d)")
                    ll = low[:, :, :].rearrange("p n d -> p (n d)")
                    if i or j:
                        dve.wait_ge(s_q, 4 * i + j)
                    nc.vector.tensor_scalar(ll, ww, half[:, i, 1:2], None, ALU.is_lt).then_inc(s_low, 1)
                    dve.wait_ge(s_low, 4 * i + j + 1)
                    nc.vector.scalar_tensor_tensor(out=ww, in0=ww, scalar=half[:, i, 0:1], in1=ll, op0=ALU.is_gt, op1=ALU.subtract).then_inc(s_q, 1)


def dest(tern, i, n):
    if i < 2:
        return tern[i][:, :, n * P:(n + 1) * P]
    a, b = n // 4, n % 4
    return tern[2][:, 4 * b:4 * b + 4, a * P:(a + 1) * P]


def feed_forward(nc, tern, scales, res, stat, out):
    EB = E // 512
    with ExitStack() as ctx:
        m = Mem(nc, ctx, "pe")
        ident = m.sb("ident", [P, P])
        eps = m.sb("eps", [P, 1])
        rstd = m.sb("rstd", [P, NCH])
        std = m.sb("std", [P, NCH])
        x1s = [m.sb(f"x1s{i}", [P, HID]) for i in range(2)]
        xT_hi = [m.sb(f"xT_hi{i}", [P, KT, P], F32R) for i in range(2)]
        xT_lo = [m.sb(f"xT_lo{i}", [P, KT, P], F32R) for i in range(2)]
        sil = [m.sb(f"sil{i}", [P, 512]) for i in range(2)]
        hid = [m.sb(f"hid{i}", [P, 512]) for i in range(2)]
        hT_hi = [m.sb(f"hT_hi{i}", [P, 4, P], F32R) for i in range(2)]
        hT_lo = [m.sb(f"hT_lo{i}", [P, 4, P], F32R) for i in range(2)]
        ys = m.sb("ys", [P, HID])
        bn = m.sb("bn", [P, 6])
        bn_all = m.sb("bn_all", [P, NCH, 6])
        ps = [m.ps(f"ps{i}") for i in range(8)]
        s_ag = m.sem("ag")
        s_id = m.sem("id")
        s_c = m.sem("c")
        s_sd = m.sem("sd")
        s_rd = m.sem("rd")
        s_x1 = m.sem("x1")
        s_xt = m.sem("xt")
        s_xh = m.sem("xh")
        s_xl = m.sem("xl")
        s_ug = m.sem("ug")
        s_si = m.sem("si")
        s_h = m.sem("h")
        s_ht = m.sem("ht")
        s_hh = m.sem("hh")
        s_hl = m.sem("hl")
        s_dn = m.sem("dn")
        s_r = m.sem("r")
        s_bn = m.sem("bn")
        s_st = m.sem("st")
        s_y = m.sem("y")
        s_out = m.sem("out")
        block = ctx.enter_context(nc.Block())
        tile = lambda t, c: t[:, bass.ds(c, 1), :].rearrange("p o d -> p (o d)")
        out_v = out.rearrange("b (c t) d -> c b t d", t=CH)

        @block.sync
        def _(sp):
            with sp.Fori(0, NCH) as c:
                sp.wait_ge(s_y, c + 1)
                for b in range(B):
                    sp.dma_start(out_v[c, b, :, :], tile(res, c)[b * CH:(b + 1) * CH, :]).then_inc(s_out, 16)
            sp.wait_ge(s_out, 16 * B * NCH)

        @block.gpsimd
        def _(pool):
            make_identity(nc, pool, ident, s_id)
            nc.gpsimd.memset(eps[:, :], EPS).then_inc(s_c, 1)

        def split_hi(act, out, bank):
            return nc.scalar.activation(out[:, :, :], bank[:, :].rearrange("p (k t) -> p k t", k=4), ACT.Copy)

        @block.scalar
        def _(act):
            act.wait_ge(s_c, 1)
            nc.scalar.activation(std[:, :], stat[:, :, 1], ACT.Sqrt, bias=eps[:, 0:1]).then_inc(s_sd, 1)

            def x_hi(c, p):
                act.wait_ge(s_xt, c + 1)
                split_hi(act, xT_hi[p], ps[7]).then_inc(s_xh, 1)

            def silu(c, e):
                act.wait_ge(s_ug, EB * c + e + 1)
                nc.scalar.activation(sil[e % 2][:, :], ps[2 * (e % 2)][:, :], ACT.Silu, scale=scales[:, 0:1]).then_inc(s_si, 1)

            def h_hi(c, e):
                act.wait_ge(s_ht, EB * c + e + 1)
                split_hi(act, hT_hi[e % 2], ps[4 + e % 2]).then_inc(s_hh, 1)

            def chunk(c, p, more):
                silu(c, 0)
                silu(c, 1)
                h_hi(c, 0)
                silu(c, 2)
                h_hi(c, 1)
                silu(c, 3)
                if more:
                    x_hi(c + 1, 1 - p)
                h_hi(c, 2)
                h_hi(c, 3)

            x_hi(0, 0)
            with act.Fori(0, NCH // 2 - 1) as i:
                for p in range(2):
                    chunk(i * 2 + p, p, True)
            chunk(NCH - 2, 0, True)
            chunk(NCH - 1, 1, False)
            act.wait_ge(s_ag, NCH)
            nc.scalar.activation(std[:, :], stat[:, :, 1], ACT.Sqrt, bias=eps[:, 0:1]).then_inc(s_sd, 1)

        @block.tensor
        def _(pe):
            pe.wait_ge(s_id, 2)

            def x_tp(c, p):
                pe.wait_ge(s_x1, c + 1)
                pe.wait_ge(s_xl, c)
                for k in range(KT):
                    last = nc.tensor.transpose(ps[7][:, k * P:(k + 1) * P], x1s[p][:, k * P:(k + 1) * P], ident[:, :])
                last.then_inc(s_xt, 1)

            def up_gate(c, p, e):
                pe.wait_ge(s_xl, c + 1)
                pe.wait_ge(s_h, EB * c + e + (2 - 1))
                for n in range(2):
                    for k in range(KT):
                        for q, xx in enumerate((xT_hi[p], xT_lo[p])):
                            last = nc.tensor.matmul(ps[2 * (e % 2) + n][:, :], xx[:, k, :], tern[n][:, k, e * 512:(e + 1) * 512],
                                                    start=(k == 0 and q == 0), stop=(k == KT - 1 and q == 1))
                last.then_inc(s_ug, 1)

            def h_t(c, e):
                pe.wait_ge(s_h, EB * c + e + 1 + 2)
                pe.wait_ge(s_hl, EB * c + e + 1)
                for k in range(4):
                    last = nc.tensor.transpose(ps[4 + e % 2][:, k * P:(k + 1) * P], hid[e % 2][:, k * P:(k + 1) * P], ident[:, :])
                last.then_inc(s_ht, 1)

            def down(c, e):
                pe.wait_ge(s_hl, EB * c + e + 1 + 2)
                if e == 0:
                    pe.wait_ge(s_r, c)
                for k in range(4):
                    for q, hh in enumerate((hT_hi[e % 2], hT_lo[e % 2])):
                        last = nc.tensor.matmul(ps[6][:, :], hh[:, k, :], tern[2][:, 4 * e + k, :],
                                                start=(e == 0 and k == 0 and q == 0), stop=(e == EB - 1 and k == 3 and q == 1))
                last.then_inc(s_dn, 1)

            def chunk(c, p, more):
                up_gate(c, p, 0)
                up_gate(c, p, 1)
                h_t(c, 0)
                up_gate(c, p, 2)
                h_t(c, 1)
                down(c, 0)
                up_gate(c, p, 3)
                h_t(c, 2)
                down(c, 1)
                if more:
                    x_tp(c + 1, 1 - p)
                h_t(c, 3)
                down(c, 2)
                down(c, 3)

            x_tp(0, 0)
            with pe.Fori(0, NCH // 2 - 1) as i:
                for p in range(2):
                    chunk(i * 2 + p, p, True)
            chunk(NCH - 2, 0, True)
            chunk(NCH - 1, 1, False)

        @block.vector
        def _(dve):
            nc.vector.memset(bn[:, :], 0.0).then_inc(s_h, 2)
            nc.vector.memset(rstd[:, :], 0.0).then_inc(s_hl, 2)
            dve.wait_ge(s_sd, 1)
            dve.wait_ge(s_hl, 2)
            nc.vector.reciprocal(rstd[:, :], std[:, :]).then_inc(s_rd, 1)
            dve.wait_ge(s_rd, 1)

            def x1(c, p):
                nc.vector.tensor_scalar(x1s[p][:, :], tile(res, c), stat[:, bass.ds(c, 1), 0:1].rearrange("p o d -> p (o d)"),
                                        rstd[:, bass.ds(c, 1)], ALU.subtract, ALU.mult).then_inc(s_x1, 1)

            def x_lo(c, p):
                dve.wait_ge(s_xh, c + 1)
                nc.vector.tensor_tensor(xT_lo[p][:, :, :], ps[7][:, :].rearrange("p (k t) -> p k t", k=4), fp32(xT_hi[p][:, :, :]), ALU.subtract).then_inc(s_xl, 1)

            def hidden(c, e):
                dve.wait_ge(s_si, EB * c + e + 1)
                nc.vector.scalar_tensor_tensor(out=hid[e % 2][:, :], in0=ps[2 * (e % 2) + 1][:, :], scalar=scales[:, 1:2], in1=sil[e % 2][:, :],
                                               op0=ALU.mult, op1=ALU.mult).then_inc(s_h, 1)

            def h_lo(c, e):
                dve.wait_ge(s_hh, EB * c + e + 1)
                nc.vector.tensor_tensor(hT_lo[e % 2][:, :, :], ps[4 + e % 2][:, :].rearrange("p (k t) -> p k t", k=4), fp32(hT_hi[e % 2][:, :, :]), ALU.subtract).then_inc(s_hl, 1)

            def chunk(c, p, more):
                if more:
                    dve.wait_ge(s_r, c)
                    x1(c + 1, 1 - p)
                hidden(c, 0)
                hidden(c, 1)
                h_lo(c, 0)
                hidden(c, 2)
                h_lo(c, 1)
                hidden(c, 3)
                if more:
                    x_lo(c + 1, 1 - p)
                h_lo(c, 2)
                h_lo(c, 3)
                dve.wait_ge(s_dn, EB * (c + 1))
                dve.wait_ge(s_x1, c + 1)
                dve.wait_ge(s_st, c)
                nc.vector.scalar_tensor_tensor(out=ys[:, :], in0=ps[6][:, :], scalar=scales[:, 2:3], in1=x1s[p][:, :],
                                               op0=ALU.mult, op1=ALU.add).then_inc(s_r, 1)
                dve.wait_ge(s_r, c + 1)
                nc.vector.bn_stats(bn[:, :], ys[:, :]).then_inc(s_bn, 1)
                nc.vector.tensor_copy(res[:, bass.ds(c, 1), :], ys[:, :].unsqueeze(1))
                dve.wait_ge(s_bn, c + 1)
                nc.vector.tensor_copy(bn_all[:, bass.ds(c, 1), :], bn[:, :].unsqueeze(1)).then_inc(s_st, 1)

            x1(0, 0)
            x_lo(0, 0)
            with dve.Fori(0, NCH // 2 - 1) as i:
                for p in range(2):
                    chunk(i * 2 + p, p, True)
            chunk(NCH - 2, 0, True)
            chunk(NCH - 1, 1, False)
            dve.wait_ge(s_st, NCH)
            for c in range(NCH):
                nc.vector.bn_aggr(stat[:, c, :], bn_all[:, c, :]).then_inc(s_ag, 1)
            dve.wait_ge(s_sd, 2)
            nc.vector.reciprocal(rstd[:, :], std[:, :]).then_inc(s_rd, 1)
            dve.wait_ge(s_rd, 2)
            with dve.Fori(0, NCH) as c:
                nc.vector.tensor_scalar(tile(res, c), tile(res, c), stat[:, bass.ds(c, 1), 0:1].rearrange("p o d -> p (o d)"),
                                        rstd[:, bass.ds(c, 1)], ALU.subtract, ALU.mult).then_inc(s_y, 1)


def layer(nc, x, Wq, Wk, Wv, Wa, ba, Wb, bb, Wg, Wo, cqw, cqb, ckw, ckb, cvw, cvb, ln_w, ln_b, W_up, W_gate, W_down, out):
    scr = {n: nc.dram_tensor(f"scratch_{n}", (NCH, P, NH, CT), F32, kind="Internal").ap() for n in ("q", "k", "ng", "vt", "A", "g", "o")}
    scr["beta"] = nc.dram_tensor("scratch_beta", (NH, TOK), F32, kind="Internal").ap()
    scr["r"] = nc.dram_tensor("scratch_r", (2, NCH, P, NH, B, NBL), F32, kind="Internal").ap()
    scr["crow"] = nc.dram_tensor("scratch_crow", (NCH, HB, P), F32, kind="Internal").ap()
    scr["gram"] = nc.dram_tensor("scratch_gram", (NCH, (BL - 1) * HB * CH + NBL * (BL * HB * CH + BL)), F32, kind="Internal").ap()
    scr["pairs"] = nc.dram_tensor("scratch_pairs", (NCH, NBL, HB, PAIRS), F32, kind="Internal").ap()
    projections(nc, x, [Wq, Wk, Wv, Wa, Wg], ba, Wb, bb, [cqw, ckw, cvw], [cqb, ckb, cvb], scr)
    decay_rows(nc, scr)
    recurrence(nc, scr)
    with ExitStack() as ctx:
        m = Mem(nc, ctx, "all")
        res = m.sb("res", [P, NCH, HID])
        stat = m.sb("stat", [P, NCH, 2])
        attention_out(nc, x, Wo, ln_w, ln_b, scr, res, stat)
        tern = [m.sb("t_up", [P, KT, E], F32R), m.sb("t_gate", [P, KT, E], F32R), m.sb("t_down", [P, E // P, HID], F32R)]
        scales = m.sb("scales", [P, 3])
        ternary(nc, [W_up, W_gate, W_down], tern, scales)
        feed_forward(nc, tern, scales, res, stat, out)


_INS = ["x", "Wq", "Wk", "Wv", "Wa", "ba", "Wb", "bb", "Wg", "Wo", "cqw", "cqb", "ckw", "ckb", "cvw", "cvb", "ln_w", "ln_b",
        "W_up", "W_gate", "W_down"]


def kernel(**inputs):
    import numpy as _np
    import concourse.bacc as _bacc
    from concourse import mybir as _mybir
    from concourse.bass_utils import run_bass_kernel_spmd as _run

    nc = _bacc.Bacc("TRN2", target_bir_lowering=False, num_devices=1)
    arrays, args = {}, []
    for name in _INS:
        full = f"L0_ffn_{name}" if name.startswith("W_") else f"L0_attn_{name}"
        a = _np.ascontiguousarray(inputs[full])
        arrays[f"in_{name}"] = a
        args.append(nc.dram_tensor(f"in_{name}", a.shape, _mybir.dt.from_np(a.dtype), kind="ExternalInput").ap())
    args.append(nc.dram_tensor("out_0", (B, S, HID), _mybir.dt.float32, kind="ExternalOutput").ap())
    layer(nc, *args)
    r = _run(nc, [arrays], core_ids=[0])
    return r.results[0]["out_0"]
```

```python
import numpy as np
import concourse.bass as bass
from concourse import mybir
from contextlib import ExitStack

F32 = mybir.dt.float32
F32R = mybir.dt.float32r
ALU = mybir.AluOpType
ACT = mybir.ActivationFunctionType
AX = mybir.AxisListType

P = 128
B, S, HID = 4, 512, 512
NH, DV, KW = 16, 128, 4
E = 2048
HB = NH * B
CH = 32
NCH = S // CH
BL = 8
NBL = CH // BL
PAIRS = BL * (BL - 1) // 2
KT = HID // P
TOK = B * S
CT = B * CH
Z_MIN = -17.25
EPS = 1e-5
assert CT == P and DV == P


def fp32(ap):
    return ap.bitcast(F32)


class Mem:

    def __init__(self, nc, ctx, phase):
        self.nc, self.ctx, self.phase = nc, ctx, phase

    def sb(self, name, shape, dt=F32):
        return self.ctx.enter_context(self.nc.sbuf_tensor(f"{self.phase}_{name}", shape, dt))

    def ps(self, name):
        return self.ctx.enter_context(self.nc.psum_tensor(f"{self.phase}_{name}", [P, 512], F32))

    def sem(self, name):
        return self.ctx.enter_context(self.nc.semaphore(f"{self.phase}_{name}"))


def make_identity(nc, pool, ident, sem):
    nc.gpsimd.memset(ident[:, :], 0.0).then_inc(sem, 1)
    pool.wait_ge(sem, 1)
    nc.gpsimd.affine_select(out=ident[:, :], in_=ident[:, :], compare_op=ALU.not_equal, fill=1.0,
                            base=0, pattern=[[-1, P]], channel_multiplier=1).then_inc(sem, 1)


def projections(nc, x, w_mats, ba, wb, bb, conv_w, conv_b, scr):
    with ExitStack() as ctx:
        m = Mem(nc, ctx, "pa")
        ident = m.sb("ident", [P, P])
        x_hi = m.sb("x_hi", [P, KT, TOK], F32R)
        x_lo = m.sb("x_lo", [P, KT, TOK], F32R)
        w_in = m.sb("w_in", [P, 5, KT, P])
        x_in = w_in[:, 1:5, :, :]
        w_hi = m.sb("w_hi", [P, 5, KT, P], F32R)
        w_lo = m.sb("w_lo", [P, 5, KT, P], F32R)
        y = [m.sb(f"y{i}", [P, B, KW - 1 + S]) for i in range(2)]
        cv = [m.sb(f"cv{i}", [P, B, S]) for i in range(3)]
        av = m.sb("av", [P, B, S])
        ra = m.sb("ra", [P, B, S])
        outs = {n: m.sb(f"o_{n}", [P, NCH, B, CH]) for n in ("q", "k", "ng", "vt", "A", "g")}
        r_out = m.sb("r_out", [P, 2, NCH, B, NBL])
        taps = m.sb("taps", [P, NH, 3, KW])
        cbias = m.sb("cbias", [P, NH, 3])
        ba_sb = m.sb("ba_sb", [P, NH])
        bb_sb = m.sb("bb_sb", [NH, 1])
        beta = cv[0][0:NH, :, :]
        ps = [m.ps(f"ps{i}") for i in range(8)]

        s_const = m.sem("const")
        s_id = m.sem("id")
        s_x = [m.sem(f"x{i}") for i in range(4)]
        s_xt = m.sem("xt")
        s_xhi = m.sem("xhi")
        s_xlo = m.sem("xlo")
        s_wb = m.sem("wb")
        s_bp = m.sem("bp")
        s_beta = m.sem("beta")
        s_bst = m.sem("bst")
        s_bb = m.sem("bb")
        s_w = [m.sem(f"w{i}") for i in range(5)]
        s_whi = m.sem("whi")
        s_wlo = m.sem("wlo")
        s_mm = m.sem("mm")
        s_y = m.sem("y")
        s_zero = m.sem("zero")
        s_tap = m.sem("tap")
        s_silu = m.sem("silu")
        s_z = m.sem("z")
        s_exp = m.sem("exp")
        s_a = m.sem("a")
        s_ra = m.sem("ra")
        s_ng = m.sem("ng")
        s_g = m.sem("g")
        s_pr = m.sem("pr")
        s_vt = m.sem("vt")
        s_st = {n: m.sem(f"st_{n}") for n in ("q", "k", "ng", "vt", "A", "g", "r")}

        x_rows = x.rearrange("b (s p) d -> (b s) p d", p=P)
        NT = TOK // P
        w_dram = [w.rearrange("(k p) (h c) -> p h k c", p=P, c=P) for w in w_mats]
        st_dram = {n: scr[n].rearrange("n c h t -> c h n t") for n in outs}
        A, G = 3, 4
        YB = (0, 1, 0)
        PER_MAT = B
        TILES = 5 * PER_MAT
        bank = [ps[j % 5] for j in range(TILES)]
        N_PR = 21
        block = ctx.enter_context(nc.Block())

        @block.sync
        def _(sp):
            for i in range(NT):
                if i >= 4:
                    sp.wait_ge(s_xt, i - 3)
                sp.dma_start(x_in[:, i % 4, :, :], x_rows[i, :, :].rearrange("p (k d) -> p k d", k=KT)).then_inc(s_x[i % 4], 16)
            sp.wait_ge(s_zero, 1)
            sp.dma_start(w_in[:, 0, :, 0:NH], wb.rearrange("(k p) h -> p k h", p=P)).then_inc(s_wb, 16)
            with nc.allow_non_contiguous_dma(reason="small constants, channels on the partitions"):
                for n in range(3):
                    sp.dma_start(taps[:, :, n, :], conv_w[n].rearrange("(h c) o k -> c h (o k)", c=P)).then_inc(s_const, 16)
                    sp.dma_start(cbias[:, :, n], conv_b[n].rearrange("(h c) -> c h", c=P)).then_inc(s_const, 16)
                sp.dma_start(ba_sb[:, :], ba.rearrange("(h c) -> c h", c=P)).then_inc(s_const, 16)
                sp.dma_start(bb_sb[:, :], bb.rearrange("(h o) -> h o", o=1)).then_inc(s_const, 16)
            sp.wait_ge(s_wlo, 1)
            sp.wait_ge(s_xt, NT)
            for mat in range(5):
                sp.dma_start(w_in[:, mat, :, :], w_dram[mat][:, 0, :, :]).then_inc(s_w[mat], 16)
            sp.wait_ge(s_beta, B)
            for b in range(B):
                sp.dma_start(scr["beta"].rearrange("h (c b t) -> h b c t", b=B, t=CH)[:, b, :, :],
                             beta[:, b, :].rearrange("h (c t) -> h c t", t=CH)).then_inc(s_bst, 16)
            sp.wait_ge(s_bst, 16 * B)

            def weights(h):
                sp.wait_ge(s_wlo, 5 * h + 1)
                for mat in range(5):
                    sp.dma_start(w_in[:, mat, :, :], w_dram[mat][:, h, :, :]).then_inc(s_w[mat], 16)

            def head(h, first, left):
                if not first:
                    sp.wait_ge(s_st["ng"], 16 * h)
                sp.dma_start(outs["ng"][:, :, :, :].rearrange("p c b t -> p (c b t)"),
                             scr["beta"][h, :].partition_broadcast(P)).then_inc(s_bb, 16)

                def store(n, h=h):
                    sp.dma_start(st_dram[n][:, h, :, :], outs[n][:, :, :, :].rearrange("p n b t -> p n (b t)")).then_inc(s_st[n], 16)

                if not first:
                    sp.wait_ge(s_vt, h)
                    store("vt", h - 1)
                sp.wait_ge(s_silu, 3 * h + 2)
                store("q")
                store("k")
                sp.wait_ge(s_ng, h + 1)
                store("ng")
                sp.wait_ge(s_g, 4 * h + 8)
                store("g")
                if left >= 2:
                    weights(h + 2)
                sp.wait_ge(s_pr, N_PR * (h + 1))
                store("A")
                for i in range(2):
                    sp.dma_start(scr["r"].rearrange("i n c h b k -> i c h n (b k)")[i, :, h, :, :],
                                 r_out[:, i, :, :, :].rearrange("p n b k -> p n (b k)")).then_inc(s_st["r"], 16)
                if left == 0:
                    sp.wait_ge(s_vt, h + 1)
                    store("vt")

            weights(1)
            head(0, True, NH - 1)
            with sp.Fori(1, NH - 2) as h:
                head(h, False, 2)
            head(NH - 2, False, 1)
            head(NH - 1, False, 0)
            for n in s_st:
                sp.wait_ge(s_st[n], (32 if n == "r" else 16) * NH)

        @block.gpsimd
        def _(pool):
            make_identity(nc, pool, ident, s_id)
            nc.gpsimd.memset(w_in[:, 0, :, :], 0.0).then_inc(s_zero, 1)
            for i in range(2):
                nc.gpsimd.memset(y[i][:, :, 0:KW - 1], 0.0).then_inc(s_zero, 1)
            nc.gpsimd.memset(r_out[:, :, :, :, :], 0.0).then_inc(s_g, 4)
            at = lambda t, i: t[:, :, :].rearrange("p b (c n i) -> p i b c n", n=NBL, i=BL)[:, i]
            to = lambda t, i: t[:, :, :, :].rearrange("p c b (n i) -> p i b c n", i=BL)[:, i]
            tA, tI = outs["A"], outs["vt"]
            rv = r_out[:, :, :, :, :].rearrange("p i c b n -> p i b c n")
            mid = BL // 2
            nc.gpsimd.memset(to(tA, mid - 1), 1.0)

            def head(h, first):
                n = [0]

                def step(ins):
                    n[0] += 1
                    ins.then_inc(s_pr, 1)
                    return n[0]

                def mul(out, in0, in1, after=None):
                    if after:
                        pool.wait_ge(s_pr, N_PR * h + after)
                    return step(nc.gpsimd.tensor_tensor(out, in0, in1, ALU.mult))

                pool.wait_ge(s_a, h + 1)
                if not first:
                    pool.wait_ge(s_st["vt"], 16 * h)
                k = mul(to(tI, 2), at(av, 3), at(av, 2))
                k = mul(to(tI, 1), to(tI, 2), at(av, 1), k)
                k = mul(to(tI, 0), to(tI, 1), at(av, 0), k)
                step(nc.gpsimd.memset(to(tI, mid), 1.0))
                step(nc.gpsimd.tensor_copy(to(tI, mid - 1), at(av, mid - 1)))
                pool.wait_ge(s_ra, h + 1)
                k = mul(to(tI, 6), at(ra, 4), at(ra, 5))
                k = mul(to(tI, 7), to(tI, 6), at(ra, 6), k)
                step(nc.gpsimd.tensor_copy(to(tI, 5), at(ra, 4)))
                if not first:
                    pool.wait_ge(s_st["A"], 16 * h)
                k = mul(to(tA, 1), at(ra, 3), at(ra, 2))
                step(nc.gpsimd.tensor_copy(to(tA, 2), at(ra, 3)))
                k = mul(to(tA, 0), to(tA, 1), at(ra, 1), k)
                step(nc.gpsimd.tensor_copy(to(tA, 4), at(av, 4)))
                k = mul(to(tA, 5), at(av, 4), at(av, 5))
                k = mul(to(tA, 6), to(tA, 5), at(av, 6), k)
                k = mul(to(tA, 7), to(tA, 6), at(av, 7), k)
                if not first:
                    pool.wait_ge(s_st["r"], 32 * h)
                mul(rv[:, 0, :, :, 1:], to(tA, 7)[:, :, :, :-1], to(tI, 0)[:, :, :, 1:], k)
                k = mul(rv[:, 0, :, 1:, 0:1], to(tA, 7)[:, :, :-1, NBL - 1:], to(tI, 0)[:, :, 1:, 0:1])
                for j in range(1, NBL):
                    before = rv[:, 1, :, :, j - 1:j] if j > 1 else rv[:, 0, :, :, 0:1]
                    k = mul(rv[:, 1, :, :, j:j + 1], before, rv[:, 0, :, :, j:j + 1], k)
                step(nc.gpsimd.tensor_copy(rv[:, 1, :, :, 0:1], rv[:, 0, :, :, 0:1]))
                assert n[0] == N_PR

            head(0, True)
            with pool.Fori(1, NH) as h:
                head(h, False)

        @block.scalar
        def _(act):
            for i in range(NT):
                act.wait_ge(s_xt, i + 1)
                nc.scalar.activation(x_hi[:, :, i * P:(i + 1) * P], ps[i % 4][:, :].rearrange("p (k t) -> p k t", k=KT), ACT.Copy).then_inc(s_xhi, 1)

            def split_hi(mat):
                nc.scalar.activation(w_hi[:, mat, :, :], w_in[:, mat, :, :], ACT.Copy).then_inc(s_whi, 1)

            act.wait_ge(s_wb, 16)
            split_hi(0)
            act.wait_ge(s_const, 128)
            for b in range(B):
                act.wait_ge(s_bp, b + 1)
                nc.scalar.activation(beta[:, b, :], ps[b][0:NH, :], ACT.Sigmoid, bias=bb_sb[:, 0:1]).then_inc(s_beta, 1)
            for mat in range(5):
                act.wait_ge(s_w[mat], 16)
                if mat == 0:
                    act.wait_ge(s_bp, B)
                split_hi(mat)

            def head(h, first, more):
                def split(mat):
                    if more:
                        act.wait_ge(s_w[mat], 16 * h + 32)
                        act.wait_ge(s_mm, TILES * h + PER_MAT * (mat + 1))
                        split_hi(mat)

                for mat in range(3):
                    if mat == 0 and not first:
                        act.wait_ge(s_tap, 12 * h)
                    if mat == 2:
                        act.wait_ge(s_tap, 12 * h + KW)
                    for b in range(B):
                        act.wait_ge(s_mm, TILES * h + PER_MAT * mat + b + 1)
                        nc.scalar.activation(y[YB[mat]][:, b, KW - 1:], bank[PER_MAT * mat + b][:, :], ACT.Copy).then_inc(s_y, 1)
                    split(mat)
                for mat, n in ((0, "q"), (1, "k"), (2, None)):
                    act.wait_ge(s_tap, 12 * h + KW * (mat + 1))
                    if n:
                        if not first:
                            act.wait_ge(s_st[n], 16 * h)
                        out = outs[n][:, :, :, :].rearrange("p c b t -> p b c t")
                        nc.scalar.activation(out, cv[mat][:, :, :].rearrange("p b (c t) -> p b c t", t=CH), ACT.Silu).then_inc(s_silu, 1)
                    else:
                        nc.scalar.activation(cv[mat][:, :, :], cv[mat][:, :, :], ACT.Silu).then_inc(s_silu, 1)
                act.wait_ge(s_z, 4 * h + 4)
                if not first:
                    act.wait_ge(s_pr, N_PR * h)
                    act.wait_ge(s_ng, h)
                nc.scalar.activation(ra[:, :, :], av[:, :, :], ACT.Exp, scale=-1.0).then_inc(s_exp, 1)
                act.wait_ge(s_exp, h + 1)
                nc.scalar.activation(av[:, :, :], av[:, :, :], ACT.Sigmoid).then_inc(s_a, 1)
                split(A)
                if not first:
                    act.wait_ge(s_st["g"], 16 * h)
                for b in range(B):
                    act.wait_ge(s_mm, TILES * h + PER_MAT * G + b + 1)
                    nc.scalar.activation(outs["g"][:, :, b, :], bank[PER_MAT * G + b][:, :].rearrange("p (c t) -> p c t", t=CH), ACT.Sigmoid).then_inc(s_g, 1)
                split(G)

            head(0, True, True)
            with act.Fori(1, NH - 1) as h:
                head(h, False, True)
            head(NH - 1, False, False)

        @block.tensor
        def _(pe):
            pe.wait_ge(s_id, 2)
            for i in range(NT):
                pe.wait_ge(s_x[i % 4], 16 * (i // 4 + 1))
                if i >= 4:
                    pe.wait_ge(s_xlo, i - 3)
                for k in range(KT):
                    last = nc.tensor.transpose(ps[i % 4][:, k * P:(k + 1) * P], x_in[:, i % 4, k, :], ident[:, :])
                last.then_inc(s_xt, 1)
            pe.wait_ge(s_xlo, NT)

            def product(out, mat, b):
                passes = [(w_hi, x_hi), (w_hi, x_lo), (w_lo, x_hi)]
                for k in range(KT):
                    for n, (w, xx) in enumerate(passes):
                        last = nc.tensor.matmul(out, w[:, mat, k, :], xx[:, k, b * S:(b + 1) * S],
                                                start=(k == 0 and n == 0), stop=(k == KT - 1 and n == 2))
                return last

            pe.wait_ge(s_wlo, 1)
            for b in range(B):
                product(ps[b][:, :], 0, b).then_inc(s_bp, 1)
            pe.wait_ge(s_beta, B)

            def head(h, first):
                for mat in range(5):
                    pe.wait_ge(s_wlo, 5 * h + mat + 2)
                    for b in range(B):
                        j = PER_MAT * mat + b
                        before = j - 5
                        if before < 0 and j == 0:
                            if not first:
                                pe.wait_ge(s_z, 4 * h)
                        elif before < 0:
                            pe.wait_ge(s_g, 4 * h + j)
                        elif before < 3 * PER_MAT:
                            pe.wait_ge(s_y, 12 * h + before + 1)
                        else:
                            pe.wait_ge(s_z, 4 * h + before - 3 * PER_MAT + 1)
                        product(bank[j][:, :], mat, b).then_inc(s_mm, 1)

            head(0, True)
            with pe.Fori(1, NH) as h:
                head(h, False)

        @block.vector
        def _(dve):
            for i in range(NT):
                dve.wait_ge(s_xhi, i + 1)
                nc.vector.tensor_tensor(x_lo[:, :, i * P:(i + 1) * P], ps[i % 4][:, :].rearrange("p (k t) -> p k t", k=KT),
                                        fp32(x_hi[:, :, i * P:(i + 1) * P]), ALU.subtract).then_inc(s_xlo, 1)

            def split_lo(mat):
                nc.vector.tensor_tensor(w_lo[:, mat, :, :], w_in[:, mat, :, :], fp32(w_hi[:, mat, :, :]), ALU.subtract).then_inc(s_wlo, 1)

            dve.wait_ge(s_whi, 1)
            split_lo(0)
            for mat in range(5):
                dve.wait_ge(s_whi, 2 + mat)
                if mat == 0:
                    dve.wait_ge(s_bp, B)
                split_lo(mat)
            dve.wait_ge(s_const, 128)
            dve.wait_ge(s_bst, 16 * B)

            tile = lambda t, b: t[:, b, :].rearrange("p (c t) -> p c t", t=CH)

            def scaled_v(h):
                dve.wait_ge(s_silu, 3 * h)
                dve.wait_ge(s_pr, N_PR * h)
                for b in range(B):
                    out = outs["vt"][:, :, b, :]
                    last = nc.vector.scalar_tensor_tensor(out=out, in0=tile(cv[2], b), scalar=float(DV) ** 0.5, in1=out,
                                                          op0=ALU.mult, op1=ALU.mult)
                last.then_inc(s_vt, 1)

            def head(h, first, more):
                def split(mat):
                    if more:
                        dve.wait_ge(s_whi, 5 * h + mat + 7)
                        split_lo(mat)

                for mat in range(3):
                    dve.wait_ge(s_y, 12 * h + 4 * mat + 4)
                    if not first:
                        dve.wait_ge(s_silu, 3 * h)
                    if mat == 0:
                        dve.wait_ge(s_zero, 3)
                    if mat == 2 and not first:
                        dve.wait_ge(s_vt, h)
                    yy, out = y[YB[mat]], cv[mat][:, :, :]
                    tap = lambda k: taps[:, bass.ds(h, 1), mat, k:k + 1].rearrange("p a k -> p (a k)")
                    bias = cbias[:, bass.ds(h, 1), mat:mat + 1].rearrange("p a k -> p (a k)")
                    nc.vector.tensor_scalar(out, yy[:, :, KW - 1:], tap(KW - 1), bias, ALU.mult, ALU.add).then_inc(s_tap, 1)
                    for k in range(KW - 1):
                        dve.wait_ge(s_tap, 12 * h + KW * mat + k + 1)
                        nc.vector.scalar_tensor_tensor(out=out, in0=yy[:, :, k:k + S], scalar=tap(k), in1=out,
                                                       op0=ALU.mult, op1=ALU.add).then_inc(s_tap, 1)
                    split(mat)
                    if mat == 0 and not first:
                        scaled_v(h)
                for b in range(B):
                    dve.wait_ge(s_mm, TILES * h + PER_MAT * A + b + 1)
                    nc.vector.tensor_scalar(av[:, b, :], bank[PER_MAT * A + b][:, :], ba_sb[:, bass.ds(h, 1)], Z_MIN,
                                            ALU.add, ALU.max).then_inc(s_z, 1)
                split(A)
                dve.wait_ge(s_exp, h + 1)
                nc.vector.tensor_scalar(ra[:, :, :], ra[:, :, :], 1.0, None, ALU.add).then_inc(s_ra, 1)
                dve.wait_ge(s_ra, h + 1)
                dve.wait_ge(s_bb, 16 * h + 16)
                for b in range(B):
                    out = outs["ng"][:, :, b, :]
                    last = nc.vector.scalar_tensor_tensor(out=out, in0=tile(ra, b), scalar=-1.0 / DV, in1=out,
                                                          op0=ALU.mult, op1=ALU.mult)
                last.then_inc(s_ng, 1)
                split(G)

            head(0, True, True)
            with dve.Fori(1, NH - 1) as h:
                head(h, False, True)
            head(NH - 1, False, False)
            scaled_v(NH)


def recurrence(nc, scr):
    GR = HB // 4
    off = [sum(BL - 1 - i for i in range(j)) for j in range(BL)]
    HALF, QUART = HB // 2, HB // 4
    with ExitStack() as ctx:
        m = Mem(nc, ctx, "pb")
        kq = [m.sb(f"kq{i}", [P, 2, HB, CH]) for i in range(2)]
        ng = m.sb("ng", [P, HB, CH])
        rr = [m.sb(f"rr{i}", [P, 2, HB, NBL]) for i in range(2)]
        vt = m.sb("vt", [P, HB, CH])
        W = m.sb("W", [P, HB, CH])
        O = [m.sb(f"O{i}", [P, HB, CH]) for i in range(2)]
        X = m.sb("X", [P, HB, CH])
        XT = m.sb("XT", [P, GR, P])
        KTr = m.sb("KT", [P, GR, P])
        Gm = m.sb("Gm", [P, GR, 2, 4, CH])
        mask = m.sb("mask", [P, 2, 4, CH])
        XD = [m.sb(f"XD{i}", [P, 4, 4, P]) for i in range(2)]
        crow = m.sb("crow", [P, HALF, P])
        UT = m.sb("UT", [P, HB, P])
        gst = m.sb("gst", [CH, 2, 512])
        gb = [m.sb(f"gb{i}", [P, HB, PAIRS]) for i in range(2)]
        tmp = m.sb("tmp", [P, HB, BL - 1])
        tk = m.sb("tk", [P, HB, BL])
        ident = m.sb("ident", [P, P])
        ps = [m.ps(f"ps{i}") for i in range(8)]
        psT, psD = ps[0:4], ps[4:8]

        s_id = m.sem("id")
        s_mask = m.sem("mask")
        s_kq = [m.sem(f"kq{i}") for i in range(2)]
        s_ngl = m.sem("ngl")
        s_rl = [m.sem(f"rl{i}") for i in range(2)]
        s_vl = m.sem("vl")
        s_crl = m.sem("crl")
        s_cr = m.sem("cr")
        s_cw = m.sem("cw")
        s_xz = m.sem("xz")
        s_gw = [m.sem(f"gw{i}") for i in range(2)]
        s_gc = m.sem("gc")
        s_gb = [m.sem(f"gb{i}") for i in range(2)]
        s_tp = m.sem("tp")
        s_te = m.sem("te")
        s_xd = m.sem("xd")
        s_dp = m.sem("dp")
        s_de = m.sem("de")
        s_gm = m.sem("gm")
        s_w = m.sem("w")
        s_x = m.sem("x")
        s_mul = m.sem("mul")
        s_add = m.sem("add")
        s_tk = m.sem("tk")
        s_wn = m.sem("wn")
        s_rs = m.sem("rs")
        s_us = m.sem("us")
        s_os = [m.sem(f"os{i}") for i in range(2)]
        T_START, T_CH = 16, 32
        T_KT, T_GRAM = 0, 6
        T_XT = [4, 10, 12, 16, 20, 22, 24, 26]
        t_xt = lambda n, hf, more: T_XT[2 * n + hf] if more else 2 * (2 * n + hf)
        t_key = lambda w, hf: 28 + 2 * hf if w else 14 + 4 * hf
        D_START, D_CH = 8, 32
        d_cross = lambda n, hf, more: 14 + 13 * hf if n == NBL - 1 and more else 2 * n + hf
        D_STATE = [6, 10, 19, 23]
        d_s = lambda j: 15 + j if j < 4 else 24 + j
        all_decays = Gm[:, :, :, :, :].rearrange("p g a i t -> p (g a i t)").rearrange("p (c x) -> p c x", c=NCH)
        decay_rows = crow[0:HB, 0:NCH, :]
        block = ctx.enter_context(nc.Block())
        flat = lambda t: t.rearrange("p h t -> p (h t)")
        window = lambda w: (slice(16 * w, 16 * w + 16), slice(max(16 * w - BL, 0), 16 * w + BL))
        solved = lambda c, n: 4 * BL * (NBL * c + n + 2)

        @block.sync
        def _(sp):
            def load(dst, name, c, sem):
                sp.dma_start(flat(dst), flat(scr[name][c, :, :, :])).then_inc(sem, 16)

            def load_kq(c, p):
                load(kq[p][:, 0, :, :], "k", c, s_kq[p])
                load(kq[p][:, 1, :, :], "q", c, s_kq[p])
                for i in range(2):
                    sp.dma_start(flat(rr[p][:, i, :, :]), scr["r"][i, c, :, :, :, :].rearrange("p h b n -> p (h b n)")).then_inc(s_rl[p], 16)

            def load_crow(c, hf):
                sp.dma_start(flat(crow[:, :, :]), scr["crow"][c, HALF * hf:HALF * (hf + 1), :].rearrange("h v -> (h v)").partition_broadcast(P)).then_inc(s_crl, 16)

            def write_grams(c, first):
                for j in range(4):
                    sp.wait_ge(s_te, first + j + 1 + 4)
                    sp.dma_start(scr["gram"][c, 0:CH * HB * CH].rearrange("(j x) -> j x", j=CH)[:, 512 * j:512 * j + 512],
                                 gst[:, j % 2, :]).then_inc(s_gw[j % 2], 16)

            def compact(c):
                for k in range(2):
                    sp.wait_ge(s_gw[k], 32 * (c + 1))
                row = HB * CH
                with nc.allow_non_contiguous_dma(reason="compaction to the pairs, once per chunk"):
                    for j in range(BL - 1):
                        first = j * row + j + 1
                        src = scr["gram"][c, first:first + NBL * (BL * row + BL)].rearrange("(n s) -> n s", n=NBL)[:, 0:row]
                        sp.dma_start(scr["pairs"][c, :, :, off[j]:off[j + 1]],
                                     src.rearrange("n (h t) -> n h t", t=CH)[:, :, 0:BL - 1 - j]).then_inc(s_gc, 16)

            def load_gb(c, n):
                sp.dma_start(flat(gb[n % 2][:, :, :]), scr["pairs"][c, n, :, :].rearrange("h k -> (h k)").partition_broadcast(P)).then_inc(s_gb[n % 2], 16)

            def chunk(c, p, more, more2):
                if more:
                    write_grams(c + 1, T_START + T_CH * c + T_GRAM)
                    sp.wait_ge(s_us, 8 * c + 4)
                    load_crow(c, 1)
                sp.wait_ge(s_x, solved(c, 0))
                load_gb(c, 2)
                if more:
                    compact(c + 1)
                sp.wait_ge(s_x, solved(c, 1))
                load_gb(c, 3)
                if more:
                    sp.wait_ge(s_gc, 16 * (BL - 1) * (c + 2))
                    load(vt[:, :, :], "vt", c + 1, s_vl)
                if more2:
                    sp.wait_ge(s_us, 8 * (c + 1))
                    load_crow(c + 1, 0)
                if more:
                    sp.wait_ge(s_x, solved(c, 2))
                    load_gb(c + 1, 0)
                    sp.wait_ge(s_x, solved(c, 3))
                    load(ng[:, :, :], "ng", c + 1, s_ngl)
                    load_gb(c + 1, 1)
                sp.wait_ge(s_de, D_START + D_CH * c + d_cross(NBL - 1, 1, more) + 1 + 4)
                sp.dma_start(flat(scr["o"][c, :, :, :]), flat(O[p][:, :, :])).then_inc(s_os[p], 16)
                if more2:
                    load_kq(c + 2, p)

            load_kq(0, 0)
            sp.dma_start(all_decays, scr["r"][1, :, :, :, :, :].rearrange("c p h b n -> p c (h b n)")).then_inc(s_cr, 16)
            write_grams(0, 0)
            load(vt[:, :, :], "vt", 0, s_vl)
            compact(0)
            load(ng[:, :, :], "ng", 0, s_ngl)
            sp.wait_ge(s_gc, 16 * (BL - 1))
            for n in range(2):
                load_gb(0, n)
            sp.wait_ge(s_te, 8 + 4)
            sp.dma_start(scr["crow"].rearrange("c h v -> h c v"), decay_rows).then_inc(s_cw, 16)
            load_kq(1, 1)
            sp.wait_ge(s_cw, 16)
            load_crow(0, 0)
            with sp.Fori(0, NCH // 2 - 1) as i:
                for p in range(2):
                    chunk(i * 2 + p, p, True, True)
            chunk(NCH - 2, 0, True, False)
            chunk(NCH - 1, 1, False, False)
            for p in range(2):
                sp.wait_ge(s_os[p], 8 * NCH + 16 * p)

        def over_chunks(eng, chunk):
            with eng.Fori(0, NCH // 2 - 1) as i:
                for p in range(2):
                    chunk(i * 2 + p, i, p, True)
            chunk(NCH - 2, NCH // 2 - 1, 0, True)
            chunk(NCH - 1, NCH // 2 - 1, 1, False)

        @block.gpsimd
        def _(pool):
            tt = nc.gpsimd.tensor_tensor
            make_identity(nc, pool, ident, s_id)
            for i in range(2):
                nc.gpsimd.memset(XD[i][:, :, :, :], 0.0).then_inc(s_xz, 1)
            nc.gpsimd.memset(UT[:, :, :], 0.0).then_inc(s_te, 4)
            nc.gpsimd.memset(O[1][:, :, :], 0.0).then_inc(s_os[1], 16)
            nc.gpsimd.memset(X[:, :, :], 0.0).then_inc(s_x, 4 * BL)
            nc.gpsimd.memset(tmp[:, :, :], 0.0).then_inc(s_de, 4)
            nc.gpsimd.memset(mask[:, :, :, :], 1.0).then_inc(s_mask, 1)
            pool.wait_ge(s_mask, 1)
            nc.gpsimd.affine_select(out=mask[:, :, :, :], in_=mask[:, :, :, :], compare_op=ALU.is_ge, fill=0.0, base=0,
                                    pattern=[[0, 2], [-CH, 4], [0, CH]], channel_multiplier=1).then_inc(s_mask, 1)
            pool.wait_ge(s_mask, 2)
            nc.gpsimd.affine_select(out=mask[:, 0, :, :], in_=mask[:, 0, :, :], compare_op=ALU.is_ge, fill=0.0, base=0,
                                    pattern=[[CH, 4], [1, CH]], channel_multiplier=-1).then_inc(s_mask, 1)
            rows = mask[:, 1, :, :].rearrange("p i (n t) -> p i n t", t=BL)
            nc.gpsimd.affine_select(out=rows, in_=rows, compare_op=ALU.is_ge, fill=0.0, base=BL - 1,
                                    pattern=[[CH, 4], [BL, NBL], [0, BL]], channel_multiplier=-1).then_inc(s_mask, 1)

            def masked(made, w, hf):
                pool.wait_ge(s_te, made + 4)
                for a, steps in enumerate(window(w)):
                    gm = Gm[:, 8 * hf:8 * hf + 8, a, :, steps]
                    by = mask[:, a, :, steps].unsqueeze(1).broadcast_to([P, 8, 4, steps.stop - steps.start])
                    tt(gm, gm, by, ALU.mult).then_inc(s_gm, 1)

            def decay(e):
                uu = UT[:, 8 * e:8 * e + 8, :]
                tt(uu, uu, crow[:, 8 * (e % 4):8 * (e % 4) + 8, :], ALU.mult).then_inc(s_us, 1)

            def chunk(c, i, p, more):
                pool.wait_ge(s_rl[p], 32 * i + 32)
                if more:
                    pool.wait_ge(s_crl, 32 * c + 16)
                    pool.wait_ge(s_dp, D_START + D_CH * c - 4)
                    decay(0)
                    decay(1)
                for n in range(NBL):
                    for hf in range(2):
                        if n + 1 < NBL:
                            pool.wait_ge(s_tp, T_START + T_CH * c + t_xt(n, hf, more) + 2)
                            xx = X[:, HALF * hf:HALF * (hf + 1), 0:BL * (n + 1)]
                            by = rr[p][:, 0, HALF * hf:HALF * (hf + 1), n + 1:n + 2].broadcast_to([P, HALF, BL * (n + 1)])
                            tt(xx, xx, by, ALU.mult).then_inc(s_rs, 1)
                        if n % 2 and more:
                            masked(T_START + T_CH * c + t_key(n // 2, hf) + 2, n // 2, hf)
                        if n + 1 < NBL and more:
                            if (n, hf) == (1, 0):
                                pool.wait_ge(s_crl, 32 * c + 32)
                                pool.wait_ge(s_dp, D_START + D_CH * c)
                            decay(2 + 2 * n + hf)

            pool.wait_ge(s_mask, 4)
            for w in range(2):
                for hf in range(2):
                    masked(8 + 4 * w + 2 * hf + 2, w, hf)
            over_chunks(pool, chunk)

        @block.scalar
        def _(act):
            def copy_t(at, j, out):
                act.wait_ge(s_tp, at + j + 1)
                nc.scalar.activation(out, psT[j % 4][:, :].rearrange("p (g k) -> p g k", g=4), ACT.Copy).then_inc(s_te, 1)

            def copy_x(c, at, hf, j):
                r, tile = 2 * hf + j, t_xt(NBL - 1, hf, True) + j
                act.wait_ge(s_tp, at + tile + 1)
                src = psT[tile % 4][:, :].rearrange("p (g k) -> p g k", g=4)
                if r >= 2:
                    act.wait_ge(s_dp, D_START + D_CH * c + D_STATE[r - 2] + 4)
                for i in range(4):
                    rows = slice(CH * i, CH * (i + 1))
                    last = nc.scalar.activation(XD[j][rows, :, i, :], src[rows, :, :], ACT.Copy)
                last.then_inc(s_xd, 1)
                nc.scalar.activation(XT[:, 4 * r:4 * r + 4, :], src, ACT.Copy).then_inc(s_te, 1)

            def copy_grams(at, first, c, fresh=False):
                for j in range(4):
                    if j >= 2 or not fresh:
                        act.wait_ge(s_gw[j % 2], 16 * (2 * c + j // 2))
                    act.wait_ge(s_tp, at + first + j + 1)
                    nc.scalar.activation(gst[:, j % 2, :], psT[(first + j) % 4][0:CH, :], ACT.Copy).then_inc(s_te, 1)

            def copy_key(at, first, w, hf):
                for j in range(2):
                    act.wait_ge(s_tp, at + first + j + 1)
                    src = psT[(first + j) % 4][:, :].rearrange("p (g a i t) -> p g a i t", g=4, a=2, i=4)
                    g = 8 * hf + 4 * j
                    for a, steps in enumerate(window(w)):
                        part = slice(16 - (steps.stop - steps.start), 16)
                        last = nc.scalar.activation(Gm[:, g:g + 4, a, :, steps], src[:, :, 1 - a, :, part], ACT.Copy)
                    last.then_inc(s_te, 1)

            def chunk(c, i, p, more):
                at = T_START + T_CH * c
                if more:
                    for j in range(4):
                        copy_t(at, T_KT + j, KTr[:, 4 * j:4 * j + 4, :])
                for n in range(NBL):
                    for hf in range(2):
                        for j in range(2):
                            g = 8 * hf + 4 * j
                            if n == NBL - 1 and more:
                                copy_x(c, at, hf, j)
                            else:
                                copy_t(at, t_xt(n, hf, more) + j, XT[:, g:g + 4, :])
                        if (n, hf) == (0, 0) and more:
                            copy_grams(at, T_GRAM, c + 1)
                        if n == 1 and more:
                            copy_key(at, t_key(0, hf), 0, hf)
                if more:
                    for hf in range(2):
                        copy_key(at, t_key(1, hf), 1, hf)

            act.wait_ge(s_xz, 2)
            copy_grams(0, 0, 0, True)
            for j in range(4):
                act.wait_ge(s_tp, 4 + j + 1)
                nc.scalar.activation(decay_rows[:, 4 * j:4 * j + 4, :], psT[j][0:HB, :].rearrange("p (c v) -> p c v", c=4), ACT.Copy).then_inc(s_te, 1)
            for w in range(2):
                for hf in range(2):
                    copy_key(0, 8 + 4 * w + 2 * hf, w, hf)
            over_chunks(act, chunk)

        @block.tensor
        def _(pe):
            pe.wait_ge(s_id, 2)

            def bank_t(at, j):
                pe.wait_ge(s_te, at + j + 1)
                return psT[j % 4]

            def bank_d(at, j):
                pe.wait_ge(s_de, at + j + 1)
                return psD[j % 4]

            def transposes(at, j, srcs):
                bank = bank_t(at, j)
                for q, src in enumerate(srcs):
                    last = nc.tensor.transpose(bank[:, q * P:(q + 1) * P], src, ident[:, :])
                last.then_inc(s_tp, 1)

            def grams(at, first, p):
                for j in range(4):
                    bank = bank_t(at, first + j)
                    for q in range(16):
                        k = kq[p][:, 0, 16 * j + q, :]
                        last = nc.tensor.matmul(bank[0:CH, CH * q:CH * (q + 1)], k, k, start=True, stop=True)
                    last.then_inc(s_tp, 1)

            def key_products(at, first, p, w, hf):
                for j in range(2):
                    bank = bank_t(at, first + j)
                    for q in range(4):
                        g = 8 * hf + 4 * j + q
                        last = nc.tensor.matmul(bank[:, q * P:(q + 1) * P].rearrange("p (a i t) -> p a i t", a=2, i=4),
                                                flat(kq[p][:, 0, 4 * g:4 * g + 4, :]), kq[p][:, :, 4 * g:4 * g + 4, 16 * w:16 * w + 16], start=True, stop=True)
                    last.then_inc(s_tp, 1)

            def state_products(at, d, p, j):
                bank = bank_d(at, d)
                for q in range(8):
                    last = nc.tensor.matmul(bank[:, 64 * q:64 * q + 64].rearrange("p (a t) -> p a t", a=2), UT[:, 8 * j + q, :],
                                            kq[p][:, :, 8 * j + q, :], start=True, stop=True)
                last.then_inc(s_dp, 1)

            def chunk(c, i, p, more):
                at_t, at_d = T_START + T_CH * c, D_START + D_CH * c

                def x_transposes(n, hf):
                    pe.wait_ge(s_x, 4 * BL * (NBL * c + n + 1) + 2 * BL * (hf + 1))
                    if n:
                        pe.wait_ge(s_rs, 6 * c + 2 * (n - 1) + hf + 1)
                    for j in range(2):
                        g = 8 * hf + 4 * j
                        transposes(at_t, t_xt(n, hf, more) + j, [flat(X[:, 4 * g + 4 * q:4 * g + 4 * q + 4, :]) for q in range(4)])

                def cross(n, hf):
                    kinds = 2 if n + 1 < NBL else 1
                    pe.wait_ge(s_te, at_t + t_xt(n, hf, more) + 2 + 4)
                    pe.wait_ge(s_gm, 8 * c + 4 * min(n, 1) + 2 * hf + 2)
                    bank = bank_d(at_d, d_cross(n, hf, more))
                    for q in range(8):
                        g = 8 * hf + q
                        last = nc.tensor.matmul(bank[:, 64 * q:64 * q + 32 * kinds].rearrange("p (a i t) -> p a i t", i=4, t=BL),
                                                XT[:, g, :], Gm[:, g, 0:kinds, :, BL * n:BL * (n + 1)], start=True, stop=True)
                    last.then_inc(s_dp, 1)

                def state(r):
                    pe.wait_ge(s_xd, 4 * c + r + 1)
                    pe.wait_ge(s_te, at_t + T_KT + 4 + 4)
                    for q in range(4):
                        bank = bank_d(at_d, D_STATE[r] + q)
                        nc.tensor.matmul(bank[:, :], KTr[:, 4 * r + q, :], XD[r % 2][:, q, :, :].rearrange("p i v -> p (i v)"),
                                         start=True, stop=True).then_inc(s_dp, 1)

                if more:
                    for j in range(4):
                        transposes(at_t, T_KT + j, [flat(kq[p][:, 0, 4 * g:4 * g + 4, :]) for g in range(4 * j, 4 * j + 4)])
                for n in range(NBL if not more else NBL - 1):
                    for hf in range(2):
                        x_transposes(n, hf)
                        cross(n, hf)
                        if (n, hf) == (0, 0) and more:
                            pe.wait_ge(s_kq[1 - p], 32 * (i + p) + 32)
                            grams(at_t, T_GRAM, 1 - p)
                        if n == 1 and more:
                            key_products(at_t, t_key(0, hf), 1 - p, 0, hf)
                if more:
                    x_transposes(NBL - 1, 0)
                    state(0)
                    x_transposes(NBL - 1, 1)
                    state(1)
                    cross(NBL - 1, 0)
                    pe.wait_ge(s_de, at_d + D_STATE[1] + 4 + 4)
                    for j in range(4):
                        state_products(at_d, d_s(j), 1 - p, j)
                    state(2)
                    state(3)
                    cross(NBL - 1, 1)
                    pe.wait_ge(s_de, at_d + D_STATE[3] + 4 + 4)
                    for j in range(4, 8):
                        state_products(at_d, d_s(j), 1 - p, j)
                    for hf in range(2):
                        key_products(at_t, t_key(1, hf), 1 - p, 1, hf)

            pe.wait_ge(s_kq[0], 32)
            grams(0, 0, 0)
            pe.wait_ge(s_te, 4)
            for j in range(4):
                state_products(0, j, 0, j)
            pe.wait_ge(s_cr, 16)
            for j in range(NCH // 4):
                bank = bank_t(0, 4 + j)
                for q in range(4):
                    decays = all_decays[:, 4 * j + q, :].rearrange("p (h n) -> p h n", n=NBL)[:, :, NBL - 1]
                    last = nc.tensor.transpose(bank[0:HB, q * P:(q + 1) * P], decays, ident[:, :])
                last.then_inc(s_tp, 1)
            for w in range(2):
                for hf in range(2):
                    key_products(0, 8 + 4 * w + 2 * hf, 0, w, hf)
            for j in range(4, 8):
                state_products(0, j, 0, j)
            over_chunks(pe, chunk)

        @block.vector
        def _(dve):
            tt = nc.vector.tensor_tensor
            blocks = lambda t: t.rearrange("p h (n t) -> p h n t", t=BL)
            groups = lambda t: t.rearrange("p (g i) t -> p g i t", i=4)

            def tile(at, j):
                dve.wait_ge(s_dp, at + j + 1)
                return psD[j % 4]

            def start(at, d, c, p, hf):
                for j in range(4):
                    src = tile(at, d + j)[:, :].rearrange("p (h a t) -> p h a t", h=8, a=2)
                    hs = slice(HALF * hf + 8 * j, HALF * hf + 8 * j + 8)
                    cr = rr[p][:, 1, hs, :].unsqueeze(3).broadcast_to([P, 8, NBL, BL])
                    tt(blocks(W[:, hs, :]), blocks(src[:, :, 0, :]), cr, ALU.mult)
                    tt(blocks(O[p][:, hs, :]), blocks(src[:, :, 1, :]), cr, ALU.mult).then_inc(s_de, 1)
                dve.wait_ge(s_vl, 16 * c + 16)
                dve.wait_ge(s_de, at + d + 4 + 4)
                hs = slice(HALF * hf, HALF * (hf + 1))
                tt(W[:, hs, :], W[:, hs, :], vt[:, hs, :], ALU.subtract).then_inc(s_w, 1)

            def chunk(c, i, p, more):
                at = D_START + D_CH * c

                def solve(n, hf):
                    m28 = 28 * (NBL * c + n) + 14 * hf
                    x0 = 4 * BL * (NBL * c + n + 1) + 2 * BL * hf
                    if n == 0:
                        dve.wait_ge(s_w, 2 * c + hf + 1)
                    else:
                        dve.wait_ge(s_wn, 6 * c + 2 * (n - 1) + hf + 1)
                    dve.wait_ge(s_gb[n % 2], 16 * (2 * c + n // 2 + 1))
                    quarters = [(q, slice(QUART * (2 * hf + q), QUART * (2 * hf + q + 1))) for q in range(2)]
                    for t in range(BL):
                        step = BL * n + t
                        w = BL - 1 - t
                        for q, hs in quarters:
                            if t:
                                dve.wait_ge(s_add, m28 + 2 * (t - 1) + q + 1)
                            tt(X[:, hs, step], ng[:, hs, step], W[:, hs, step], ALU.mult).then_inc(s_x, 1)
                        if not w:
                            break
                        for q, hs in quarters:
                            dve.wait_ge(s_x, x0 + 2 * t + q + 1)
                            tt(tmp[:, hs, 0:w], gb[n % 2][:, hs, off[t]:off[t] + w], X[:, hs, step:step + 1].broadcast_to([P, QUART, w]),
                               ALU.mult).then_inc(s_mul, 1)
                        for q, hs in quarters:
                            dve.wait_ge(s_mul, m28 + 2 * t + q + 1)
                            ww = W[:, hs, step + 1:BL * (n + 1)]
                            tt(ww, ww, tmp[:, hs, 0:w], ALU.add).then_inc(s_add, 1)

                def cross(n, hf):
                    src = tile(at, d_cross(n, hf, more))[:, :].rearrange("p (g a i t) -> p g a i t", g=8, a=2, i=4)
                    hs = slice(HALF * hf, HALF * (hf + 1))
                    if n + 1 < NBL:
                        rb = groups(rr[p][:, 0, hs, n + 1:n + 2]).broadcast_to([P, 8, 4, BL])
                        tt(groups(tk[:, hs, :]), src[:, :, 1, :, :], rb, ALU.mult).then_inc(s_tk, 1)
                    oo = groups(O[p][:, hs, BL * n:BL * (n + 1)])
                    tt(oo, oo, src[:, :, 0, :, :], ALU.add).then_inc(s_de, 1)
                    if n + 1 < NBL:
                        dve.wait_ge(s_tk, 6 * c + 2 * n + hf + 1)
                        ww = W[:, hs, BL * (n + 1):BL * (n + 2)]
                        tt(ww, ww, tk[:, hs, :], ALU.add).then_inc(s_wn, 1)

                def state(r):
                    dve.wait_ge(s_us, 8 * c + 2 * (r + 1))
                    for q in range(4):
                        g = 4 * r + q
                        uu = flat(UT[:, 4 * g:4 * g + 4, :])
                        tt(uu, uu, tile(at, D_STATE[r] + q)[:, :], ALU.add).then_inc(s_de, 1)

                dve.wait_ge(s_ngl, 16 * c + 16)
                for n in range(NBL):
                    for hf in range(2):
                        if (n, hf) == (0, 1):
                            start(at, -4, c, p, 1)
                        if n:
                            cross(n - 1, hf)
                        solve(n, hf)
                if not more:
                    cross(NBL - 1, 0)
                    cross(NBL - 1, 1)
                    return
                state(0)
                state(1)
                cross(NBL - 1, 0)
                dve.wait_ge(s_rl[1 - p], 32 * (i + p) + 32)
                dve.wait_ge(s_os[1 - p], 16 * (i + 1))
                start(at, d_s(0), c + 1, 1 - p, 0)
                state(2)
                state(3)
                cross(NBL - 1, 1)

            dve.wait_ge(s_rl[0], 32)
            start(0, 0, 0, 0, 0)
            over_chunks(dve, chunk)


def attention_out(nc, x, wo, ln_w, ln_b, scr, res, stat):
    with ExitStack() as ctx:
        m = Mem(nc, ctx, "pc")
        wo_more = [m.sb(f"wo_in{i}", [P, 4, HID]) for i in range(1, 4)]
        wo_hi = m.sb("wo_hi", [P, NH, HID], F32R)
        wo_lo = m.sb("wo_lo", [P, NH, HID], F32R)
        o_in = [m.sb(f"o_in{i}", [P, NH, CT]) for i in range(2)]
        g_in = m.sb("g_in", [P, NH, CT])
        a_in = m.sb("a_in", [P, NH, CT])
        x_in = [m.sb(f"x_in{i}", [P, HID]) for i in range(2)]
        sq = m.sb("sq", [P, NH, CT])
        og_hi = [m.sb(f"og_hi{i}", [P, NH, CT], F32R) for i in range(2)]
        og_lo = [m.sb(f"og_lo{i}", [P, NH, CT], F32R) for i in range(2)]
        lnw = m.sb("lnw", [P, 1])
        lnb = m.sb("lnb", [P, 1])
        eps = m.sb("eps", [P, 1])
        mean1 = m.sb("mean1", [P, P])
        rs = m.sb("rs", [P, HID])
        bn = m.sb("bn", [P, 6])
        bn_all = m.sb("bn_all", [P, NCH, 6])
        none = m.sb("none", [P, 4])
        ps = [m.ps(f"ps{i}") for i in range(8)]

        s_c = m.sem("c")
        s_wl = [m.sem(f"wl{i}") for i in range(4)]
        s_wh = m.sem("wh")
        s_wo = m.sem("wo")
        s_o = [m.sem(f"o{i}") for i in range(2)]
        s_a = m.sem("a")
        s_oa = m.sem("oa")
        s_g = m.sem("g")
        s_x = [m.sem(f"x{i}") for i in range(2)]
        s_mu = m.sem("mu")
        s_d = m.sem("d")
        s_sq = m.sem("sq")
        s_var = m.sem("var")
        s_ln = m.sem("ln")
        s_rs = m.sem("rs")
        s_n = m.sem("n")
        s_hi = m.sem("hi")
        s_lo = m.sem("lo")
        s_p = m.sem("p")
        s_r = m.sem("r")
        s_bn = m.sem("bn")
        s_st = m.sem("st")
        wo_in = [o_in[1][:, :, :].rearrange("p (h x) t -> p h (x t)", h=4)] + [t[:, :, :] for t in wo_more]
        block = ctx.enter_context(nc.Block())
        four = lambda t, j: t[:, 4 * j:4 * j + 4, :].rearrange("p h t -> p (h t)")

        @block.sync
        def _(sp):
            sp.dma_start(lnw[:, :], ln_w.rearrange("(p o) -> p o", o=1)).then_inc(s_c, 16)
            sp.dma_start(lnb[:, :], ln_b.rearrange("(p o) -> p o", o=1)).then_inc(s_c, 16)

            flat = lambda t: t.rearrange("p h t -> p (h t)")

            def load(dst, name, c, sem):
                sp.dma_start(flat(dst[:, :, :]), flat(scr[name][c, :, :, :])).then_inc(sem, 16)

            def load_x(c, p):
                for b in range(B):
                    sp.dma_start(x_in[p][b * CH:(b + 1) * CH, :], x.rearrange("b (c t) d -> c b t d", t=CH)[c, b, :, :]).then_inc(s_x[p], 16)

            load(o_in[0], "o", 0, s_o[0])
            load(a_in, "A", 0, s_a)
            load(g_in, "g", 0, s_g)
            for j in range(4):
                sp.dma_start(wo_in[j], wo.rearrange("(h p) d -> p h d", p=P)[:, 4 * j:4 * j + 4, :]).then_inc(s_wl[j], 16)
            sp.wait_ge(s_wo, 4)
            load(o_in[1], "o", 1, s_o[1])
            for c in (1, 2):
                sp.wait_ge(s_oa, c)
                load(a_in, "A", c, s_a)
            load_x(0, 0)
            sp.wait_ge(s_n, 6)
            load(g_in, "g", 1, s_g)

            def chunk(c, p, left):
                if left >= 2:
                    sp.wait_ge(s_lo, c + 1)
                    load(o_in[p], "o", c + 2, s_o[p])
                sp.wait_ge(s_r, c + 2)
                load_x(c + 1, 1 - p)
                if left >= 2:
                    sp.wait_ge(s_n, 3 * c + 9)
                    load(g_in, "g", c + 2, s_g)
                if left >= 3:
                    sp.wait_ge(s_oa, c + 3)
                    load(a_in, "A", c + 3, s_a)

            with sp.Fori(0, NCH // 2 - 2) as i:
                for p in range(2):
                    chunk(i * 2 + p, p, 3)
            for left in (3, 2, 1):
                chunk(NCH - 1 - left, (NCH - 1 - left) % 2, left)

        @block.gpsimd
        def _(pool):
            nc.gpsimd.memset(mean1[:, :], 1.0 / DV).then_inc(s_c, 1)
            nc.gpsimd.memset(eps[:, :], EPS).then_inc(s_c, 1)
            for j, (sem, start) in enumerate([(s_n, 3), (s_ln, 4), (s_p, 2), (s_r, 2)]):
                nc.gpsimd.memset(none[:, j:j + 1], 0.0).then_inc(sem, start)
            nc.gpsimd.memset(bn[:, :], 0.0).then_inc(s_st, 1)
            with pool.Fori(0, NCH // 2) as i:
                for p in range(2):
                    pool.wait_ge(s_o[p], 16 * i + 16)
                    pool.wait_ge(s_a, 32 * i + 16 * p + 16)
                    nc.gpsimd.tensor_tensor(o_in[p][:, :, :], o_in[p][:, :, :], a_in[:, :, :], ALU.mult).then_inc(s_oa, 1)

        @block.scalar
        def _(act):
            act.wait_ge(s_c, 34)

            def stage1(c, i, p):
                act.wait_ge(s_n, 3 * c + 3)
                for j in range(4):
                    act.wait_ge(s_d, 4 * c + j + 1)
                    nc.scalar.activation(four(sq, j), four(o_in[p], j), ACT.Square).then_inc(s_sq, 1)
                for j in range(4):
                    act.wait_ge(s_var, 4 * c + j + 1)
                    nc.scalar.activation(four(sq, j), ps[j][:, :], ACT.Ln, bias=eps[:, 0:1]).then_inc(s_ln, 1)
                act.wait_ge(s_ln, 4 * c + 8)
                nc.scalar.activation(sq[:, :, :], sq[:, :, :], ACT.Exp, scale=-0.5).then_inc(s_rs, 1)

            def stage2(c, i, p):
                act.wait_ge(s_n, 3 * c + 6)
                act.wait_ge(s_p, c + 1)
                nc.scalar.activation(og_hi[p][:, :, :], o_in[p][:, :, :], ACT.Copy).then_inc(s_hi, 1)

            stage1(0, 0, 0)
            for h in range(NH):
                if h % 4 == 0:
                    act.wait_ge(s_wl[h // 4], 16)
                nc.scalar.activation(wo_hi[:, h, :], wo_in[h // 4][:, h % 4, :], ACT.Copy).then_inc(s_wh, 1)
            stage2(0, 0, 0)
            stage1(1, 0, 1)
            stage2(1, 0, 1)
            with act.Fori(0, NCH // 2 - 1) as i:
                for p in range(2):
                    stage1(i * 2 + p + 2, i + 1, p)
                    stage2(i * 2 + p + 2, i + 1, p)

        @block.tensor
        def _(pe):
            pe.wait_ge(s_c, 34)

            def stage1(c, i, p):
                pe.wait_ge(s_oa, c + 1)
                pe.wait_ge(s_ln, 4 * c + 4)
                for j in range(4):
                    nc.tensor.matmul(ps[j][:, :], mean1[:, :], four(o_in[p], j), start=True, stop=True).then_inc(s_mu, 1)

            def stage1b(c):
                for j in range(4):
                    pe.wait_ge(s_sq, 4 * c + j + 1)
                    nc.tensor.matmul(ps[j][:, :], mean1[:, :], four(sq, j), start=True, stop=True).then_inc(s_var, 1)

            def stage2(c, i, p):
                pe.wait_ge(s_lo, c + 1)
                pe.wait_ge(s_wo, NH)
                pe.wait_ge(s_r, c + 1)
                passes = [(og_hi[p], wo_hi), (og_hi[p], wo_lo), (og_lo[p], wo_hi)]
                for h in range(NH):
                    for n, (og, w) in enumerate(passes):
                        last = nc.tensor.matmul(ps[4 + p][:, :], og[:, h, :], w[:, h, :], start=(h == 0 and n == 0), stop=(h == NH - 1 and n == 2))
                last.then_inc(s_p, 1)

            stage1(0, 0, 0)
            stage1b(0)
            with pe.Fori(0, NCH // 2 - 1) as i:
                for p in range(2):
                    stage1(i * 2 + p + 1, i + p, 1 - p)
                    stage1b(i * 2 + p + 1)
                    stage2(i * 2 + p, i, p)
            stage1(NCH - 1, NCH // 2 - 1, 1)
            stage1b(NCH - 1)
            stage2(NCH - 2, NCH // 2 - 1, 0)
            stage2(NCH - 1, NCH // 2 - 1, 1)

        @block.vector
        def _(dve):
            dve.wait_ge(s_c, 34)

            def stage1(c, i, p):
                for j in range(4):
                    dve.wait_ge(s_mu, 4 * c + j + 1)
                    nc.vector.tensor_tensor(four(o_in[p], j), four(o_in[p], j), ps[j][:, :], ALU.subtract).then_inc(s_d, 1)

            def stage2(c, i, p):
                t = o_in[p][:, :, :]
                dve.wait_ge(s_rs, c + 1)
                nc.vector.tensor_tensor(t, t, sq[:, :, :], ALU.mult).then_inc(s_n, 1)
                dve.wait_ge(s_n, 3 * c + 4)
                nc.vector.tensor_scalar(t, t, lnw[:, 0:1], lnb[:, 0:1], ALU.mult, ALU.add).then_inc(s_n, 1)
                dve.wait_ge(s_n, 3 * c + 5)
                dve.wait_ge(s_g, 16 * c + 16)
                nc.vector.tensor_tensor(t, t, g_in[:, :, :], ALU.mult).then_inc(s_n, 1)

            def low(c, p):
                dve.wait_ge(s_hi, c + 1)
                nc.vector.tensor_tensor(og_lo[p][:, :, :], o_in[p][:, :, :], fp32(og_hi[p][:, :, :]), ALU.subtract).then_inc(s_lo, 1)

            def stage3(c, i, p):
                dve.wait_ge(s_p, c + 1 + 2)
                dve.wait_ge(s_x[p], 64 * i + 64)
                dve.wait_ge(s_st, c + 1)
                nc.vector.tensor_tensor(rs[:, :], ps[4 + p][:, :], x_in[p][:, :], ALU.add).then_inc(s_r, 1)
                dve.wait_ge(s_r, c + 1 + 2)
                nc.vector.bn_stats(bn[:, :], rs[:, :]).then_inc(s_bn, 1)
                nc.vector.tensor_copy(res[:, bass.ds(c, 1), :], rs[:, :].unsqueeze(1))
                dve.wait_ge(s_bn, c + 1)
                nc.vector.tensor_copy(bn_all[:, bass.ds(c, 1), :], bn[:, :].unsqueeze(1)).then_inc(s_st, 1)

            stage1(0, 0, 0)
            for h in range(NH):
                dve.wait_ge(s_wh, h + 1)
                nc.vector.tensor_tensor(wo_lo[:, h, :], wo_in[h // 4][:, h % 4, :], fp32(wo_hi[:, h, :]), ALU.subtract).then_inc(s_wo, 1)
            stage2(0, 0, 0)
            stage1(1, 0, 1)
            low(0, 0)
            stage2(1, 0, 1)
            with dve.Fori(0, NCH // 2 - 1) as i:
                for p in range(2):
                    stage1(i * 2 + p + 2, i + 1, p)
                    low(i * 2 + p + 1, 1 - p)
                    stage3(i * 2 + p, i, p)
                    stage2(i * 2 + p + 2, i + 1, p)
            low(NCH - 1, 1)
            stage3(NCH - 2, NCH // 2 - 1, 0)
            stage3(NCH - 1, NCH // 2 - 1, 1)
            dve.wait_ge(s_st, NCH + 1)
            for c in range(NCH):
                nc.vector.bn_aggr(stat[:, c, :], bn_all[:, c, :])


def ternary(nc, mats, tern, scales):
    NP = E * HID // P // HID
    COUNT = float(E * HID)
    with ExitStack() as ctx:
        m = Mem(nc, ctx, "pd")
        w = [m.sb(f"w{i}", [P, NP, HID]) for i in range(2)]
        junk = m.sb("junk", [P, 4, HID], mybir.dt.bfloat16)
        low = m.sb("low", [P, 4, HID])
        ident = m.sb("ident", [P, P])
        ones = m.sb("ones", [P, P])
        part = m.sb("part", [P, 3, 4])
        tot = m.sb("tot", [P, 3])
        half = m.sb("half", [P, 3, 2])
        ps = [m.ps(f"ps{i}") for i in range(8)]
        s_id = m.sem("id")
        s_c = m.sem("c")
        s_w = [[m.sem(f"w{i}_{j}") for j in range(4)] for i in range(2)]
        s_abs = m.sem("abs")
        s_tot = m.sem("tot")
        s_sum = m.sem("sum")
        s_sc = m.sem("sc")
        s_low = m.sem("low")
        s_q = m.sem("q")
        s_tr = m.sem("tr")
        s_ev = m.sem("ev")
        block = ctx.enter_context(nc.Block())
        views = [mats[0].rearrange("(n p) d -> p n d", p=P), mats[1].rearrange("(n p) d -> p n d", p=P),
                 mats[2].rearrange("(n p) (m d) -> p n m d", p=P, d=HID)]

        @block.sync
        def _(sp):
            for i in range(3):
                for j in range(4):
                    if i == 2:
                        sp.wait_ge(s_tr, 4 * j + 4)
                    part_in = views[i][:, 4 * j:4 * j + 4, :] if i < 2 else views[i][:, j, :, :]
                    sp.dma_start(w[i % 2][:, 4 * j:4 * j + 4, :], part_in).then_inc(s_w[i % 2][j], 16)

        @block.gpsimd
        def _(pool):
            make_identity(nc, pool, ident, s_id)
            nc.gpsimd.memset(ones[:, :], 1.0).then_inc(s_c, 1)

        @block.scalar
        def _(act):
            def absolute(i, j):
                act.wait_ge(s_w[i % 2][j], 16 * (i // 2 + 1))
                if i or j:
                    act.wait_ge(s_abs, 4 * i + j)
                nc.scalar.activation(junk[:, :, :], w[i % 2][:, 4 * j:4 * j + 4, :], ACT.Abs,
                                     accum_out=part[:, i, j:j + 1]).then_inc(s_abs, 1)

            for i in range(2):
                for j in range(4):
                    absolute(i, j)
            for i in range(3):
                for n in range(NP):
                    act.wait_ge(s_tr, NP * i + n + 1)
                    nc.scalar.activation(dest(tern, i, n), ps[2 + n % 4][:, :].rearrange("p (k e) -> p k e", k=4), ACT.Copy).then_inc(s_ev, 1)
                    if i == 1 and n % 3 == 2 and n < 12:
                        absolute(2, n // 3)

        @block.tensor
        def _(pe):
            pe.wait_ge(s_c, 1)
            pe.wait_ge(s_id, 2)
            for i in range(3):
                pe.wait_ge(s_tot, i + 1)
                nc.tensor.matmul(ps[i % 2][:, 0:1], ones[:, :], tot[:, i:i + 1], start=True, stop=True).then_inc(s_sum, 1)
                for n in range(NP):
                    j = NP * i + n
                    pe.wait_ge(s_q, 4 * i + n // 4 + 1)
                    if j >= 4:
                        pe.wait_ge(s_ev, j - 3)
                    for k in range(4):
                        last = nc.tensor.transpose(ps[2 + n % 4][:, k * P:(k + 1) * P], w[i % 2][:, n, k * P:(k + 1) * P], ident[:, :])
                    last.then_inc(s_tr, 1)

        @block.vector
        def _(dve):
            for i in range(3):
                dve.wait_ge(s_abs, 4 * i + 4)
                nc.vector.tensor_reduce(tot[:, i:i + 1], part[:, i, :], AX.X, ALU.add).then_inc(s_tot, 1)
                dve.wait_ge(s_sum, i + 1)
                nc.vector.tensor_scalar(scales[:, i:i + 1], ps[i % 2][:, 0:1], 1.0 / COUNT, 1e-8, ALU.mult, ALU.add).then_inc(s_sc, 1)
                dve.wait_ge(s_sc, 3 * i + 1)
                nc.vector.tensor_scalar(half[:, i, 0:1], scales[:, i:i + 1], 0.5, None, ALU.mult).then_inc(s_sc, 1)
                nc.vector.tensor_scalar(half[:, i, 1:2], scales[:, i:i + 1], -0.5, None, ALU.mult).then_inc(s_sc, 1)
                dve.wait_ge(s_sc, 3 * i + 3)
                for j in range(4):
                    ww = w[i % 2][:, 4 * j:4 * j + 4, :].rearrange("p n d -> p (n d)")
                    ll = low[:, :, :].rearrange("p n d -> p (n d)")
                    if i or j:
                        dve.wait_ge(s_q, 4 * i + j)
                    nc.vector.tensor_scalar(ll, ww, half[:, i, 1:2], None, ALU.is_lt).then_inc(s_low, 1)
                    dve.wait_ge(s_low, 4 * i + j + 1)
                    nc.vector.scalar_tensor_tensor(out=ww, in0=ww, scalar=half[:, i, 0:1], in1=ll, op0=ALU.is_gt, op1=ALU.subtract).then_inc(s_q, 1)


def dest(tern, i, n):
    if i < 2:
        return tern[i][:, :, n * P:(n + 1) * P]
    a, b = n // 4, n % 4
    return tern[2][:, 4 * b:4 * b + 4, a * P:(a + 1) * P]


def feed_forward(nc, tern, scales, res, stat, out):
    EB = E // 512
    with ExitStack() as ctx:
        m = Mem(nc, ctx, "pe")
        ident = m.sb("ident", [P, P])
        eps = m.sb("eps", [P, 1])
        rstd = m.sb("rstd", [P, NCH])
        std = m.sb("std", [P, NCH])
        x1s = [m.sb(f"x1s{i}", [P, HID]) for i in range(2)]
        xT_hi = [m.sb(f"xT_hi{i}", [P, KT, P], F32R) for i in range(2)]
        xT_lo = [m.sb(f"xT_lo{i}", [P, KT, P], F32R) for i in range(2)]
        sil = [m.sb(f"sil{i}", [P, 512]) for i in range(2)]
        hid = [m.sb(f"hid{i}", [P, 512]) for i in range(2)]
        hT_hi = [m.sb(f"hT_hi{i}", [P, 4, P], F32R) for i in range(2)]
        hT_lo = [m.sb(f"hT_lo{i}", [P, 4, P], F32R) for i in range(2)]
        ys = [m.sb(f"ys{i}", [P, HID]) for i in range(2)]
        bn = m.sb("bn", [P, 6])
        mv = m.sb("mv", [P, 2])
        sd = m.sb("sd", [P, 1])
        rs = m.sb("rs", [P, 1])
        ps = [m.ps(f"ps{i}") for i in range(8)]
        s_id = m.sem("id")
        s_c = m.sem("c")
        s_sd = m.sem("sd")
        s_rd = m.sem("rd")
        s_x1 = m.sem("x1")
        s_xt = m.sem("xt")
        s_xh = m.sem("xh")
        s_xl = m.sem("xl")
        s_ug = m.sem("ug")
        s_si = m.sem("si")
        s_h = m.sem("h")
        s_ht = m.sem("ht")
        s_hh = m.sem("hh")
        s_hl = m.sem("hl")
        s_dn = m.sem("dn")
        s_r = m.sem("r")
        s_bn = m.sem("bn")
        s_mv = m.sem("mv")
        s_rs = m.sem("rs")
        s_y = m.sem("y")
        s_out = [m.sem(f"out{i}") for i in range(2)]
        block = ctx.enter_context(nc.Block())
        tile = lambda t, c: t[:, bass.ds(c, 1), :].rearrange("p o d -> p (o d)")
        out_v = out.rearrange("b (c t) d -> c b t d", t=CH)

        @block.sync
        def _(sp):
            with sp.Fori(0, NCH // 2) as i:
                for p in range(2):
                    c = i * 2 + p
                    sp.wait_ge(s_y, c + 1)
                    for b in range(B):
                        sp.dma_start(out_v[c, b, :, :], ys[p][b * CH:(b + 1) * CH, :]).then_inc(s_out[p], 16)
            for p in range(2):
                sp.wait_ge(s_out[p], 16 * B * (NCH // 2 + 1))

        @block.gpsimd
        def _(pool):
            make_identity(nc, pool, ident, s_id)
            nc.gpsimd.memset(eps[:, :], EPS).then_inc(s_c, 1)
            for p in range(2):
                nc.gpsimd.memset(ys[p][:, :], 0.0).then_inc(s_out[p], 16 * B)

        def split_hi(act, out, bank):
            return nc.scalar.activation(out[:, :, :], bank[:, :].rearrange("p (k t) -> p k t", k=4), ACT.Copy)

        @block.scalar
        def _(act):
            act.wait_ge(s_c, 1)
            nc.scalar.activation(std[:, :], stat[:, :, 1], ACT.Sqrt, bias=eps[:, 0:1]).then_inc(s_sd, 1)

            def x_hi(c, p):
                act.wait_ge(s_xt, c + 1)
                split_hi(act, xT_hi[p], ps[7]).then_inc(s_xh, 1)

            def silu(c, e):
                act.wait_ge(s_ug, EB * c + e + 1)
                nc.scalar.activation(sil[e % 2][:, :], ps[2 * (e % 2)][:, :], ACT.Silu, scale=scales[:, 0:1]).then_inc(s_si, 1)

            def h_hi(c, e):
                act.wait_ge(s_ht, EB * c + e + 1)
                split_hi(act, hT_hi[e % 2], ps[4 + e % 2]).then_inc(s_hh, 1)

            def deviation(c):
                act.wait_ge(s_mv, c + 1)
                nc.scalar.activation(sd[:, :], mv[:, 1:2], ACT.Sqrt, bias=eps[:, 0:1]).then_inc(s_sd, 1)

            def chunk(c, p, more, first=False):
                silu(c, 0)
                silu(c, 1)
                h_hi(c, 0)
                silu(c, 2)
                h_hi(c, 1)
                silu(c, 3)
                if more:
                    x_hi(c + 1, 1 - p)
                h_hi(c, 2)
                h_hi(c, 3)
                if not first:
                    deviation(c - 1)

            x_hi(0, 0)
            chunk(0, 0, True, True)
            with act.Fori(0, NCH // 2 - 1) as i:
                chunk(i * 2 + 1, 1, True)
                chunk(i * 2 + 2, 0, True)
            chunk(NCH - 1, 1, False)
            deviation(NCH - 1)

        @block.tensor
        def _(pe):
            pe.wait_ge(s_id, 2)

            def x_tp(c, p, first=False):
                pe.wait_ge(s_x1, c + 1)
                if not first:
                    pe.wait_ge(s_xl, c)
                for k in range(KT):
                    last = nc.tensor.transpose(ps[7][:, k * P:(k + 1) * P], x1s[p][:, k * P:(k + 1) * P], ident[:, :])
                last.then_inc(s_xt, 1)

            def up_gate(c, p, e):
                pe.wait_ge(s_xl, c + 1)
                pe.wait_ge(s_h, EB * c + e + (2 - 1))
                for n in range(2):
                    for k in range(KT):
                        for q, xx in enumerate((xT_hi[p], xT_lo[p])):
                            last = nc.tensor.matmul(ps[2 * (e % 2) + n][:, :], xx[:, k, :], tern[n][:, k, e * 512:(e + 1) * 512],
                                                    start=(k == 0 and q == 0), stop=(k == KT - 1 and q == 1))
                last.then_inc(s_ug, 1)

            def h_t(c, e):
                pe.wait_ge(s_h, EB * c + e + 1 + 2)
                pe.wait_ge(s_hl, EB * c + e + 1)
                for k in range(4):
                    last = nc.tensor.transpose(ps[4 + e % 2][:, k * P:(k + 1) * P], hid[e % 2][:, k * P:(k + 1) * P], ident[:, :])
                last.then_inc(s_ht, 1)

            def down(c, e, first=False):
                pe.wait_ge(s_hl, EB * c + e + 1 + 2)
                if e == 0 and not first:
                    pe.wait_ge(s_r, c)
                for k in range(4):
                    for q, hh in enumerate((hT_hi[e % 2], hT_lo[e % 2])):
                        last = nc.tensor.matmul(ps[6][:, :], hh[:, k, :], tern[2][:, 4 * e + k, :],
                                                start=(e == 0 and k == 0 and q == 0), stop=(e == EB - 1 and k == 3 and q == 1))
                last.then_inc(s_dn, 1)

            def chunk(c, p, more, first=False):
                up_gate(c, p, 0)
                up_gate(c, p, 1)
                h_t(c, 0)
                up_gate(c, p, 2)
                h_t(c, 1)
                down(c, 0, first)
                up_gate(c, p, 3)
                h_t(c, 2)
                down(c, 1)
                if more:
                    x_tp(c + 1, 1 - p)
                h_t(c, 3)
                down(c, 2)
                down(c, 3)

            x_tp(0, 0, True)
            chunk(0, 0, True, True)
            with pe.Fori(0, NCH // 2 - 1) as i:
                chunk(i * 2 + 1, 1, True)
                chunk(i * 2 + 2, 0, True)
            chunk(NCH - 1, 1, False)

        @block.vector
        def _(dve):
            nc.vector.memset(bn[:, :], 0.0).then_inc(s_h, 2)
            nc.vector.memset(rstd[:, :], 0.0).then_inc(s_hl, 2)
            dve.wait_ge(s_sd, 1)
            dve.wait_ge(s_hl, 2)
            nc.vector.reciprocal(rstd[:, :], std[:, :]).then_inc(s_rd, 1)
            dve.wait_ge(s_rd, 1)

            def x1(c, p):
                nc.vector.tensor_scalar(x1s[p][:, :], tile(res, c), stat[:, bass.ds(c, 1), 0:1].rearrange("p o d -> p (o d)"),
                                        rstd[:, bass.ds(c, 1)], ALU.subtract, ALU.mult).then_inc(s_x1, 1)

            def x_lo(c, p):
                dve.wait_ge(s_xh, c + 1)
                nc.vector.tensor_tensor(xT_lo[p][:, :, :], ps[7][:, :].rearrange("p (k t) -> p k t", k=4), fp32(xT_hi[p][:, :, :]), ALU.subtract).then_inc(s_xl, 1)

            def hidden(c, e):
                dve.wait_ge(s_si, EB * c + e + 1)
                nc.vector.scalar_tensor_tensor(out=hid[e % 2][:, :], in0=ps[2 * (e % 2) + 1][:, :], scalar=scales[:, 1:2], in1=sil[e % 2][:, :],
                                               op0=ALU.mult, op1=ALU.mult).then_inc(s_h, 1)

            def h_lo(c, e):
                dve.wait_ge(s_hh, EB * c + e + 1)
                nc.vector.tensor_tensor(hT_lo[e % 2][:, :, :], ps[4 + e % 2][:, :].rearrange("p (k t) -> p k t", k=4), fp32(hT_hi[e % 2][:, :, :]), ALU.subtract).then_inc(s_hl, 1)

            def chunk(c, i, p, more, first=False):
                def x1_next():
                    if more:
                        x1(c + 1, 1 - p)

                if first:
                    x1_next()
                else:
                    statistics(c - 1, x1_next)
                hidden(c, 0)
                hidden(c, 1)
                h_lo(c, 0)
                hidden(c, 2)
                h_lo(c, 1)
                hidden(c, 3)
                if more:
                    x_lo(c + 1, 1 - p)
                h_lo(c, 2)
                h_lo(c, 3)
                if not first:
                    last_norm(c - 1, 1 - p)
                dve.wait_ge(s_dn, EB * (c + 1))
                dve.wait_ge(s_x1, c + 1)
                dve.wait_ge(s_out[p], 16 * B * i + 16 * B)
                nc.vector.scalar_tensor_tensor(out=ys[p][:, :], in0=ps[6][:, :], scalar=scales[:, 2:3], in1=x1s[p][:, :],
                                               op0=ALU.mult, op1=ALU.add).then_inc(s_r, 1)
                dve.wait_ge(s_r, c + 1)
                nc.vector.bn_stats(bn[:, :], ys[p][:, :]).then_inc(s_bn, 1)

            def statistics(c, between):
                dve.wait_ge(s_bn, c + 1)
                between()
                nc.vector.bn_aggr(mv[:, :], bn[:, :]).then_inc(s_mv, 1)

            def last_norm(c, p):
                dve.wait_ge(s_sd, c + 2)
                nc.vector.reciprocal(rs[:, :], sd[:, :]).then_inc(s_rs, 1)
                dve.wait_ge(s_rs, c + 1)
                nc.vector.tensor_scalar(ys[p][:, :], ys[p][:, :], mv[:, 0:1], rs[:, 0:1], ALU.subtract, ALU.mult).then_inc(s_y, 1)

            x1(0, 0)
            x_lo(0, 0)
            chunk(0, 0, 0, True, True)
            with dve.Fori(0, NCH // 2 - 1) as i:
                chunk(i * 2 + 1, i, 1, True)
                chunk(i * 2 + 2, i + 1, 0, True)
            chunk(NCH - 1, NCH // 2 - 1, 1, False)
            statistics(NCH - 1, lambda: None)
            last_norm(NCH - 1, 1)


def layer(nc, x, Wq, Wk, Wv, Wa, ba, Wb, bb, Wg, Wo, cqw, cqb, ckw, ckb, cvw, cvb, ln_w, ln_b, W_up, W_gate, W_down, out):
    scr = {n: nc.dram_tensor(f"scratch_{n}", (NCH, P, NH, CT), F32, kind="Internal").ap() for n in ("q", "k", "ng", "vt", "A", "g", "o")}
    scr["beta"] = nc.dram_tensor("scratch_beta", (NH, TOK), F32, kind="Internal").ap()
    scr["r"] = nc.dram_tensor("scratch_r", (2, NCH, P, NH, B, NBL), F32, kind="Internal").ap()
    scr["crow"] = nc.dram_tensor("scratch_crow", (NCH, HB, P), F32, kind="Internal").ap()
    scr["gram"] = nc.dram_tensor("scratch_gram", (NCH, (BL - 1) * HB * CH + NBL * (BL * HB * CH + BL)), F32, kind="Internal").ap()
    scr["pairs"] = nc.dram_tensor("scratch_pairs", (NCH, NBL, HB, PAIRS), F32, kind="Internal").ap()
    projections(nc, x, [Wq, Wk, Wv, Wa, Wg], ba, Wb, bb, [cqw, ckw, cvw], [cqb, ckb, cvb], scr)
    recurrence(nc, scr)
    with ExitStack() as ctx:
        m = Mem(nc, ctx, "all")
        res = m.sb("res", [P, NCH, HID])
        stat = m.sb("stat", [P, NCH, 2])
        attention_out(nc, x, Wo, ln_w, ln_b, scr, res, stat)
        tern = [m.sb("t_up", [P, KT, E], F32R), m.sb("t_gate", [P, KT, E], F32R), m.sb("t_down", [P, E // P, HID], F32R)]
        scales = m.sb("scales", [P, 3])
        ternary(nc, [W_up, W_gate, W_down], tern, scales)
        feed_forward(nc, tern, scales, res, stat, out)


_INS = ["x", "Wq", "Wk", "Wv", "Wa", "ba", "Wb", "bb", "Wg", "Wo", "cqw", "cqb", "ckw", "ckb", "cvw", "cvb", "ln_w", "ln_b",
        "W_up", "W_gate", "W_down"]


def kernel(**inputs):
    import numpy as _np
    import concourse.bacc as _bacc
    from concourse import mybir as _mybir
    from concourse.bass_utils import run_bass_kernel_spmd as _run

    nc = _bacc.Bacc("TRN2", target_bir_lowering=False, num_devices=1)
    arrays, args = {}, []
    for name in _INS:
        full = f"L0_ffn_{name}" if name.startswith("W_") else f"L0_attn_{name}"
        a = _np.ascontiguousarray(inputs[full])
        arrays[f"in_{name}"] = a
        args.append(nc.dram_tensor(f"in_{name}", a.shape, _mybir.dt.from_np(a.dtype), kind="ExternalInput").ap())
    args.append(nc.dram_tensor("out_0", (B, S, HID), _mybir.dt.float32, kind="ExternalOutput").ap())
    layer(nc, *args)
    r = _run(nc, [arrays], core_ids=[0])
    return r.results[0]["out_0"]
```
